# Optimizing a Trainium2 kernel written in Bass

```python
import numpy as np
import jax
import jax.numpy as jnp

def _softmax(x, axis=-1):
    return jax.nn.softmax(x, axis=axis)

def _gelu(x):
    return jax.nn.gelu(x, approximate=True)

def _silu(x):
    return jax.nn.silu(x)

def _sigmoid(x):
    return jax.nn.sigmoid(x)

def _layernorm(x, axis=-1, eps=1e-05):
    m = jnp.mean(x, axis=axis, keepdims=True)
    v = jnp.var(x, axis=axis, keepdims=True)
    return (x - m) / jnp.sqrt(v + eps)

def _scatter_add(tgt, idx, src, axis=0):
    return tgt.at[idx].add(src)

def _segment_sum(src, seg, n):
    return jax.ops.segment_sum(src, seg, n)
kernel_name = 'mk_gnn_ffn_d2_gnn_r8_4e0767'

def setup_inputs(seed: int=0):
    np.random.seed(seed)
    _w = jnp.asarray

    def _rec_inputs():
        import jax
        import jax.numpy as jnp
        _gk = jax.random.key(seed)
        x = -0.0002117 + 1 * jax.random.normal(jax.random.fold_in(_gk, 1), (1250, 512), jnp.float32)
        src = jax.random.randint(jax.random.fold_in(_gk, 2), (20000,), 0, 1250, jnp.int32)
        dst = jnp.minimum((1250 * jax.random.uniform(jax.random.fold_in(_gk, 3), (20000,)) ** 2.0).astype(jnp.int32), 9999)
        _o = jnp.argsort(dst, stable=True)
        src = src[_o]
        dst = dst[_o]
        edge_attr_4 = 0.00171547 + 0.999346 * jax.random.normal(jax.random.fold_in(_gk, 11), (20000, 4), jnp.float32)
        edge_attr_8 = 0.000126197 + 0.999763 * jax.random.normal(jax.random.fold_in(_gk, 12), (20000, 8), jnp.float32)
        edge_weight = jax.random.uniform(jax.random.fold_in(_gk, 14), (20000,), jnp.float32, 0.0, 0.999999)
        return (x, src, dst, edge_attr_4, edge_attr_8, edge_weight)
    x, src, dst, edge_attr_4, edge_attr_8, edge_weight = _rec_inputs()

    def _L0_gnn_setup():
        import jax, jax.numpy as jnp
        import numpy as np
        N_NODES = 6250
        N_EDGES = 200000
        IN_F = 512
        OUT_F = 512
        key = jax.random.key(seed)
        k1, k2, k3, k4, k5 = jax.random.split(key, 5)
        input = jax.random.normal(k1, (N_NODES, IN_F), dtype=jnp.float32)
        edge_index = jax.random.randint(k2, (2, N_EDGES), 0, N_NODES, dtype=jnp.int64)
        edge_vals = jax.random.uniform(k3, (N_EDGES,), dtype=jnp.float32)
        stdv = 1.0 / np.sqrt(OUT_F)
        weight = jax.random.uniform(k4, (IN_F, OUT_F), dtype=jnp.float32, minval=-stdv, maxval=stdv)
        bias = jax.random.uniform(k5, (OUT_F,), dtype=jnp.float32, minval=-stdv, maxval=stdv)
        return {'input': input, 'edge_index': edge_index, 'edge_vals': edge_vals, 'weight': weight, 'bias': bias}
    _L0_gnn_all = _L0_gnn_setup()
    _L0_gnn_in = {k: v for k, v in _L0_gnn_all.items() if k in ('weight', 'bias')}
    del _L0_gnn_all

    def _L0_ffn_setup():
        import jax, jax.numpy as jnp
        import numpy as np
        EPS = 1e-05
        NUM_HEADS = 8
        TOP_K = 2
        CAP_FACTOR = 2

        def layernorm(x, g, b):
            m = jnp.mean(x, axis=-1, keepdims=True)
            v = jnp.var(x, axis=-1, keepdims=True)
            return (x - m) * jax.lax.rsqrt(v + EPS) * g + b
        key = jax.random.key(seed)
        ks = jax.random.split(key, 16)
        B, S, H, E, F = (2, 256, 512, 64, 256)
        s = 0.02
        return {'x': jax.random.normal(ks[0], (B, S, H), jnp.float32), 'ln1_g': jnp.ones((H,), jnp.float32), 'ln1_b': jnp.zeros((H,), jnp.float32), 'wq': jax.random.normal(ks[1], (H, H), jnp.float32) * s, 'wk': jax.random.normal(ks[2], (H, H), jnp.float32) * s, 'wv': jax.random.normal(ks[3], (H, H), jnp.float32) * s, 'wo': jax.random.normal(ks[4], (H, H), jnp.float32) * s, 'ln2_g': jnp.ones((H,), jnp.float32), 'ln2_b': jnp.zeros((H,), jnp.float32), 'wr': jax.random.normal(ks[5], (H, E), jnp.float32) * s, 'w1': jax.random.normal(ks[6], (E, H, F), jnp.float32) * s, 'b1': jnp.zeros((E, F), jnp.float32), 'w2': jax.random.normal(ks[7], (E, F, H), jnp.float32) * s, 'b2': jnp.zeros((E, H), jnp.float32)}
    _L0_ffn_all = _L0_ffn_setup()
    _L0_ffn_in = {k: v for k, v in _L0_ffn_all.items() if k in ('ln1_g', 'ln1_b', 'wq', 'wk', 'wv', 'wo', 'ln2_g', 'ln2_b', 'wr', 'w1', 'b1', 'w2', 'b2')}
    del _L0_ffn_all

    def _L1_gnn_setup():
        import jax, jax.numpy as jnp
        import numpy as np
        MUL = 128
        N_NODES = 1250
        N_EDGES = 20000
        R_BASIS = 8
        HIDDEN = 64
        W_NUMEL = 4 * MUL
        SQRT3 = 3.0 ** 0.5
        SILU_2MOM = 1.679177
        AVG_NUM_NEIGHBORS = 10.0

        def _lin_irreps(x0, x1, W0, W1):
            y0 = x0 @ W0 / jnp.sqrt(jnp.float32(W0.shape[0]))
            y1 = jnp.einsum('num,uv->nvm', x1, W1) / jnp.sqrt(jnp.float32(W1.shape[0]))
            return (y0, y1)

        def _forward(node_feats, edge_attrs, edge_feats, edge_index, W_up0, W_up1, W_mlp1, W_mlp2, W_mlp3, W_mlp4, W_out0, W_out1):
            num_nodes = node_feats.shape[0]
            sender, receiver = (edge_index[0], edge_index[1])
            x0 = node_feats[:, :MUL]
            x1 = node_feats[:, MUL:].reshape(num_nodes, MUL, 3)
            x0, x1 = _lin_irreps(x0, x1, W_up0, W_up1)
            h = edge_feats
            for W in (W_mlp1, W_mlp2, W_mlp3):
                h = SILU_2MOM * jax.nn.silu(h @ W / jnp.sqrt(jnp.float32(W.shape[0])))
            tpw = h @ W_mlp4 / jnp.sqrt(jnp.float32(W_mlp4.shape[0]))
            w1, w2, w3, w4 = jnp.split(tpw, 4, axis=-1)
            s0 = x0[sender]
            s1 = x1[sender]
            y0 = edge_attrs[:, 0:1]
            y1 = edge_attrs[:, 1:4]
            p1 = w1 * s0 * y0
            p2 = (w2 * s0)[:, :, None] * y1[:, None, :]
            p3 = w3[:, :, None] * s1 * y0[:, None, :]
            p4 = w4 * jnp.einsum('eum,em->eu', s1, y1) / SQRT3
            m0 = jnp.concatenate([p1, p4], axis=-1)
            m1 = jnp.concatenate([p2, p3], axis=1)
            msg0 = jax.ops.segment_sum(m0, receiver, num_segments=num_nodes)
            msg1 = jax.ops.segment_sum(m1, receiver, num_segments=num_nodes)
            o0, o1 = _lin_irreps(msg0, msg1, W_out0, W_out1)
            out = jnp.concatenate([o0, o1.reshape(num_nodes, 3 * MUL)], axis=-1)
            return out / AVG_NUM_NEIGHBORS
        key = jax.random.key(seed)
        ks = jax.random.split(key, 12)
        rn = lambda k, s: jax.random.normal(k, s, dtype=jnp.float32)
        return {'node_feats': rn(ks[0], (N_NODES, 4 * MUL)), 'edge_attrs': rn(ks[1], (N_EDGES, 4)), 'edge_feats': rn(ks[2], (N_EDGES, R_BASIS)), 'edge_index': jax.random.randint(ks[3], (2, N_EDGES), 0, N_NODES), 'W_up0': rn(ks[4], (MUL, MUL)), 'W_up1': rn(ks[5], (MUL, MUL)), 'W_mlp1': rn(ks[6], (R_BASIS, HIDDEN)), 'W_mlp2': rn(ks[7], (HIDDEN, HIDDEN)), 'W_mlp3': rn(ks[8], (HIDDEN, HIDDEN)), 'W_mlp4': rn(ks[9], (HIDDEN, W_NUMEL)), 'W_out0': rn(ks[10], (2 * MUL, MUL)), 'W_out1': rn(ks[11], (2 * MUL, MUL))}
    _L1_gnn_all = _L1_gnn_setup()
    _L1_gnn_in = {k: v for k, v in _L1_gnn_all.items() if k in ('W_up0', 'W_up1', 'W_mlp1', 'W_mlp2', 'W_mlp3', 'W_mlp4', 'W_out0', 'W_out1')}
    del _L1_gnn_all

    def _L1_ffn_setup():
        import jax, jax.numpy as jnp
        import numpy as np
        D = 512
        H = 8
        K = 4
        HD = D // H

        def _ln(x, w, b, eps=1e-05):
            m = x.mean(-1, keepdims=True)
            v = ((x - m) ** 2).mean(-1, keepdims=True)
            return (x - m) / jnp.sqrt(v + eps) * w + b

        def _spatial_experts(xn, idx, in_w, in_b, out_w, out_b):
            W = in_w[idx]
            qkv = jnp.einsum('btd,bed->bte', xn, W) + in_b[idx][:, None, :]
            q, k, v = jnp.split(qkv, 3, axis=-1)
            B, T, _ = xn.shape
            q = q.reshape(B, T, H, HD) * HD ** (-0.5)
            k = k.reshape(B, T, H, HD)
            v = v.reshape(B, T, H, HD)
            att = jax.nn.softmax(jnp.einsum('bthd,bshd->bhts', q, k), axis=-1)
            o = jnp.einsum('bhts,bshd->bthd', att, v).reshape(B, T, D)
            return jnp.einsum('btd,bod->bto', o, out_w[idx]) + out_b[idx][:, None, :]

        def _temporal_experts(xt, idx, qw, qb, kw, kb, vw, vb, pw, pb):
            B, T, _ = xt.shape
            q = (jnp.einsum('btd,bod->bto', xt, qw[idx]) + qb[idx][:, None, :]).reshape(B, T, H, HD)
            k = (jnp.einsum('btd,bod->bto', xt, kw[idx]) + kb[idx][:, None, :]).reshape(B, T, H, HD)
            v = (jnp.einsum('btd,bod->bto', xt, vw[idx]) + vb[idx][:, None, :]).reshape(B, T, H, HD)
            logits = jnp.einsum('bthd,bshd->bhts', q, k) * HD ** (-0.5)
            causal = jnp.tril(jnp.ones((T, T), dtype=bool))
            logits = jnp.where(causal, logits, -jnp.inf)
            att = jax.nn.softmax(logits, axis=-1)
            o = jnp.einsum('bhts,bshd->bthd', att, v).reshape(B, T, D)
            o = jnp.einsum('btd,bod->bto', o, pw[idx]) + pb[idx][:, None, :]
            return xt + o

        def _cross_mha(q_in, kv_in, in_w, in_b, out_w, out_b):
            B, T, _ = q_in.shape
            S = kv_in.shape[1]
            Wq, Wk, Wv = (in_w[:D], in_w[D:2 * D], in_w[2 * D:])
            bq, bk, bv = (in_b[:D], in_b[D:2 * D], in_b[2 * D:])
            q = (q_in @ Wq.T + bq).reshape(B, T, H, HD) * HD ** (-0.5)
            k = (kv_in @ Wk.T + bk).reshape(B, S, H, HD)
            v = (kv_in @ Wv.T + bv).reshape(B, S, H, HD)
            att = jax.nn.softmax(jnp.einsum('bthd,bshd->bhts', q, k), axis=-1)
            o = jnp.einsum('bhts,bshd->bthd', att, v).reshape(B, T, D)
            return o @ out_w.T + out_b
        key = jax.random.key(seed)
        ks = iter(jax.random.split(key, 40))
        B, T = (256, 64)
        p = lambda *shape: jax.random.normal(next(ks), shape, dtype=jnp.float32) * 0.02
        inp = {'x': jax.random.normal(next(ks), (B, T, D), dtype=jnp.float32), 'router_w1': p(128, D), 'router_b1': jnp.zeros((128,), jnp.float32), 'router_w2': p(2 * K, 128), 'router_b2': jnp.zeros((2 * K,), jnp.float32), 'norm_s_w': jnp.ones((D,), jnp.float32), 'norm_s_b': jnp.zeros((D,), jnp.float32), 'norm_t_w': jnp.ones((D,), jnp.float32), 'norm_t_b': jnp.zeros((D,), jnp.float32), 'sp_in_w': p(K, 3 * D, D), 'sp_in_b': jnp.zeros((K, 3 * D), jnp.float32), 'sp_out_w': p(K, D, D), 'sp_out_b': jnp.zeros((K, D), jnp.float32), 'tq_w': p(K, D, D), 'tq_b': jnp.zeros((K, D), jnp.float32), 'tk_w': p(K, D, D), 'tk_b': jnp.zeros((K, D), jnp.float32), 'tv_w': p(K, D, D), 'tv_b': jnp.zeros((K, D), jnp.float32), 'tp_w': p(K, D, D), 'tp_b': jnp.zeros((K, D), jnp.float32), 'cross_in_w': p(3 * D, D), 'cross_in_b': jnp.zeros((3 * D,), jnp.float32), 'cross_out_w': p(D, D), 'cross_out_b': jnp.zeros((D,), jnp.float32), 'norm_mlp_w': jnp.ones((D,), jnp.float32), 'norm_mlp_b': jnp.zeros((D,), jnp.float32), 'mlp_w1': p(4 * D, D), 'mlp_b1': jnp.zeros((4 * D,), jnp.float32), 'mlp_w2': p(D, 4 * D), 'mlp_b2': jnp.zeros((D,), jnp.float32)}
        return inp
    _L1_ffn_all = _L1_ffn_setup()
    _L1_ffn_in = {k: v for k, v in _L1_ffn_all.items() if k in ('router_w1', 'router_b1', 'router_w2', 'router_b2', 'norm_s_w', 'norm_s_b', 'norm_t_w', 'norm_t_b', 'sp_in_w', 'sp_in_b', 'sp_out_w', 'sp_out_b', 'tq_w', 'tq_b', 'tk_w', 'tk_b', 'tv_w', 'tv_b', 'tp_w', 'tp_b', 'cross_in_w', 'cross_in_b', 'cross_out_w', 'cross_out_b', 'norm_mlp_w', 'norm_mlp_b', 'mlp_w1', 'mlp_b1', 'mlp_w2', 'mlp_b2')}
    del _L1_ffn_all
    return {'x': x, 'src': src, 'dst': dst, 'edge_attr_4': edge_attr_4, 'edge_attr_8': edge_attr_8, 'edge_weight': edge_weight, 'L0_gnn_weight': _L0_gnn_in['weight'], 'L0_gnn_bias': _L0_gnn_in['bias'], 'L0_ffn_ln1_g': _L0_ffn_in['ln1_g'], 'L0_ffn_ln1_b': _L0_ffn_in['ln1_b'], 'L0_ffn_wq': _L0_ffn_in['wq'], 'L0_ffn_wk': _L0_ffn_in['wk'], 'L0_ffn_wv': _L0_ffn_in['wv'], 'L0_ffn_wo': _L0_ffn_in['wo'], 'L0_ffn_ln2_g': _L0_ffn_in['ln2_g'], 'L0_ffn_ln2_b': _L0_ffn_in['ln2_b'], 'L0_ffn_wr': _L0_ffn_in['wr'], 'L0_ffn_w1': _L0_ffn_in['w1'], 'L0_ffn_b1': _L0_ffn_in['b1'], 'L0_ffn_w2': _L0_ffn_in['w2'], 'L0_ffn_b2': _L0_ffn_in['b2'], 'L1_gnn_W_up0': _L1_gnn_in['W_up0'], 'L1_gnn_W_up1': _L1_gnn_in['W_up1'], 'L1_gnn_W_mlp1': _L1_gnn_in['W_mlp1'], 'L1_gnn_W_mlp2': _L1_gnn_in['W_mlp2'], 'L1_gnn_W_mlp3': _L1_gnn_in['W_mlp3'], 'L1_gnn_W_mlp4': _L1_gnn_in['W_mlp4'], 'L1_gnn_W_out0': _L1_gnn_in['W_out0'], 'L1_gnn_W_out1': _L1_gnn_in['W_out1'], 'L1_ffn_router_w1': _L1_ffn_in['router_w1'], 'L1_ffn_router_b1': _L1_ffn_in['router_b1'], 'L1_ffn_router_w2': _L1_ffn_in['router_w2'], 'L1_ffn_router_b2': _L1_ffn_in['router_b2'], 'L1_ffn_norm_s_w': _L1_ffn_in['norm_s_w'], 'L1_ffn_norm_s_b': _L1_ffn_in['norm_s_b'], 'L1_ffn_norm_t_w': _L1_ffn_in['norm_t_w'], 'L1_ffn_norm_t_b': _L1_ffn_in['norm_t_b'], 'L1_ffn_sp_in_w': _L1_ffn_in['sp_in_w'], 'L1_ffn_sp_in_b': _L1_ffn_in['sp_in_b'], 'L1_ffn_sp_out_w': _L1_ffn_in['sp_out_w'], 'L1_ffn_sp_out_b': _L1_ffn_in['sp_out_b'], 'L1_ffn_tq_w': _L1_ffn_in['tq_w'], 'L1_ffn_tq_b': _L1_ffn_in['tq_b'], 'L1_ffn_tk_w': _L1_ffn_in['tk_w'], 'L1_ffn_tk_b': _L1_ffn_in['tk_b'], 'L1_ffn_tv_w': _L1_ffn_in['tv_w'], 'L1_ffn_tv_b': _L1_ffn_in['tv_b'], 'L1_ffn_tp_w': _L1_ffn_in['tp_w'], 'L1_ffn_tp_b': _L1_ffn_in['tp_b'], 'L1_ffn_cross_in_w': _L1_ffn_in['cross_in_w'], 'L1_ffn_cross_in_b': _L1_ffn_in['cross_in_b'], 'L1_ffn_cross_out_w': _L1_ffn_in['cross_out_w'], 'L1_ffn_cross_out_b': _L1_ffn_in['cross_out_b'], 'L1_ffn_norm_mlp_w': _L1_ffn_in['norm_mlp_w'], 'L1_ffn_norm_mlp_b': _L1_ffn_in['norm_mlp_b'], 'L1_ffn_mlp_w1': _L1_ffn_in['mlp_w1'], 'L1_ffn_mlp_b1': _L1_ffn_in['mlp_b1'], 'L1_ffn_mlp_w2': _L1_ffn_in['mlp_w2'], 'L1_ffn_mlp_b2': _L1_ffn_in['mlp_b2']}

def reference(x, src, dst, edge_attr_4, edge_attr_8, edge_weight, L0_gnn_weight, L0_gnn_bias, L0_ffn_ln1_g, L0_ffn_ln1_b, L0_ffn_wq, L0_ffn_wk, L0_ffn_wv, L0_ffn_wo, L0_ffn_ln2_g, L0_ffn_ln2_b, L0_ffn_wr, L0_ffn_w1, L0_ffn_b1, L0_ffn_w2, L0_ffn_b2, L1_gnn_W_up0, L1_gnn_W_up1, L1_gnn_W_mlp1, L1_gnn_W_mlp2, L1_gnn_W_mlp3, L1_gnn_W_mlp4, L1_gnn_W_out0, L1_gnn_W_out1, L1_ffn_router_w1, L1_ffn_router_b1, L1_ffn_router_w2, L1_ffn_router_b2, L1_ffn_norm_s_w, L1_ffn_norm_s_b, L1_ffn_norm_t_w, L1_ffn_norm_t_b, L1_ffn_sp_in_w, L1_ffn_sp_in_b, L1_ffn_sp_out_w, L1_ffn_sp_out_b, L1_ffn_tq_w, L1_ffn_tq_b, L1_ffn_tk_w, L1_ffn_tk_b, L1_ffn_tv_w, L1_ffn_tv_b, L1_ffn_tp_w, L1_ffn_tp_b, L1_ffn_cross_in_w, L1_ffn_cross_in_b, L1_ffn_cross_out_w, L1_ffn_cross_out_b, L1_ffn_norm_mlp_w, L1_ffn_norm_mlp_b, L1_ffn_mlp_w1, L1_ffn_mlp_b1, L1_ffn_mlp_w2, L1_ffn_mlp_b2):
    import jax
    import jax.numpy as jnp

    def _L0_gnn_ref(input, edge_index, edge_vals, weight, bias):
        import jax, jax.numpy as jnp
        import numpy as np
        N_NODES = 6250
        N_EDGES = 200000
        IN_F = 512
        OUT_F = 512
        support = jnp.matmul(input, weight)
        dst, src = (edge_index[0], edge_index[1])
        messages = support[src] * edge_vals[:, None]
        output = jax.ops.segment_sum(messages, dst, num_segments=input.shape[0])
        return output + bias

    def _L0_ffn_ref(x, ln1_g, ln1_b, wq, wk, wv, wo, ln2_g, ln2_b, wr, w1, b1, w2, b2):
        import jax, jax.numpy as jnp
        import numpy as np
        EPS = 1e-05
        NUM_HEADS = 8
        TOP_K = 2
        CAP_FACTOR = 2

        def layernorm(x, g, b):
            m = jnp.mean(x, axis=-1, keepdims=True)
            v = jnp.var(x, axis=-1, keepdims=True)
            return (x - m) * jax.lax.rsqrt(v + EPS) * g + b
        B, S, H = x.shape
        NH = NUM_HEADS
        dh = H // NH
        x1 = layernorm(x, ln1_g, ln1_b)
        q = (x1 @ wq).reshape(B, S, NH, dh)
        k = (x1 @ wk).reshape(B, S, NH, dh)
        v = (x1 @ wv).reshape(B, S, NH, dh)
        scores = jnp.einsum('bqhd,bkhd->bhqk', q, k) * dh ** (-0.5)
        p = jax.nn.softmax(scores, axis=-1)
        attn_out = jnp.einsum('bhqk,bkhd->bqhd', p, v).reshape(B, S, H) @ wo
        x = x + attn_out
        x2 = layernorm(x, ln2_g, ln2_b).reshape(B * S, H)
        T = B * S
        E = wr.shape[1]
        C = CAP_FACTOR * (T * TOP_K // E)
        probs = jax.nn.softmax(x2 @ wr, axis=-1)
        gate_v, gate_i = jax.lax.top_k(probs, TOP_K)
        gate_v = gate_v / jnp.sum(gate_v, axis=-1, keepdims=True)
        ef = gate_i.reshape(-1)
        gf = gate_v.reshape(-1)
        oh = jax.nn.one_hot(ef, E, dtype=x2.dtype)
        pos = jnp.sum((jnp.cumsum(oh, axis=0) - oh) * oh, axis=1).astype(jnp.int32)
        keep = (pos < C).astype(x2.dtype)
        posc = jnp.minimum(pos, C - 1)
        tok = jnp.repeat(x2, TOP_K, axis=0) * keep[:, None]
        buf = jnp.zeros((E, C, H), x2.dtype).at[ef, posc].add(tok)
        h = jax.nn.gelu(jnp.einsum('ech,ehf->ecf', buf, w1) + b1[:, None, :])
        y = jnp.einsum('ecf,efh->ech', h, w2) + b2[:, None, :]
        ys = y[ef, posc] * (gf * keep)[:, None]
        moe_out = ys.reshape(T, TOP_K, H).sum(axis=1).reshape(B, S, H)
        return x + moe_out

    def _L1_gnn_ref(node_feats, edge_attrs, edge_feats, edge_index, W_up0, W_up1, W_mlp1, W_mlp2, W_mlp3, W_mlp4, W_out0, W_out1):
        import jax, jax.numpy as jnp
        import numpy as np
        MUL = 128
        N_NODES = 1250
        N_EDGES = 20000
        R_BASIS = 8
        HIDDEN = 64
        W_NUMEL = 4 * MUL
        SQRT3 = 3.0 ** 0.5
        SILU_2MOM = 1.679177
        AVG_NUM_NEIGHBORS = 10.0

        def _lin_irreps(x0, x1, W0, W1):
            y0 = x0 @ W0 / jnp.sqrt(jnp.float32(W0.shape[0]))
            y1 = jnp.einsum('num,uv->nvm', x1, W1) / jnp.sqrt(jnp.float32(W1.shape[0]))
            return (y0, y1)

        def _forward(node_feats, edge_attrs, edge_feats, edge_index, W_up0, W_up1, W_mlp1, W_mlp2, W_mlp3, W_mlp4, W_out0, W_out1):
            num_nodes = node_feats.shape[0]
            sender, receiver = (edge_index[0], edge_index[1])
            x0 = node_feats[:, :MUL]
            x1 = node_feats[:, MUL:].reshape(num_nodes, MUL, 3)
            x0, x1 = _lin_irreps(x0, x1, W_up0, W_up1)
            h = edge_feats
            for W in (W_mlp1, W_mlp2, W_mlp3):
                h = SILU_2MOM * jax.nn.silu(h @ W / jnp.sqrt(jnp.float32(W.shape[0])))
            tpw = h @ W_mlp4 / jnp.sqrt(jnp.float32(W_mlp4.shape[0]))
            w1, w2, w3, w4 = jnp.split(tpw, 4, axis=-1)
            s0 = x0[sender]
            s1 = x1[sender]
            y0 = edge_attrs[:, 0:1]
            y1 = edge_attrs[:, 1:4]
            p1 = w1 * s0 * y0
            p2 = (w2 * s0)[:, :, None] * y1[:, None, :]
            p3 = w3[:, :, None] * s1 * y0[:, None, :]
            p4 = w4 * jnp.einsum('eum,em->eu', s1, y1) / SQRT3
            m0 = jnp.concatenate([p1, p4], axis=-1)
            m1 = jnp.concatenate([p2, p3], axis=1)
            msg0 = jax.ops.segment_sum(m0, receiver, num_segments=num_nodes)
            msg1 = jax.ops.segment_sum(m1, receiver, num_segments=num_nodes)
            o0, o1 = _lin_irreps(msg0, msg1, W_out0, W_out1)
            out = jnp.concatenate([o0, o1.reshape(num_nodes, 3 * MUL)], axis=-1)
            return out / AVG_NUM_NEIGHBORS
        return _forward(node_feats, edge_attrs, edge_feats, edge_index, W_up0, W_up1, W_mlp1, W_mlp2, W_mlp3, W_mlp4, W_out0, W_out1)

    def _L1_ffn_ref(x, router_w1, router_b1, router_w2, router_b2, norm_s_w, norm_s_b, norm_t_w, norm_t_b, sp_in_w, sp_in_b, sp_out_w, sp_out_b, tq_w, tq_b, tk_w, tk_b, tv_w, tv_b, tp_w, tp_b, cross_in_w, cross_in_b, cross_out_w, cross_out_b, norm_mlp_w, norm_mlp_b, mlp_w1, mlp_b1, mlp_w2, mlp_b2):
        import jax, jax.numpy as jnp
        import numpy as np
        D = 512
        H = 8
        K = 4
        HD = D // H

        def _ln(x, w, b, eps=1e-05):
            m = x.mean(-1, keepdims=True)
            v = ((x - m) ** 2).mean(-1, keepdims=True)
            return (x - m) / jnp.sqrt(v + eps) * w + b

        def _spatial_experts(xn, idx, in_w, in_b, out_w, out_b):
            W = in_w[idx]
            qkv = jnp.einsum('btd,bed->bte', xn, W) + in_b[idx][:, None, :]
            q, k, v = jnp.split(qkv, 3, axis=-1)
            B, T, _ = xn.shape
            q = q.reshape(B, T, H, HD) * HD ** (-0.5)
            k = k.reshape(B, T, H, HD)
            v = v.reshape(B, T, H, HD)
            att = jax.nn.softmax(jnp.einsum('bthd,bshd->bhts', q, k), axis=-1)
            o = jnp.einsum('bhts,bshd->bthd', att, v).reshape(B, T, D)
            return jnp.einsum('btd,bod->bto', o, out_w[idx]) + out_b[idx][:, None, :]

        def _temporal_experts(xt, idx, qw, qb, kw, kb, vw, vb, pw, pb):
            B, T, _ = xt.shape
            q = (jnp.einsum('btd,bod->bto', xt, qw[idx]) + qb[idx][:, None, :]).reshape(B, T, H, HD)
            k = (jnp.einsum('btd,bod->bto', xt, kw[idx]) + kb[idx][:, None, :]).reshape(B, T, H, HD)
            v = (jnp.einsum('btd,bod->bto', xt, vw[idx]) + vb[idx][:, None, :]).reshape(B, T, H, HD)
            logits = jnp.einsum('bthd,bshd->bhts', q, k) * HD ** (-0.5)
            causal = jnp.tril(jnp.ones((T, T), dtype=bool))
            logits = jnp.where(causal, logits, -jnp.inf)
            att = jax.nn.softmax(logits, axis=-1)
            o = jnp.einsum('bhts,bshd->bthd', att, v).reshape(B, T, D)
            o = jnp.einsum('btd,bod->bto', o, pw[idx]) + pb[idx][:, None, :]
            return xt + o

        def _cross_mha(q_in, kv_in, in_w, in_b, out_w, out_b):
            B, T, _ = q_in.shape
            S = kv_in.shape[1]
            Wq, Wk, Wv = (in_w[:D], in_w[D:2 * D], in_w[2 * D:])
            bq, bk, bv = (in_b[:D], in_b[D:2 * D], in_b[2 * D:])
            q = (q_in @ Wq.T + bq).reshape(B, T, H, HD) * HD ** (-0.5)
            k = (kv_in @ Wk.T + bk).reshape(B, S, H, HD)
            v = (kv_in @ Wv.T + bv).reshape(B, S, H, HD)
            att = jax.nn.softmax(jnp.einsum('bthd,bshd->bhts', q, k), axis=-1)
            o = jnp.einsum('bhts,bshd->bthd', att, v).reshape(B, T, D)
            return o @ out_w.T + out_b
        pooled = x.mean(axis=1)
        h = jax.nn.gelu(pooled @ router_w1.T + router_b1, approximate=False)
        route = jax.nn.softmax(h @ router_w2.T + router_b2, axis=-1)
        idx_s = jnp.argmax(route[:, :K], axis=-1)
        idx_t = jnp.argmax(route[:, K:], axis=-1)
        xn = _ln(x, norm_s_w, norm_s_b)
        spatial_out = _spatial_experts(xn, idx_s, sp_in_w, sp_in_b, sp_out_w, sp_out_b)
        xt = _ln(x, norm_t_w, norm_t_b)
        temporal_out = _temporal_experts(xt, idx_t, tq_w, tq_b, tk_w, tk_b, tv_w, tv_b, tp_w, tp_b)
        fused = _cross_mha(spatial_out, temporal_out, cross_in_w, cross_in_b, cross_out_w, cross_out_b)
        x = x + fused
        h2 = _ln(x, norm_mlp_w, norm_mlp_b)
        x = x + (jax.nn.gelu(h2 @ mlp_w1.T + mlp_b1, approximate=False) @ mlp_w2.T + mlp_b2)
        return x
    edge_index = jnp.stack([src, dst])
    x = x + _L0_gnn_ref(_layernorm(x, axis=-1), edge_index, edge_weight, L0_gnn_weight, L0_gnn_bias)
    x = x + _L0_ffn_ref(_layernorm(x, axis=-1)[None], L0_ffn_ln1_g, L0_ffn_ln1_b, L0_ffn_wq, L0_ffn_wk, L0_ffn_wv, L0_ffn_wo, L0_ffn_ln2_g, L0_ffn_ln2_b, L0_ffn_wr, L0_ffn_w1, L0_ffn_b1, L0_ffn_w2, L0_ffn_b2)[0]
    x = x + _L1_gnn_ref(_layernorm(x, axis=-1), edge_attr_4, edge_attr_8, edge_index, L1_gnn_W_up0, L1_gnn_W_up1, L1_gnn_W_mlp1, L1_gnn_W_mlp2, L1_gnn_W_mlp3, L1_gnn_W_mlp4, L1_gnn_W_out0, L1_gnn_W_out1)
    x = x + _L1_ffn_ref(_layernorm(x, axis=-1)[None], L1_ffn_router_w1, L1_ffn_router_b1, L1_ffn_router_w2, L1_ffn_router_b2, L1_ffn_norm_s_w, L1_ffn_norm_s_b, L1_ffn_norm_t_w, L1_ffn_norm_t_b, L1_ffn_sp_in_w, L1_ffn_sp_in_b, L1_ffn_sp_out_w, L1_ffn_sp_out_b, L1_ffn_tq_w, L1_ffn_tq_b, L1_ffn_tk_w, L1_ffn_tk_b, L1_ffn_tv_w, L1_ffn_tv_b, L1_ffn_tp_w, L1_ffn_tp_b, L1_ffn_cross_in_w, L1_ffn_cross_in_b, L1_ffn_cross_out_w, L1_ffn_cross_out_b, L1_ffn_norm_mlp_w, L1_ffn_norm_mlp_b, L1_ffn_mlp_w1, L1_ffn_mlp_b1, L1_ffn_mlp_w2, L1_ffn_mlp_b2)[0]
    return x

_drawn_inputs = setup_inputs


def setup_inputs(seed=0):
    import zlib

    import numpy as np

    out = dict(_drawn_inputs(seed))
    spreads = {'L0_ffn_ln1_g': (1.0, 0.6),
     'L0_ffn_ln1_b': (0.0, 0.769),
     'L0_ffn_ln2_g': (1.0, 0.6),
     'L0_ffn_ln2_b': (0.0, 0.569),
     'L0_ffn_b1': (0.0, 0.8),
     'L0_ffn_b2': (0.0, 0.302),
     'L1_ffn_router_b1': (0.0, 0.8),
     'L1_ffn_router_b2': (0.0, 0.1),
     'L1_ffn_norm_s_w': (1.0, 0.6),
     'L1_ffn_norm_s_b': (0.0, 0.8),
     'L1_ffn_norm_t_w': (1.0, 0.6),
     'L1_ffn_norm_t_b': (0.0, 0.8),
     'L1_ffn_sp_in_b': (0.0, 0.8),
     'L1_ffn_sp_out_b': (0.0, 0.8),
     'L1_ffn_tq_b': (0.0, 0.8),
     'L1_ffn_tk_b': (0.0, 2.0),
     'L1_ffn_tv_b': (0.0, 0.8),
     'L1_ffn_tp_b': (0.0, 0.8),
     'L1_ffn_cross_in_b': (0.0, 0.631),
     'L1_ffn_cross_out_b': (0.0, 2.0),
     'L1_ffn_norm_mlp_w': (1.0, 0.6),
     'L1_ffn_norm_mlp_b': (0.0, 2.0),
     'L1_ffn_mlp_b1': (0.0, 2.0),
     'L1_ffn_mlp_b2': (0.0, 2.0)}
    factors = {'L0_gnn_bias': 3.508,
     'L0_ffn_wq': 8.0,
     'L0_ffn_wk': 8.0,
     'L0_ffn_wv': 3.755,
     'L0_ffn_wo': 3.778,
     'L1_ffn_router_w1': 8.0,
     'L1_ffn_router_w2': 8.0,
     'L1_ffn_sp_in_w': 8.0,
     'L1_ffn_sp_out_w': 8.0,
     'L1_ffn_tq_w': 8.0,
     'L1_ffn_tk_w': 8.0,
     'L1_ffn_tv_w': 8.0,
     'L1_ffn_tp_w': 8.0,
     'L1_ffn_cross_in_w': 4.92,
     'L1_ffn_cross_out_w': 3.465,
     'L1_ffn_mlp_w1': 8.0,
     'L1_ffn_mlp_w2': 8.0}
    for name, (base, spread) in spreads.items():
        noise = np.random.default_rng([zlib.crc32(name.encode()), seed]).standard_normal(out[name].shape)
        drawn = base * np.exp(spread * noise) if base else spread * noise
        out[name] = jnp.asarray(drawn.astype(out[name].dtype))
    for name, factor in factors.items():
        out[name] = (out[name] * factor).astype(out[name].dtype)
    return out
```

```python
from contextlib import ExitStack, contextmanager

import numpy as np

import concourse.bass as bass
from concourse import mybir

F32 = mybir.dt.float32
BF16 = mybir.dt.bfloat16
I32 = mybir.dt.int32
U32 = mybir.dt.uint32
ALU = mybir.AluOpType
ACT = mybir.ActivationFunctionType
AX = mybir.AxisListType.X

N = 1250
D = 512
TN = 125
NT = N // TN
DC = D // 128
E = 20000
EC = E // TN
TE = 128
GE = 14
GROUPS = -(-((E + NT * (TE - 1)) // TE) // GE)
NS = GE * GROUPS
ROW = 16
HEADS = 8
HD = D // HEADS
EXPERTS = 64
CAP = 2 * (N * 2 // EXPERTS)
CAPW = 96
FF = 256
MLP = 4 * D
EPS = 1e-5
SILU_GAIN = 1.679177
COLS = [slice(0, 512), slice(512, 1024), slice(1024, N)]

PCOL = {}
_at = 0
for _n, _w in (("ln1_g", 4), ("ln1_b", 4), ("ln2_g", 4), ("ln2_b", 4), ("ns_w", 4), ("ns_b", 4),
               ("nt_w", 4), ("nt_b", 4), ("nm_w", 4), ("nm_b", 4), ("co_b", 4), ("mlp_b1", 16),
               ("rt_b1", 1), ("moe_b1", EXPERTS * FF // 128)):
    PCOL[_n] = slice(_at, _at + _w)
    _at += _w
NPCOL = _at


class Core:
    pass


@contextmanager
def stage(nc, *names):
    sems = [nc.alloc_semaphore(f"{n}_{nc.next_id()}") for n in names]
    with nc.Block() as block:
        yield (block, *sems)
    nc.clear_and_free_semaphores(sems)
    nc.all_engine_barrier()


class Chain:

    def __init__(self, eng, sem):
        self.eng, self.sem, self.n = eng, sem, 0

    def mark(self, ins):
        self.n += 1
        ins.then_inc(self.sem, 1)

    def step(self, ins):
        self.mark(ins)
        self.eng.wait_ge(self.sem, self.n)

    def join(self):
        self.eng.wait_ge(self.sem, self.n)


def tiles_of(dram):
    return dram.rearrange("(i p) d -> p i d", p=TN)


def make_constants(nc, c):
    with stage(nc, "made", "loaded") as (block, made, loaded):
        @block.sync
        def _(sp):
            sp.dma_start(c.pcol[:, :], c.pcol_d).then_inc(loaded, 16)
            sp.wait_ge(loaded, 16)

        @block.gpsimd
        def _(pool):
            own = Chain(pool, made)
            pool.memset(c.ident[:, :], 0.0).then_inc(made, 1)
            pool.memset(c.lower[:, :], 1.0).then_inc(made, 1)
            pool.memset(c.ones[:, :], 1.0).then_inc(made, 1)
            pool.memset(c.causal[:, :], 0.0).then_inc(made, 1)
            pool.memset(c.mean_col[:, :], 1.0 / N).then_inc(made, 1)
            pool.iota(c.iota_i[:, :], [[1, 256]], base=0, channel_multiplier=0).then_inc(made, 1)
            pool.iota(c.node_i[:, :], [[TN, NT]], base=0, channel_multiplier=1).then_inc(made, 1)
            own.n = 7
            own.join()
            own.mark(pool.affine_select(out=c.ident[:, :], in_=c.ident[:, :], compare_op=ALU.not_equal,
                                        fill=1.0, base=0, pattern=[[-1, 128]], channel_multiplier=1))
            own.mark(pool.affine_select(out=c.lower[:, :], in_=c.lower[:, :], compare_op=ALU.is_gt,
                                        fill=0.0, base=0, pattern=[[1, 128]], channel_multiplier=-1))
            own.mark(pool.affine_select(out=c.causal[:, :], in_=c.causal[:, :], compare_op=ALU.is_ge,
                                        fill=-3.0e38, base=0, pattern=[[-1, TN]], channel_multiplier=1))
            own.mark(pool.tensor_copy(c.iota[:, :], c.iota_i[:, :]))
            own.mark(pool.tensor_copy(c.node[:, :], c.node_i[:, :]))
            own.join()


def normalize(nc, c, src, first_out=None, last_out=None, double=False, targets=(), column=None):
    column = column or (lambda k: slice(128 * k, 128 * k + 128))
    with ExitStack() as ctx:
        sb = lambda name, shape, dt=F32: ctx.enter_context(nc.sbuf_tensor(f"{name}_{nc.next_id()}", shape, dt))
        x = sb("ln_x", [TN, NT, D])
        y = sb("ln_y", [TN, NT, D])
        z = sb("ln_z", [TN, NT, D]) if double else y
        stats = sb("ln_stats", [TN, NT, 6])
        mv = sb("ln_mv", [TN, NT, 2])
        root = sb("ln_root", [TN, NT])
        ps = ctx.enter_context(nc.psum_tensor(f"ln_ps_{nc.next_id()}", [128, 4, 512], F32))
        passes = [(x, y), (y, z)] if double else [(x, y)]
        with stage(nc, "loaded", "loaded2", "own", "var", "rooted", "normed", "turned", "copied", "stored", "copied2") as (
                block, loaded, loaded2, own_s, var, rooted, normed, turned, copied, stored, copied2):
            halves = [slice(0, NT // 2), slice(NT // 2, NT)]

            @block.sync
            def _(sp):
                for s, h in zip((loaded, loaded2), halves):
                    sp.dma_start(x[:, h, :], tiles_of(src)[:, h, :]).then_inc(s, 16)
                n = 0
                if first_out is not None:
                    sp.wait_ge(normed, NT)
                    sp.dma_start(tiles_of(first_out), y[:, :, :]).then_inc(stored, 16)
                    n += 16
                if last_out is not None:
                    sp.wait_ge(normed, NT * len(passes))
                    sp.dma_start(tiles_of(last_out), z[:, :, :]).then_inc(stored, 16)
                    n += 16
                if n:
                    sp.wait_ge(stored, n)

            @block.vector
            def _(dve):
                own = Chain(dve, own_s)
                for k, (a, b) in enumerate(passes):
                    for i in range(NT):
                        if k == 0:
                            dve.wait_ge(loaded if i < NT // 2 else loaded2, 16)
                        own.mark(dve.bn_stats(stats[:, i, :], a[:, i, :]))
                    own.join()
                    for i in range(NT):
                        own.mark(dve.bn_aggr(mv[:, i, :], stats[:, i, :]))
                    own.join()
                    own.mark(dve.tensor_scalar(root[:, :], mv[:, :, 1], EPS, None, ALU.add))
                    own.join()
                    dve.engine_nop().then_inc(var, 1)
                    dve.wait_ge(rooted, k + 1)
                    own.step(dve.reciprocal(root[:, :], root[:, :]))
                    for i in range(NT):
                        dve.tensor_scalar(b[:, i, :], a[:, i, :], mv[:, i, 0:1], root[:, i:i + 1],
                                          ALU.subtract, ALU.mult).then_inc(normed, 1)
                    dve.wait_ge(normed, NT * (k + 1))
                if len(targets) > 1:
                    d, g, b = targets[1]
                    for i in range(NT):
                        dve.wait_ge(copied, i + 1)
                        for k in range(DC):
                            ins = dve.tensor_scalar(d[:, k, TN * i:TN * i + TN], ps[:, i % 4, TN * k:TN * k + TN],
                                                    g[:, k:k + 1], b[:, k:k + 1], ALU.mult, ALU.add)
                        ins.then_inc(copied2, 1)

            @block.scalar
            def _(act):
                for k in range(len(passes)):
                    act.wait_ge(var, k + 1)
                    act.activation(root[:, :], root[:, :], ACT.Sqrt).then_inc(rooted, 1)
                if targets:
                    d, g, b = targets[0]
                    for i in range(NT):
                        act.wait_ge(turned, i + 1)
                        if g is None:
                            ins = act.activation(d[:, :, TN * i:TN * i + TN],
                                                 ps[:, i % 4, 0:DC * TN].rearrange("p (k n) -> p k n", k=DC), ACT.Copy)
                        else:
                            for k in range(DC):
                                ins = act.activation(d[:, k, TN * i:TN * i + TN], ps[:, i % 4, TN * k:TN * k + TN],
                                                     ACT.Identity, bias=b[:, k:k + 1], scale=g[:, k:k + 1])
                        ins.then_inc(copied, 1)

            @block.tensor
            def _(pe):
                if targets:
                    for i in range(NT):
                        pe.wait_ge(normed, NT * (len(passes) - 1) + i + 1)
                        if i >= 4:
                            pe.wait_ge(copied, i - 3)
                            if len(targets) > 1:
                                pe.wait_ge(copied2, i - 3)
                        for k in range(DC):
                            ins = pe.transpose(ps[:, i % 4, TN * k:TN * k + TN], z[:, i, column(k)], c.ident[0:TN, 0:TN])
                        ins.then_inc(turned, 1)


def project_tokens(nc, c, src_t, nk, w_d, out_d, bias_d=None, residuals=(), width=D, scale=None):
    with ExitStack() as ctx:
        sb = lambda name, shape, dt=F32: ctx.enter_context(nc.sbuf_tensor(f"{name}_{nc.next_id()}", shape, dt))
        w = sb("pt_w", [128, nk, width])
        res = [sb("pt_res", [TN, 2, width]) for _ in residuals]
        y = sb("pt_y", [TN, 2, width])
        bias = sb("pt_bias", [TN, width]) if bias_d is not None else None
        ps = ctx.enter_context(nc.psum_tensor(f"pt_ps_{nc.next_id()}", [128, 4, 512], F32))
        with stage(nc, "weights", "res0", "res1", "summed", "added", "st0", "st1", "own") as (
                block, weights, res0, res1, summed, added, st0, st1, own_s):
            res_in = (res0, res1)
            st = (st0, st1)
            per = 16 * len(residuals)

            @block.sync
            def _(sp):
                for k in range(0, nk, 4):
                    sp.dma_start(w[:, k:k + 4, :], w_d[:, k:k + 4, :]).then_inc(weights, 16)
                if bias is not None:
                    sp.dma_start(bias[:, :], bias_d.to_broadcast((TN, width)) if bias_d.shape[0] == 1 else bias_d).then_inc(weights, 16)
                for i in range(NT + 1):
                    if i < NT and residuals:
                        if i >= 2:
                            sp.wait_ge(added, i - 1)
                        for r, d in zip(res, residuals):
                            sp.dma_start(r[:, i % 2, :], tiles_of(d)[:, i, :]).then_inc(res_in[i % 2], 16)
                    if i >= 1:
                        sp.wait_ge(added, i)
                        sp.dma_start(tiles_of(out_d)[:, i - 1, :], y[:, (i - 1) % 2, :]).then_inc(st[(i - 1) % 2], 16)
                for s in st:
                    sp.wait_ge(s, 16 * NT // 2)

            @block.tensor
            def _(pe):
                pe.wait_ge(weights, 16 * (nk // 4 + (bias is not None)))
                for i in range(NT):
                    if i >= 4:
                        pe.wait_ge(added, i - 3)
                    for k in range(nk):
                        ins = pe.matmul(ps[0:TN, i % 4, 0:width], src_t[:, k, TN * i:TN * i + TN], w[:, k, :],
                                        start=(k == 0), stop=(k == nk - 1))
                    ins.then_inc(summed, 1)

            @block.vector
            def _(dve):
                own = Chain(dve, own_s)
                dve.wait_ge(weights, 16 * (nk // 4 + (bias is not None)))
                for i in range(NT):
                    dve.wait_ge(summed, i + 1)
                    if residuals:
                        dve.wait_ge(res_in[i % 2], per * (i // 2 + 1))
                    if i >= 2:
                        dve.wait_ge(st[i % 2], 16 * (i // 2))
                    terms = ([bias[:, :]] if bias is not None else []) + [r[:, i % 2, :] for r in res]
                    cur = ps[0:TN, i % 4, 0:width]
                    out = y[:, i % 2, :]
                    if not terms:
                        ins = dve.tensor_copy(out, cur)
                    for n, t in enumerate(terms):
                        ins = dve.tensor_tensor(out, cur, t, ALU.add)
                        cur = out
                        if n < len(terms) - 1:
                            own.step(ins)
                    ins.then_inc(added, 1)


def project_features(nc, c, src_t, w_d, bias_d, nout, dst_t, residual_t=None, func=None, pick=None):
    with ExitStack() as ctx:
        sb = lambda name, shape, dt=F32: ctx.enter_context(nc.sbuf_tensor(f"{name}_{nc.next_id()}", shape, dt))
        w = sb("pf_w", [128, DC, 128 * nout])
        bias = sb("pf_bias", [128, nout])
        ps = ctx.enter_context(nc.psum_tensor(f"pf_ps_{nc.next_id()}", [128, 6, 512], F32))
        units = [(o, s) for o in range(nout) for s in COLS]
        with stage(nc, "weights", "summed", "done") as (block, weights, summed, done):
            @block.sync
            def _(sp):
                e = sp.value_load(pick, min_val=0, max_val=3) if pick is not None else None
                sp.dma_start(w[:, :, :], w_d(e)).then_inc(weights, 16)
                sp.dma_start(bias[:, :], bias_d(e)).then_inc(weights, 16)
                sp.wait_ge(weights, 32)

            @block.tensor
            def _(pe):
                pe.wait_ge(weights, 32)
                for u, (o, s) in enumerate(units):
                    if u >= 6:
                        pe.wait_ge(done, u - 5)
                    for k in range(DC):
                        ins = pe.matmul(ps[:, u % 6, 0:s.stop - s.start], w[:, k, 128 * o:128 * o + 128],
                                        src_t[:, k, s], start=(k == 0), stop=(k == DC - 1))
                    ins.then_inc(summed, 1)

            if func is None:
                @block.vector
                def _(dve):
                    dve.wait_ge(weights, 32)
                    for u, (o, s) in enumerate(units):
                        dve.wait_ge(summed, u + 1)
                        cur = ps[:, u % 6, 0:s.stop - s.start]
                        if residual_t is None:
                            ins = dve.tensor_scalar(dst_t[:, o, s], cur, bias[:, o:o + 1], None, ALU.add)
                        else:
                            ins = dve.scalar_tensor_tensor(dst_t[:, o, s], cur, bias[:, o:o + 1],
                                                           residual_t[:, o, s], ALU.add, ALU.add)
                        ins.then_inc(done, 1)
            else:
                @block.scalar
                def _(act):
                    act.wait_ge(weights, 32)
                    for u, (o, s) in enumerate(units):
                        act.wait_ge(summed, u + 1)
                        act.activation(dst_t[:, o, s], ps[:, u % 6, 0:s.stop - s.start], func,
                                       bias=bias[:, o:o + 1]).then_inc(done, 1)


def attention(nc, c, q_src, kv_src, out_t, wq_d, wk_d, wv_d, bq_d, bk_d, bv_d, causal=False, pick=None):
    biased = bq_d is not None
    with ExitStack() as ctx:
        sb = lambda name, shape, dt=F32: ctx.enter_context(nc.sbuf_tensor(f"{name}_{nc.next_id()}", shape, dt))
        wq, wk, wv = (sb(f"at_w{n}", [128, DC, 128]) for n in "qkv")
        bq, bk = sb("at_bq", [128, 1]), sb("at_bk", [128, 1])
        bv = sb("at_bv", [TN, 128])
        q_pad = [sb("at_qa", [128, N]), sb("at_qb", [128, N])]
        k_t = sb("at_k", [128, N])
        v = sb("at_v", [TN, NT, 128])
        p = sb("at_p", [TN, 2, N])
        p_t = sb("at_pt", [TN, 2, NT, TN])
        o = sb("at_o", [TN, NT, 128])
        neg_max = sb("at_max", [TN, 2 * NT])
        shift = sb("at_shift", [TN, 2 * NT])
        total = sb("at_sum", [TN, 2 * NT])
        inverse = sb("at_inv", [TN, 2 * NT])
        pscore = ctx.enter_context(nc.psum_tensor(f"at_ps_{nc.next_id()}", [128, 3, 512], F32))
        pturn = ctx.enter_context(nc.psum_tensor(f"at_pt_{nc.next_id()}", [128, 3, 512], F32))
        pout = ctx.enter_context(nc.psum_tensor(f"at_po_{nc.next_id()}", [128, 2, 512], F32))
        score = pscore[:, :, :].rearrange("p a b -> p (a b)")
        units = [(h, i) for h in range(2) for i in range(NT)]
        NU = len(units)
        keys = [(i + 1 if causal else NT) for _, i in units]
        copies = [-(-n // 4) for n in keys]
        upto = lambda u: sum(copies[:u])

        with stage(nc, "zeroed") as (block, zeroed):
            @block.vector
            def _(dve):
                dve.memset(q_pad[0][64:128, :], 0.0).then_inc(zeroed, 1)
                dve.memset(q_pad[1][0:64, :], 0.0).then_inc(zeroed, 1)
                if not biased:
                    for b in (bq, bk, bv):
                        dve.memset(b[:, :], 0.0).then_inc(zeroed, 1)
                dve.wait_ge(zeroed, 2 if biased else 5)

        with nc.Fori(0, HEADS // 2) as pair:
            with stage(nc, "weights", "q_sum", "k_sum", "v_sum", "q_done", "k_done", "v_done", "scored", "max_own",
                       "max_ready", "exp_done", "turned", "pt_ready", "pv_done", "o_own", "o_ready", "o_turned",
                       "o_stored") as (
                    block, weights, q_sum, k_sum, v_sum, q_done, k_done, v_done, scored, max_own, max_ready,
                    exp_done, turned, pt_ready, pv_done, o_own, o_ready, o_turned, o_stored):
                NW = 96 if biased else 48

                @block.sync
                def _(sp):
                    e = sp.value_load(pick, min_val=0, max_val=3) if pick is not None else None
                    for dst, src in ((wq, wq_d), (wk, wk_d), (wv, wv_d)):
                        sp.dma_start(dst[:, :, :], src(e, pair)).then_inc(weights, 16)
                    if biased:
                        sp.dma_start(bq[:, :], bq_d(e, pair)).then_inc(weights, 16)
                        sp.dma_start(bk[:, :], bk_d(e, pair)).then_inc(weights, 16)
                        sp.dma_start(bv[:, :], bv_d(e, pair).to_broadcast((TN, 128))).then_inc(weights, 16)
                    sp.wait_ge(weights, NW)

                @block.tensor
                def _(pe):
                    pe.wait_ge(weights, NW)
                    for w, src, dst, ready in ((wq, q_src, pscore, q_sum), (wk, kv_src, pturn, k_sum)):
                        for n, s in enumerate(COLS):
                            for k in range(DC):
                                ins = pe.matmul(dst[:, n, 0:s.stop - s.start], w[:, k, :], src[:, k, s],
                                                start=(k == 0), stop=(k == DC - 1))
                            ins.then_inc(ready, 1)
                    for i in range(NT):
                        if i == 8:
                            pe.wait_ge(q_done, 2)
                        dst = pout[0:TN, i // 4, 128 * (i % 4):128 * (i % 4) + 128] if i < 8 \
                            else pscore[0:TN, 0, 128 * (i - 8):128 * (i - 8) + 128]
                        for k in range(DC):
                            ins = pe.matmul(dst, kv_src[:, k, TN * i:TN * i + TN], wv[:, k, :],
                                            start=(k == 0), stop=(k == DC - 1))
                        ins.then_inc(v_sum, 1)
                    pe.wait_ge(q_done, 6)
                    pe.wait_ge(k_done, 3)
                    pe.wait_ge(v_done, 3)
                    for u in range(NU + 2):
                        if u < NU:
                            h, i = units[u]
                            if u >= 1:
                                pe.wait_ge(exp_done, u)
                            for a in range(0, TN * keys[u], 512):
                                b = min(a + 512, TN * keys[u])
                                ins = pe.matmul(score[0:TN, a:b], q_pad[h][:, TN * i:TN * i + TN], k_t[:, a:b],
                                                start=True, stop=True)
                            ins.then_inc(scored, 1)
                        if 1 <= u <= NU:
                            t = u - 1
                            pe.wait_ge(exp_done, t + 1)
                            for j in range(keys[t]):
                                if j % 4 == 0 and t >= 1 and j // 4 < copies[t - 1]:
                                    pe.wait_ge(pt_ready, upto(t - 1) + j // 4 + 1)
                                ins = pe.transpose(pturn[0:TN, j // 4, TN * (j % 4):TN * (j % 4) + TN],
                                                   p[:, t % 2, TN * j:TN * j + TN], c.ident[0:TN, 0:TN])
                                if j % 4 == 3 or j == keys[t] - 1:
                                    ins.then_inc(turned, 1)
                        if u >= 2:
                            t = u - 2
                            h, i = units[t]
                            pe.wait_ge(pt_ready, upto(t + 1))
                            if t >= 2:
                                pe.wait_ge(o_ready, t - 1)
                            for j in range(keys[t]):
                                ins = pe.matmul(pout[0:TN, t % 2, 0:HD], p_t[:, t % 2, j, :],
                                                v[:, j, HD * h:HD * h + HD], start=(j == 0), stop=(j == keys[t] - 1))
                            ins.then_inc(pv_done, 1)
                    pe.wait_ge(o_ready, NU)
                    for i in range(NT):
                        ins = pe.transpose(pturn[:, i // 4, TN * (i % 4):TN * (i % 4) + TN], o[:, i, :],
                                           c.ident[0:TN, 0:TN])
                        if i % 4 == 3 or i == NT - 1:
                            ins.then_inc(o_turned, 1)

                @block.scalar
                def _(act):
                    act.wait_ge(weights, NW)
                    for n, s in enumerate(COLS):
                        act.wait_ge(q_sum, n + 1)
                        for h in range(2):
                            r = slice(64 * h, 64 * h + 64)
                            act.activation(q_pad[h][r, s], pscore[r, n, 0:s.stop - s.start], ACT.Identity,
                                           bias=bq[r, 0:1]).then_inc(q_done, 1)
                    for u in range(NU):
                        act.wait_ge(max_ready, u + 1)
                        if u >= 2:
                            act.wait_ge(turned, upto(u - 1))
                        w = TN * keys[u]
                        act.activation(p[:, u % 2, 0:w], score[0:TN, 0:w], ACT.Exp, bias=shift[:, u:u + 1],
                                       scale=HD ** -0.5, accum_out=total[:, u:u + 1]).then_inc(exp_done, 1)
                    for n in range(3):
                        act.wait_ge(o_turned, n + 1)
                        w = min(4 * TN, N - 4 * TN * n)
                        act.activation(out_t[:, bass.ds(pair, 1), 4 * TN * n:4 * TN * n + w]
                                       .rearrange("p a n -> p (a n)"), pturn[:, n, 0:w], ACT.Copy).then_inc(o_stored, 1)
                    act.wait_ge(o_stored, 3)

                @block.vector
                def _(dve):
                    own = Chain(dve, max_own)
                    dve.wait_ge(weights, NW)
                    for n, s in enumerate(COLS):
                        dve.wait_ge(k_sum, n + 1)
                        dve.tensor_scalar(k_t[:, s], pturn[:, n, 0:s.stop - s.start], bk[:, 0:1], None,
                                          ALU.add).then_inc(k_done, 1)
                    for n in range(3):
                        m = min(4, NT - 4 * n)
                        dve.wait_ge(v_sum, 4 * n + m)
                        src = (pout[0:TN, n, 0:128 * m] if n < 2 else pscore[0:TN, 0, 0:128 * m])
                        dve.tensor_tensor(v[:, 4 * n:4 * n + m, :], src.rearrange("p (a b) -> p a b", b=128),
                                          bv[:, :].unsqueeze(1).to_broadcast((TN, m, 128)), ALU.add).then_inc(v_done, 1)
                    for u in range(NU + 2):
                        if u < NU:
                            w = TN * keys[u]
                            dve.wait_ge(scored, u + 1)
                            if causal:
                                diag = score[0:TN, w - TN:w]
                                own.step(dve.tensor_tensor(diag, diag, c.causal[:, :], ALU.add))
                            own.step(dve.tensor_reduce(neg_max[:, u:u + 1], score[0:TN, 0:w], AX, ALU.max, negate=True))
                            dve.tensor_scalar(shift[:, u:u + 1], neg_max[:, u:u + 1], HD ** -0.5, None,
                                              ALU.mult).then_inc(max_ready, 1)
                        if 1 <= u <= NU:
                            t = u - 1
                            if t >= 2:
                                dve.wait_ge(pv_done, t - 1)
                            for n in range(copies[t]):
                                dve.wait_ge(turned, upto(t) + n + 1)
                                m = min(4, keys[t] - 4 * n)
                                dve.tensor_copy(p_t[:, t % 2, 4 * n:4 * n + m, :],
                                                pturn[0:TN, n, 0:TN * m].rearrange("p (a b) -> p a b", b=TN))\
                                    .then_inc(pt_ready, 1)
                        if u >= 2:
                            t = u - 2
                            h, i = units[t]
                            dve.wait_ge(exp_done, t + 1)
                            dve.reciprocal(inverse[:, t:t + 1], total[:, t:t + 1]).then_inc(o_own, 1)
                            dve.wait_ge(o_own, t + 1)
                            dve.wait_ge(pv_done, t + 1)
                            dve.tensor_scalar(o[:, i, HD * h:HD * h + HD], pout[0:TN, t % 2, 0:HD],
                                              inverse[:, t:t + 1], None, ALU.mult).then_inc(o_ready, 1)


def sort_edges(nc, c, key_d, other_d, w_d, a4_d, a8_d, table_d, tile_base):
    with ExitStack() as ctx:
        sb = lambda name, shape, dt=F32: ctx.enter_context(nc.sbuf_tensor(f"{name}_{nc.next_id()}", shape, dt))
        key = sb("so_key", [TN, EC], I32)
        rows = sb("so_rows", [TN, EC, ROW])
        rows_i = rows[:, :, :].bitcast(I32)
        other = sb("so_other", [TN, EC], I32)
        w = sb("so_w", [TN, EC])
        a4 = sb("so_a4", [TN, EC * 4])
        a8 = sb("so_a8", [TN, EC * 8])
        zero = sb("so_zero", [128, NS * ROW])
        keyf = sb("so_keyf", [TN, EC])
        bucket = sb("so_bucket", [TN, EC])
        oh = sb("so_oh", [TN, NT, EC], BF16)
        flat = sb("so_flat", [128, NT * EC])
        run = sb("so_run", [128, NT * EC])
        start = sb("so_start", [128, NT + 1])
        count = sb("so_count", [128, NT])
        count_i = sb("so_counti", [128, NT], I32)
        ntile = sb("so_ntile", [128, NT])
        off = sb("so_off", [128, NT])
        delta = sb("so_delta", [128, NT])
        val = sb("so_val", [TN, NT, EC])
        slot = sb("so_slot", [TN, EC])
        slot_i = sb("so_sloti", [TN, EC], I32)
        part_i = sb("so_parti", [TN, EC], I32)
        tile_i = sb("so_tilei", [TN, EC], I32)
        base = sb("so_base", [128, NS])
        ps = ctx.enter_context(nc.psum_tensor(f"so_ps_{nc.next_id()}", [128, 8, 512], F32))
        B = 3 * EC
        banks = [(n, 3 * n, min(3, NT - 3 * n)) for n in range(-(-NT // 3))]
        row3 = lambda d: d.rearrange("(p t) c -> p (t c)", p=TN)
        with stage(nc, "loaded", "own", "zeroed", "hot", "counted", "placed", "filled", "sent") as (
                block, loaded, own_s, zeroed, hot, counted, placed, filled, sent):
            @block.sync
            def _(sp):
                sp.dma_start(key[:, :], key_d.rearrange("(p t) -> p t", p=TN)).then_inc(loaded, 16)
                sp.dma_start(other[:, :], other_d.rearrange("(p t) -> p t", p=TN)).then_inc(loaded, 16)
                sp.dma_start(w[:, :], w_d.rearrange("(p t) -> p t", p=TN)).then_inc(loaded, 16)
                sp.dma_start(a4[:, :], row3(a4_d)).then_inc(loaded, 16)
                sp.dma_start(a8[:, :], row3(a8_d)).then_inc(loaded, 16)
                sp.wait_ge(zeroed, 1)
                sp.dma_start(table_d.rearrange("(p t) c -> p (t c)", p=128), zero[:, :]).then_inc(filled, 16)
                sp.wait_ge(filled, 16)

            @block.tensor
            def _(pe):
                pe.wait_ge(hot, NT)
                for n, j, m in banks:
                    pe.matmul(ps[:, n, 0:m * EC], c.ones[0:TN, :], oh[:, j:j + m, :].rearrange("p a b -> p (a b)"),
                              start=True, stop=True).then_inc(counted, 1)
                for n, j, m in banks:
                    pe.matmul(ps[0:TN, 4 + n, 0:m * EC], c.lower[0:TN, 0:TN],
                              oh[:, j:j + m, :].rearrange("p a b -> p (a b)"), start=True, stop=True).then_inc(counted, 1)

            @block.vector
            def _(dve):
                dve.memset(zero[:, :], 0.0).then_inc(zeroed, 1)
                own = Chain(dve, own_s)
                dve.wait_ge(loaded, 80)
                own.mark(dve.tensor_copy(rows_i[:, :, 0], other[:, :]))
                own.mark(dve.tensor_copy(rows[:, :, 2], w[:, :]))
                own.mark(dve.memset(rows[:, :, 3], 0.0))
                own.mark(dve.tensor_copy(rows[:, :, 4:8], a4[:, :].rearrange("p (t c) -> p t c", c=4)))
                own.mark(dve.tensor_copy(rows[:, :, 8:16], a8[:, :].rearrange("p (t c) -> p t c", c=8)))
                own.step(dve.tensor_copy(keyf[:, :], key[:, :]))
                own.step(dve.tensor_scalar(bucket[:, :], keyf[:, :], float(TN), None, ALU.is_ge))
                for j in range(2, NT):
                    own.step(dve.scalar_tensor_tensor(bucket[:, :], keyf[:, :], float(TN * j), bucket[:, :],
                                                      ALU.is_ge, ALU.add))
                own.mark(dve.scalar_tensor_tensor(rows[:, :, 1], bucket[:, :], -float(TN), keyf[:, :],
                                                  ALU.mult, ALU.add))
                for j in range(NT):
                    dve.tensor_scalar(oh[:, j, :], bucket[:, :], float(j), None, ALU.is_equal).then_inc(hot, 1)
                for n, j, m in banks:
                    dve.wait_ge(counted, n + 1)
                    own.mark(dve.tensor_copy(flat[:, j * EC:(j + m) * EC], ps[:, n, 0:m * EC]))
                own.join()
                own.step(dve.tensor_tensor_scan(run[:, :], flat[:, :], flat[:, :], 0.0, ALU.add, ALU.bypass))
                own.mark(dve.memset(start[:, 0:1], 0.0))
                own.mark(dve.tensor_copy(start[:, 1:NT + 1],
                                         run[:, :].rearrange("p (j t) -> p j t", j=NT)[:, :, EC - 1]))
                own.join()
                own.mark(dve.tensor_tensor(run[:, :], run[:, :], flat[:, :], ALU.subtract))
                own.step(dve.tensor_tensor(count[:, :], start[:, 1:NT + 1], start[:, 0:NT], ALU.subtract))
                own.step(dve.tensor_scalar(count_i[:, :], count[:, :], float(TE - 1), None, ALU.add))
                own.step(dve.tensor_scalar(count_i[:, :], count_i[:, :], TE.bit_length() - 1, None,
                                           ALU.arith_shift_right))
                own.step(dve.tensor_copy(ntile[:, :], count_i[:, :]))
                own.step(dve.tensor_tensor_scan(off[:, :], ntile[:, :], ntile[:, :], 0.0, ALU.add, ALU.bypass))
                own.step(dve.tensor_tensor(off[:, :], off[:, :], ntile[:, :], ALU.subtract))
                own.step(dve.scalar_tensor_tensor(delta[:, :], off[:, :], float(TE), start[:, 0:NT],
                                                  ALU.mult, ALU.subtract))
                own.step(dve.tensor_scalar(base[:, :], c.iota[:, 0:NS], off[:, 1:2], None, ALU.is_ge))
                for j in range(2, NT):
                    own.step(dve.scalar_tensor_tensor(base[:, :], c.iota[:, 0:NS], off[:, j:j + 1], base[:, :],
                                                      ALU.is_ge, ALU.add))
                own.mark(dve.tensor_copy(tile_base[:, :], base[0:1, :]))
                dve.wait_ge(counted, 8)
                for n, j, m in banks:
                    own.mark(dve.tensor_tensor(val[:, j:j + m, :].rearrange("p a b -> p (a b)"),
                                               run[0:TN, j * EC:(j + m) * EC], ps[0:TN, 4 + n, 0:m * EC], ALU.add))
                own.join()
                for j in range(NT):
                    own.mark(dve.scalar_tensor_tensor(val[:, j, :], val[:, j, :], delta[0:TN, j:j + 1], oh[:, j, :],
                                                      ALU.add, ALU.mult))
                own.join()
                own.step(dve.tensor_reduce(slot[:, :], val[:, :, :].rearrange("p j t -> p t j"), AX, ALU.add))
                own.step(dve.tensor_copy(slot_i[:, :], slot[:, :]))
                own.mark(dve.tensor_scalar(part_i[:, :], slot_i[:, :], TE - 1, None, ALU.bitwise_and))
                own.mark(dve.tensor_scalar(tile_i[:, :], slot_i[:, :], TE.bit_length() - 1, None, ALU.arith_shift_right))
                own.join()
                dve.scalar_tensor_tensor(slot_i[:, :], part_i[:, :], float(NS), tile_i[:, :],
                                         ALU.mult, ALU.add).then_inc(placed, 1)

            @block.gpsimd
            def _(pool):
                pool.wait_ge(placed, 1)
                pool.wait_ge(filled, 16)
                for t in range(EC):
                    pool.indirect_dma_start(table_d, bass.IndirectOffsetOnAxis(ap=slot_i[:, t:t + 1], axis=0),
                                            rows[:, t, :], None).then_inc(sent, 16)
                pool.wait_ge(sent, 16 * EC)


def graph_sum0(nc, c, table_d, tile_base, support_d, x_d, bias_d, out_d):
    with ExitStack() as ctx:
        sb = lambda name, shape, dt=F32: ctx.enter_context(nc.sbuf_tensor(f"{name}_{nc.next_id()}", shape, dt))
        acc = sb("g0_acc", [TN, NT, D])
        bias = sb("g0_bias", [TN, D])
        edges = sb("g0_edges", [128, GE, ROW])
        got = sb("g0_got", [128, GE, D])
        hot = sb("g0_hot", [128, GE, TN])
        ps = ctx.enter_context(nc.psum_tensor(f"g0_ps_{nc.next_id()}", [128, 4, 512], F32))
        with stage(nc, "loaded", "own") as (block, loaded, own_s):
            @block.sync
            def _(sp):
                sp.dma_start(acc[:, :, :], tiles_of(x_d)).then_inc(loaded, 16)
                sp.dma_start(bias[:, :], bias_d.to_broadcast((TN, D))).then_inc(loaded, 16)

            @block.vector
            def _(dve):
                dve.wait_ge(loaded, 32)
                for i in range(NT):
                    dve.tensor_tensor(acc[:, i, :], acc[:, i, :], bias[:, :], ALU.add).then_inc(own_s, 1)
                dve.wait_ge(own_s, NT)
        table = table_d.rearrange("(p t) c -> p t c", p=128)
        with nc.Fori(0, GROUPS) as g:
            with stage(nc, "loaded", "hot_ready", "summed", "added", *(f"got{i}" for i in range(GE))) as (
                    block, loaded, hot_ready, summed, added, *got_s):
                @block.sync
                def _(sp):
                    sp.dma_start(edges[:, :, :], table[:, bass.ds(g * GE, GE), :]).then_inc(loaded, 16)
                    sp.wait_ge(loaded, 16)

                @block.gpsimd
                def _(pool):
                    pool.wait_ge(loaded, 16)
                    ids = edges[:, :, :].bitcast(I32)
                    for i in range(GE):
                        pool.indirect_dma_start(got[:, i, :], None, support_d,
                                                bass.IndirectOffsetOnAxis(ap=ids[:, i, 0:1], axis=0)).then_inc(got_s[i], 16)

                @block.vector
                def _(dve):
                    dve.wait_ge(loaded, 16)
                    for i in range(GE):
                        dve.tensor_scalar(hot[:, i, :], c.iota[:, 0:TN], edges[:, i, 1:2], edges[:, i, 2:3],
                                          ALU.is_equal, ALU.mult).then_inc(hot_ready, 1)
                    for i in range(GE):
                        at = dve.value_load(tile_base[0:1, bass.ds(g * GE + i, 1)], min_val=0, max_val=NT - 1)
                        dve.wait_ge(summed, i + 1)
                        if i:
                            dve.wait_ge(added, i)
                        dst = acc[:, bass.ds(at, 1), :].rearrange("p a b -> p (a b)")
                        dve.tensor_tensor(dst, dst, ps[0:TN, i % 4, :], ALU.add).then_inc(added, 1)
                    dve.wait_ge(added, GE)

                @block.tensor
                def _(pe):
                    for i in range(GE):
                        pe.wait_ge(hot_ready, i + 1)
                        pe.wait_ge(got_s[i], 16)
                        if i >= 4:
                            pe.wait_ge(added, i - 3)
                        pe.matmul(ps[0:TN, i % 4, :], hot[:, i, :], got[:, i, :], start=True, stop=True).then_inc(summed, 1)
        with stage(nc, "stored") as (block, stored):
            @block.sync
            def _(sp):
                sp.dma_start(tiles_of(out_d), acc[:, :, :]).then_inc(stored, 16)
                sp.wait_ge(stored, 16)


def route_tokens(nc, c, xn_t, wr_d, b2_d, slot_tok, y_row, gate, moe_bias_d):
    with ExitStack() as ctx:
        sb = lambda name, shape, dt=F32: ctx.enter_context(nc.sbuf_tensor(f"{name}_{nc.next_id()}", shape, dt))
        wr = sb("rt_w", [128, DC, EXPERTS])
        b2 = sb("rt_b2", [EXPERTS, D])
        logit = sb("rt_logit", [TN, NT, EXPERTS])
        probs = sb("rt_probs", [TN, NT, EXPERTS])
        small = sb("rt_small", [TN, 4, NT])
        top = sb("rt_top", [TN, NT, 8])
        idx = sb("rt_idx", [TN, NT, 8], U32)
        expert = sb("rt_expert", [TN, 2, NT])
        hot = sb("rt_hot", [TN, 2, NT, EXPERTS], BF16)
        both = sb("rt_both", [TN, NT, EXPERTS], BF16)
        before = sb("rt_before", [TN, NT, EXPERTS])
        mine = sb("rt_mine", [TN, NT, EXPERTS])
        pos = sb("rt_pos", [TN, 2, NT])
        keep = sb("rt_keep", [TN, 2, NT])
        place = sb("rt_place", [TN, 2, NT, CAP])
        named = sb("rt_named", [TN, 2, NT, EXPERTS])
        spread = sb("rt_spread", [TN, NT, EXPERTS])
        spread_t = sb("rt_spreadt", [EXPERTS, NT, TN])
        yb = sb("rt_yb", [TN, NT, D])
        ps = ctx.enter_context(nc.psum_tensor(f"rt_ps_{nc.next_id()}", [128, 8, 512], F32))
        with stage(nc, "loaded", "own", "logits", "shifted", "exps", "hot_ready", "ranked", "named_ready", "tokens",
                   "spread_ready", "turned", "copied", "biased", "kept", "stored") as (
                block, loaded, own_s, logits, shifted, exps, hot_ready, ranked, named_ready, tokens, spread_ready,
                turned, copied, biased, kept, stored):
            @block.sync
            def _(sp):
                sp.dma_start(wr[:, :, :], wr_d).then_inc(loaded, 16)
                sp.dma_start(b2[:, :], b2_d).then_inc(loaded, 16)
                sp.wait_ge(kept, NT)
                sp.dma_start(tiles_of(moe_bias_d), yb[:, :, :]).then_inc(stored, 16)
                sp.wait_ge(stored, 16)

            @block.tensor
            def _(pe):
                pe.wait_ge(loaded, 32)
                for i in range(NT):
                    for k in range(DC):
                        ins = pe.matmul(ps[0:TN, i // 8, EXPERTS * (i % 8):EXPERTS * (i % 8) + EXPERTS],
                                        xn_t[:, k, TN * i:TN * i + TN], wr[:, k, :], start=(k == 0), stop=(k == DC - 1))
                    ins.then_inc(logits, 1)
                pe.wait_ge(hot_ready, 1)
                for i in range(NT):
                    dst = ps[0:TN, 2 + i // 8, EXPERTS * (i % 8):EXPERTS * (i % 8) + EXPERTS]
                    for j in range(i):
                        pe.matmul(dst, c.ones[0:TN, 0:TN], both[:, j, :], start=(j == 0), stop=False)
                    pe.matmul(dst, c.lower[0:TN, 0:TN], both[:, i, :], start=(i == 0), stop=True).then_inc(ranked, 1)
                pe.wait_ge(named_ready, 1)
                for n in range(2 * NT):
                    ins = pe.matmul(ps[0:CAP, 4, 0:EXPERTS], place[:, n % 2, n // 2, :], named[:, n % 2, n // 2, :],
                                    start=(n == 0), stop=(n == 2 * NT - 1))
                ins.then_inc(tokens, 1)
                pe.wait_ge(spread_ready, 1)
                for i in range(NT):
                    pe.transpose(ps[0:EXPERTS, 5, 0:TN], spread[:, i, :],
                                 c.ident[0:TN, 0:TN]).then_inc(turned, 1)
                    pe.wait_ge(copied, i + 1)
                    if i >= 2:
                        pe.wait_ge(kept, i - 1)
                    pe.matmul(ps[0:TN, 6 + i % 2, :], spread_t[:, i, :], b2[:, :], start=True, stop=True).then_inc(biased, 1)

            @block.scalar
            def _(act):
                act.wait_ge(shifted, 1)
                act.activation(probs[:, :, :], logit[:, :, :], ACT.Exp).then_inc(exps, 1)
                for i in range(NT):
                    act.wait_ge(turned, i + 1)
                    act.activation(spread_t[:, i, :], ps[0:EXPERTS, 5, 0:TN], ACT.Copy)\
                        .then_inc(copied, 1)
                    act.wait_ge(biased, i + 1)
                    act.activation(yb[:, i, :], ps[0:TN, 6 + i % 2, :], ACT.Copy).then_inc(kept, 1)

            @block.vector
            def _(dve):
                own = Chain(dve, own_s)
                peak, total, inv, pair = (small[:, n, :] for n in range(4))
                bc = lambda a, n: a.unsqueeze(2).to_broadcast((TN, NT, n))
                dve.wait_ge(logits, NT)
                for i in range(0, NT, 8):
                    m = min(8, NT - i)
                    own.mark(dve.tensor_copy(logit[:, i:i + m, :], ps[0:TN, i // 8, 0:EXPERTS * m]
                                             .rearrange("p (a b) -> p a b", b=EXPERTS)))
                own.join()
                own.step(dve.tensor_reduce(peak, logit[:, :, :], AX, ALU.max))
                dve.tensor_tensor(logit[:, :, :], logit[:, :, :], bc(peak, EXPERTS), ALU.subtract).then_inc(shifted, 1)
                dve.wait_ge(exps, 1)
                own.step(dve.tensor_reduce(total, probs[:, :, :], AX, ALU.add))
                own.step(dve.reciprocal(inv, total))
                own.step(dve.tensor_tensor(probs[:, :, :], probs[:, :, :], bc(inv, EXPERTS), ALU.mult))
                for i in range(NT):
                    own.mark(dve.max(top[:, i, :], probs[:, i, :]))
                own.join()
                for i in range(NT):
                    own.mark(dve.max_index(idx[:, i, :], top[:, i, :], probs[:, i, :]))
                own.step(dve.tensor_tensor(pair, top[:, :, 0], top[:, :, 1], ALU.add))
                own.step(dve.reciprocal(pair, pair))
                for k in range(2):
                    own.mark(dve.tensor_copy(expert[:, k, :], idx[:, :, k]))
                    own.mark(dve.tensor_tensor(gate[:, k, :], top[:, :, k], pair, ALU.mult))
                own.join()
                for k in range(2):
                    for i in range(NT):
                        own.mark(dve.tensor_scalar(hot[:, k, i, :], c.iota[0:TN, 0:EXPERTS], expert[:, k, i:i + 1],
                                                   None, ALU.is_equal))
                own.join()
                dve.tensor_tensor(both[:, :, :], hot[:, 0, :, :], hot[:, 1, :, :], ALU.add).then_inc(hot_ready, 1)
                dve.wait_ge(ranked, NT)
                for i in range(0, NT, 8):
                    m = min(8, NT - i)
                    own.mark(dve.tensor_copy(before[:, i:i + m, :], ps[0:TN, 2 + i // 8, 0:EXPERTS * m]
                                             .rearrange("p (a b) -> p a b", b=EXPERTS)))
                own.join()
                for k in range(2):
                    own.step(dve.tensor_tensor(mine[:, :, :], before[:, :, :], hot[:, k, :, :], ALU.mult))
                    own.step(dve.tensor_reduce(pos[:, k, :], mine[:, :, :], AX, ALU.add))
                for k in range(2):
                    for i in range(NT):
                        own.mark(dve.tensor_scalar(place[:, k, i, :], c.iota[0:TN, 0:CAP], pos[:, k, i:i + 1], None,
                                                   ALU.is_equal))
                        own.mark(dve.tensor_scalar(named[:, k, i, :], c.iota[0:TN, 0:EXPERTS], expert[:, k, i:i + 1],
                                                   c.node[0:TN, i:i + 1], ALU.is_equal, ALU.mult))
                own.join()
                dve.engine_nop().then_inc(named_ready, 1)
                own.step(dve.tensor_scalar(keep[:, :, :], pos[:, :, :], float(CAP), None, ALU.is_lt))
                own.mark(dve.tensor_tensor(gate[:, :, :], gate[:, :, :], keep[:, :, :], ALU.mult))
                own.step(dve.tensor_scalar(pos[:, :, :], pos[:, :, :], float(CAP - 1), None, ALU.min))
                own.step(dve.scalar_tensor_tensor(y_row[:, :, :], expert[:, :, :], float(CAP), pos[:, :, :],
                                                  ALU.mult, ALU.add))
                for i in range(NT):
                    own.mark(dve.tensor_scalar(spread[:, i, :], c.iota[0:TN, 0:EXPERTS], expert[:, 0, i:i + 1],
                                               gate[:, 0, i:i + 1], ALU.is_equal, ALU.mult))
                    own.mark(dve.tensor_scalar(mine[:, i, :], c.iota[0:TN, 0:EXPERTS], expert[:, 1, i:i + 1],
                                               gate[:, 1, i:i + 1], ALU.is_equal, ALU.mult))
                own.join()
                dve.tensor_tensor(spread[:, :, :], spread[:, :, :], mine[:, :, :], ALU.add).then_inc(spread_ready, 1)
                dve.wait_ge(tokens, 1)
                own.step(dve.tensor_copy(slot_tok[:, :], ps[0:CAP, 4, 0:EXPERTS]))


def run_experts(nc, c, z_d, slot_tok, w1_d, w2_d, y_d):
    HALF = 4
    TURN = 2 * HALF
    with ExitStack() as ctx:
        sb = lambda name, shape, dt=F32: ctx.enter_context(nc.sbuf_tensor(f"{name}_{nc.next_id()}", shape, dt))
        w1 = sb("mo_w1", [128, 2, HALF, DC, FF])
        w2 = sb("mo_w2", [128, 2, HALF, FF // 128, D])
        ids = sb("mo_ids", [CAP, EXPERTS], I32)
        ids_now = sb("mo_idsnow", [CAP, TURN], I32)
        b1_now = sb("mo_b1", [128, TURN * FF // 128])
        x = sb("mo_x", [CAP, TURN, D])
        x_t = sb("mo_xt", [128, 2, DC, CAPW])
        h_t = sb("mo_ht", [128, 2, FF // 128, CAPW])
        y = sb("mo_y", [CAP, 2, D])
        pt = ctx.enter_context(nc.psum_tensor(f"mo_pt_{nc.next_id()}", [128, 2, 512], F32))
        ph = ctx.enter_context(nc.psum_tensor(f"mo_ph_{nc.next_id()}", [128, 2, 512], F32))
        py = ctx.enter_context(nc.psum_tensor(f"mo_py_{nc.next_id()}", [128, 2, 512], F32))
        w1_v = w1_d.rearrange("e (k p) f -> p e k f", p=128)
        w2_v = w2_d.rearrange("e (k p) f -> p e k f", p=128)

        with stage(nc, "ready", "loaded") as (block, ready, loaded):
            @block.vector
            def _(dve):
                dve.tensor_copy(ids[:, :], slot_tok[:, :]).then_inc(ready, 1)
                dve.memset(x_t[:, :, :, :], 0.0).then_inc(ready, 1)
                dve.wait_ge(ready, 2)

            @block.sync
            def _(sp):
                load_one(sp, w1[:, 0], w1_v, 0, HALF, loaded)
                load_one(sp, w2[:, 0], w2_v, 0, HALF, loaded)
                sp.wait_ge(loaded, 16 * 2 * HALF)

        def turn(g, last):
            with stage(nc, "ids_ready", "first_done", "half1", "half0", "turned", "xt_ready", "h_sum", "h_ready",
                       "y_sum", "y_ready", "y0", "y1", *(f"got{i}" for i in range(TURN))) as (
                    block, ids_ready, first_done, half1, half0, turned, xt_ready, h_sum, h_ready, y_sum, y_ready,
                    y0, y1, *got_s):
                stores = (y0, y1)

                @block.sync
                def _(sp):
                    load_one(sp, w1[:, 1], w1_v, g * TURN + HALF, HALF, half1)
                    load_one(sp, w2[:, 1], w2_v, g * TURN + HALF, HALF, half1)
                    if not last:
                        sp.wait_ge(first_done, 1)
                        load_one(sp, w1[:, 0], w1_v, g * TURN + TURN, HALF, half0)
                        load_one(sp, w2[:, 0], w2_v, g * TURN + TURN, HALF, half0)
                        sp.wait_ge(half0, 32 * HALF)

                @block.gpsimd
                def _(pool):
                    pool.wait_ge(ids_ready, 1)
                    for e in range(TURN):
                        pool.indirect_dma_start(x[:, e, :], None, z_d,
                                                bass.IndirectOffsetOnAxis(ap=ids_now[:, e:e + 1], axis=0)).then_inc(got_s[e], 16)

                @block.tensor
                def _(pe):
                    for e in range(TURN + 1):
                        if e < TURN:
                            pe.wait_ge(got_s[e], 16)
                            if e >= 2:
                                pe.wait_ge(xt_ready, e - 1)
                            for k in range(DC):
                                ins = pe.transpose(pt[:, e % 2, 128 * k:128 * k + CAP], x[:, e, 128 * k:128 * k + 128],
                                                   c.ident[0:CAP, 0:CAP])
                            ins.then_inc(turned, 1)
                        if e >= 1:
                            f = e - 1
                            if f == HALF:
                                pe.wait_ge(half1, 32 * HALF)
                            pe.wait_ge(xt_ready, f + 1)
                            if f >= 2:
                                pe.wait_ge(h_ready, f - 1)
                            for m in range(FF // 128):
                                for k in range(DC):
                                    ins = pe.matmul(ph[:, f % 2, 128 * m:128 * m + CAPW],
                                                    w1[:, f // HALF, f % HALF, k, 128 * m:128 * m + 128],
                                                    x_t[:, f % 2, k, :], start=(k == 0), stop=(k == DC - 1))
                            ins.then_inc(h_sum, 1)
                            pe.wait_ge(h_ready, f + 1)
                            if f >= 2:
                                pe.wait_ge(y_ready, f - 1)
                            for m in range(FF // 128):
                                ins = pe.matmul(py[0:CAP, f % 2, :], h_t[:, f % 2, m, 0:CAP],
                                                w2[:, f // HALF, f % HALF, m, :], start=(m == 0), stop=(m == FF // 128 - 1))
                            ins.then_inc(y_sum, 1)
                    pe.wait_ge(y_sum, HALF)

                @block.scalar
                def _(act):
                    act.wait_ge(ids_ready, 2)
                    for e in range(TURN + 1):
                        if e < TURN:
                            act.wait_ge(turned, e + 1)
                            if e >= 2:
                                act.wait_ge(h_sum, e - 1)
                            for k in range(DC):
                                ins = act.activation(x_t[:, e % 2, k, 0:CAP], pt[:, e % 2, 128 * k:128 * k + CAP], ACT.Identity,
                                                     bias=c.pcol[:, PCOL["ln2_b"]][:, k:k + 1],
                                                     scale=c.pcol[:, PCOL["ln2_g"]][:, k:k + 1])
                            ins.then_inc(xt_ready, 1)
                        if e >= 1:
                            f = e - 1
                            act.wait_ge(h_sum, f + 1)
                            if f >= 2:
                                act.wait_ge(y_sum, f - 1)
                            for m in range(FF // 128):
                                ins = act.activation(h_t[:, f % 2, m, :], ph[:, f % 2, 128 * m:128 * m + CAPW],
                                                     ACT.Gelu_apprx_tanh, bias=b1_now[:, 2 * f + m:2 * f + m + 1])
                            ins.then_inc(h_ready, 1)

                @block.vector
                def _(dve):
                    dve.tensor_copy(ids_now[:, :], ids[:, bass.ds(g * TURN, TURN)]).then_inc(ids_ready, 1)
                    dve.tensor_copy(b1_now[:, :], c.pcol[:, PCOL["moe_b1"]][:, bass.ds(g * (TURN * 2), TURN * 2)])\
                        .then_inc(ids_ready, 1)
                    for f in range(TURN):
                        dve.wait_ge(y_sum, f + 1)
                        if f == HALF - 1:
                            dve.engine_nop().then_inc(first_done, 1)
                        if f >= 2:
                            dve.wait_ge(stores[f % 2], 16 * (f // 2))
                        dve.tensor_copy(y[:, f % 2, :], py[0:CAP, f % 2, :]).then_inc(y_ready, 1)

                @block.gpsimd
                def _(pool):
                    for f in range(TURN):
                        pool.wait_ge(y_ready, f + 1)
                        pool.dma_start(y_d[bass.ds(g * TURN + f, 1), :, :].rearrange("e s d -> (e s) d"),
                                       y[:, f % 2, :]).then_inc(stores[f % 2], 16)
                    for s in stores:
                        pool.wait_ge(s, 16 * TURN // 2)

        with nc.Fori(0, EXPERTS // TURN - 1) as g:
            turn(g, False)
        turn(EXPERTS // TURN - 1, True)


def load_one(sp, dst, src, first, count, sem):
    for e in range(count):
        sp.dma_start(dst[:, e, :, :], src[:, bass.ds(first + e, 1), :, :].rearrange("p e k f -> p (e k) f")).then_inc(sem, 16)


def combine_experts(nc, c, y_d, y_row, gate, parts, out_d):
    with ExitStack() as ctx:
        sb = lambda name, shape, dt=F32: ctx.enter_context(nc.sbuf_tensor(f"{name}_{nc.next_id()}", shape, dt))
        ids = sb("cb_ids", [TN, 2, NT], I32)
        got = sb("cb_got", [TN, 2, NT, D])
        acc = sb("cb_acc", [TN, NT, D])
        part = sb("cb_part", [TN, 2, NT, D])
        rows = y_d.rearrange("e s d -> (e s) d")
        with stage(nc, "ready", "loaded", "loaded1", "got0", "got1", "own", "stored") as (
                block, ready, loaded, loaded1, got0, got1, own_s, stored):
            @block.sync
            def _(sp):
                sp.dma_start(acc[:, :, :], tiles_of(parts[0])).then_inc(loaded, 16)
                for n, d in enumerate(parts[1:]):
                    sp.dma_start(part[:, n, :, :], tiles_of(d)).then_inc(loaded, 16)
                for i in range(NT):
                    sp.wait_ge(own_s, 1 + 4 * (i + 1))
                    sp.dma_start(tiles_of(out_d)[:, i, :], acc[:, i, :]).then_inc(stored, 16)
                sp.wait_ge(stored, 16 * NT)

            @block.gpsimd
            def _(pool):
                pool.wait_ge(ready, 1)
                for i in range(NT):
                    for k in range(2):
                        pool.indirect_dma_start(got[:, k, i, :], None, rows,
                                                bass.IndirectOffsetOnAxis(ap=ids[:, k, i:i + 1], axis=0))\
                            .then_inc((got0, got1)[k], 16)

            @block.vector
            def _(dve):
                own = Chain(dve, own_s)
                dve.tensor_copy(ids[:, :, :], y_row[:, :, :]).then_inc(ready, 1)
                own.n = 1
                dve.engine_nop().then_inc(own_s, 1)
                dve.wait_ge(loaded, 16 * len(parts))
                dve.wait_ge(got0, 16 * NT)
                dve.wait_ge(got1, 16 * NT)
                for i in range(NT):
                    for n in range(2):
                        own.step(dve.tensor_tensor(acc[:, i, :], acc[:, i, :], part[:, n, i, :], ALU.add))
                    for k in range(2):
                        own.step(dve.scalar_tensor_tensor(acc[:, i, :], got[:, k, i, :], gate[:, k, i:i + 1],
                                                          acc[:, i, :], ALU.mult, ALU.add))


def edge_mlp(nc, c, table_d, w_d, h_d):
    HG = GE // 2
    W = HG * TE
    HW = W // 2
    with ExitStack() as ctx:
        sb = lambda name, shape, dt=F32: ctx.enter_context(nc.sbuf_tensor(f"{name}_{nc.next_id()}", shape, dt))
        edges = sb("em_edges", [128, NS, ROW])
        attr = sb("em_attr", [128, NS, 8])
        w1 = sb("em_w1", [GE * 8, HG, 128])
        w23 = sb("em_w23", [128, 2, 128])
        a_t = sb("em_at", [GE * 8, 2, TE])
        h = sb("em_h", [128, 3, 2, W])
        ps = ctx.enter_context(nc.psum_tensor(f"em_ps_{nc.next_id()}", [128, 8, 512], F32))
        with stage(nc, "zeroed", "loaded", "wts", "packed") as (block, zeroed, loaded, wts, packed):
            @block.vector
            def _(dve):
                dve.memset(w1[:, :, :], 0.0).then_inc(zeroed, 1)
                dve.memset(w23[:, :, :], 0.0).then_inc(zeroed, 1)
                dve.wait_ge(loaded, 16)
                dve.tensor_copy(attr[:, :, :], edges[:, :, 8:16]).then_inc(packed, 1)
                dve.wait_ge(packed, 1)

            @block.sync
            def _(sp):
                sp.dma_start(edges[:, :, :], table_d.rearrange("(p t) c -> p t c", p=128)).then_inc(loaded, 16)
                sp.wait_ge(zeroed, 2)
                for i in range(HG):
                    sp.dma_start(w1[8 * i:8 * i + 8, i, 0:64], w_d[0]).then_inc(wts, 16)
                    sp.dma_start(w1[8 * (i + HG):8 * (i + HG) + 8, i, 64:128], w_d[0]).then_inc(wts, 16)
                for n in range(2):
                    sp.dma_start(w23[0:64, n, 0:64], w_d[1 + n]).then_inc(wts, 16)
                    sp.dma_start(w23[64:128, n, 64:128], w_d[1 + n]).then_inc(wts, 16)
                sp.wait_ge(wts, 16 * (2 * HG + 4))
        with stage(nc, "turned", "copied", "s1", "s2", "s3", "a1", "a2", "a3", "st0", "st1") as (
                block, turned, copied, s1, s2, s3, a1, a2, a3, st0, st1):
            s, a, st = (s1, s2, s3), (a1, a2, a3), (st0, st1)
            @block.tensor
            def _(pe):
                for g in range(GROUPS + 3):
                    if g < GROUPS:
                        if g >= 2:
                            pe.wait_ge(copied, g - 1)
                        pe.transpose(ps[0:GE * 8, 6 + g % 2, 0:TE], attr[:, g * GE:(g + 1) * GE, :]
                                     .rearrange("p t c -> p (t c)"), c.ident[:, :]).then_inc(turned, 1)
                    for layer in range(3):
                        t = g - 1 - layer
                        if not 0 <= t < GROUPS:
                            continue
                        if layer == 0:
                            pe.wait_ge(copied, t + 1)
                        else:
                            pe.wait_ge(a[layer - 1], 2 * (t + 1))
                        if t >= 1:
                            pe.wait_ge(a[layer], 2 * t)
                        for half in range(2):
                            dst = ps[:, 2 * layer + half, :]
                            if layer == 0:
                                for i in range(HG):
                                    lo, hi = max(i * TE, half * HW), min((i + 1) * TE, (half + 1) * HW)
                                    if lo < hi:
                                        ins = pe.matmul(dst[:, lo - half * HW:hi - half * HW], w1[:, i, :],
                                                        a_t[:, t % 2, lo - i * TE:hi - i * TE], start=True, stop=True)
                            else:
                                ins = pe.matmul(dst[:, 0:HW], w23[:, layer - 1, :],
                                                h[:, layer - 1, t % 2, half * HW:(half + 1) * HW], start=True, stop=True)
                            ins.then_inc(s[layer], 1)

            @block.vector
            def _(dve):
                for g in range(GROUPS):
                    dve.wait_ge(turned, g + 1)
                    if g >= 2:
                        dve.wait_ge(s1, 2 * (g - 1))
                    dve.tensor_copy(a_t[:, g % 2, :], ps[0:GE * 8, 6 + g % 2, 0:TE]).then_inc(copied, 1)

            @block.scalar
            def _(act):
                for g in range(GROUPS + 3):
                    for layer in range(3):
                        t = g - 1 - layer
                        if not 0 <= t < GROUPS:
                            continue
                        if t >= 2:
                            if layer < 2:
                                act.wait_ge(s[layer + 1], 2 * (t - 1))
                            else:
                                act.wait_ge(st[t % 2], 16 * (t // 2))
                        for half in range(2):
                            act.wait_ge(s[layer], 2 * t + half + 1)
                            act.activation(h[:, layer, t % 2, half * HW:(half + 1) * HW],
                                           ps[:, 2 * layer + half, 0:HW], ACT.Silu,
                                           scale=(8 ** -0.5, SILU_GAIN / 8, SILU_GAIN / 8)[layer]).then_inc(a[layer], 1)

            @block.sync
            def _(sp):
                for g in range(GROUPS):
                    sp.wait_ge(a3, 2 * (g + 1))
                    sp.dma_start(h_d[g, :, :], h[:, 2, g % 2, :]).then_inc(st[g % 2], 16)
                for x in st:
                    sp.wait_ge(x, 16 * GROUPS // 2)


def up_project(nc, c, x_t, up_d, out_d):
    with ExitStack() as ctx:
        sb = lambda name, shape, dt=F32: ctx.enter_context(nc.sbuf_tensor(f"{name}_{nc.next_id()}", shape, dt))
        up = sb("up_w", [128, 2, 128])
        y = sb("up_y", [TN, NT, D])
        ps = ctx.enter_context(nc.psum_tensor(f"up_ps_{nc.next_id()}", [128, 4, 512], F32))
        with stage(nc, "loaded", "summed", "copied", "stored") as (block, loaded, summed, copied, stored):
            @block.sync
            def _(sp):
                for n in range(2):
                    sp.dma_start(up[:, n, :], up_d[n]).then_inc(loaded, 16)
                sp.wait_ge(copied, NT)
                sp.dma_start(tiles_of(out_d), y[:, :, :]).then_inc(stored, 16)
                sp.wait_ge(stored, 16)

            @block.tensor
            def _(pe):
                pe.wait_ge(loaded, 32)
                for i in range(NT):
                    if i >= 4:
                        pe.wait_ge(copied, i - 3)
                    for k in range(4):
                        ins = pe.matmul(ps[0:TN, i % 4, 128 * k:128 * k + 128], x_t[:, k, TN * i:TN * i + TN],
                                        up[:, min(k, 1), :], start=True, stop=True)
                    ins.then_inc(summed, 1)

            @block.scalar
            def _(act):
                for i in range(NT):
                    act.wait_ge(summed, i + 1)
                    act.activation(y[:, i, :], ps[0:TN, i % 4, :], ACT.Copy, scale=128 ** -0.5).then_inc(copied, 1)


def graph_sum1(nc, c, table_d, tile_base, nodes_d, h_d, w4_d, out0_d, out1_d, x_d, out_d):
    HG = GE // 2
    with ExitStack() as ctx:
        sb = lambda name, shape, dt=F32: ctx.enter_context(nc.sbuf_tensor(f"{name}_{nc.next_id()}", shape, dt))
        acc = sb("g1_acc", [TN, NT, 2 * D])
        w4 = sb("g1_w4", [128, 2, D])
        wo = sb("g1_wo", [128, 2, 2, 128])
        with ExitStack() as inner:
            sb2 = lambda name, shape, dt=F32: inner.enter_context(nc.sbuf_tensor(f"{name}_{nc.next_id()}", shape, dt))
            edges = sb2("g1_edges", [128, GE, ROW])
            h = sb2("g1_h", [128, HG * TE])
            got = sb2("g1_got", [128, GE, D])
            hot = sb2("g1_hot", [128, GE, TN])
            both = sb2("g1_w2s0", [128, 2, 128])
            dot = sb2("g1_dot", [128, 2, 128])
            msg = sb2("g1_msg", [128, 2, 2 * D])
            pw = inner.enter_context(nc.psum_tensor(f"g1_pw_{nc.next_id()}", [128, 2, 512], F32))
            pm = inner.enter_context(nc.psum_tensor(f"g1_pm_{nc.next_id()}", [128, 4, 512], F32))
            with stage(nc, "loaded", "own") as (block, loaded, own_s):
                @block.vector
                def _(dve):
                    dve.memset(acc[:, :, :], 0.0).then_inc(own_s, 1)
                    dve.memset(w4[:, :, :], 0.0).then_inc(own_s, 1)
                    dve.wait_ge(own_s, 2)

                @block.sync
                def _(sp):
                    for n in range(2):
                        sp.dma_start(wo[:, 0, n, :], out0_d[128 * n:128 * n + 128, :]).then_inc(loaded, 16)
                        sp.dma_start(wo[:, 1, n, :], out1_d[128 * n:128 * n + 128, :]).then_inc(loaded, 16)
                    sp.wait_ge(own_s, 2)
                    sp.dma_start(w4[0:64, 0, :], w4_d).then_inc(loaded, 16)
                    sp.dma_start(w4[64:128, 1, :], w4_d).then_inc(loaded, 16)
                    sp.wait_ge(loaded, 96)
            table = table_d.rearrange("(p t) c -> p t c", p=128)
            with nc.Fori(0, GROUPS) as g:
                with stage(nc, "loaded", "h_in", "hot_ready", "weighed", "bp_ready", "dp_ready", "w_used", "msg_v",
                           "msg_a", "own", "summed", "added", *(f"got{i}" for i in range(GE))) as (
                        block, loaded, h_in, hot_ready, weighed, bp_ready, dp_ready, w_used, msg_v, msg_a, own_s,
                        summed, added, *got_s):
                    @block.sync
                    def _(sp):
                        sp.dma_start(edges[:, :, :], table[:, bass.ds(g * GE, GE), :]).then_inc(loaded, 16)
                        sp.dma_start(h[:, :], h_d[bass.ds(g, 1), :, :].rearrange("g p n -> (g p) n")).then_inc(h_in, 16)
                        sp.wait_ge(loaded, 16)
                        sp.wait_ge(h_in, 16)

                    @block.gpsimd
                    def _(pool):
                        pool.wait_ge(loaded, 16)
                        ids = edges[:, :, :].bitcast(I32)
                        for i in range(GE):
                            pool.indirect_dma_start(got[:, i, :], None, nodes_d,
                                                    bass.IndirectOffsetOnAxis(ap=ids[:, i, 0:1], axis=0)).then_inc(got_s[i], 16)
                        for i in range(GE):
                            pool.tensor_scalar(hot[:, i, :], c.iota[:, 0:TN], edges[:, i, 1:2], None,
                                               ALU.is_equal).then_inc(hot_ready, 1)

                    @block.tensor
                    def _(pe):
                        pe.wait_ge(h_in, 16)
                        for i in range(GE + 1):
                            if i < GE:
                                if i >= 2:
                                    pe.wait_ge(w_used, i - 1)
                                col = TE * (i % HG)
                                pe.matmul(pw[:, i % 2, :], h[:, col:col + TE], w4[:, i // HG, :],
                                          start=True, stop=True).then_inc(weighed, 1)
                            if i >= 1:
                                t = i - 1
                                pe.wait_ge(hot_ready, t + 1)
                                pe.wait_ge(msg_v, t + 1)
                                pe.wait_ge(msg_a, t + 1)
                                if t >= 2:
                                    pe.wait_ge(added, t - 1)
                                for n in range(2):
                                    ins = pe.matmul(pm[0:TN, 2 * (t % 2) + n, :], hot[:, t, :],
                                                    msg[:, t % 2, 512 * n:512 * n + 512], start=True, stop=True)
                                ins.then_inc(summed, 1)

                    @block.scalar
                    def _(act):
                        act.wait_ge(loaded, 16)
                        for i in range(GE):
                            act.wait_ge(got_s[i], 16)
                            if i >= 2:
                                act.wait_ge(msg_v, i - 1)
                                act.wait_ge(summed, i - 1)
                            act.activation(dot[:, i % 2, :], got[:, i, 128:256], ACT.Copy,
                                           scale=edges[:, i, 5:6]).then_inc(dp_ready, 1)
                            act.wait_ge(bp_ready, i + 1)
                            for m in range(3):
                                ins = act.activation(msg[:, i % 2, 256 + 128 * m:384 + 128 * m], both[:, i % 2, :], ACT.Copy,
                                                     scale=edges[:, i, 5 + m:6 + m])
                            ins.then_inc(msg_a, 1)

                    @block.vector
                    def _(dve):
                        own = Chain(dve, own_s)
                        dve.wait_ge(loaded, 16)
                        for i in range(GE + 1):
                            if i < GE:
                                s0 = got[:, i, 0:128]
                                y0 = edges[:, i, 4:5]
                                w = lambda n: pw[:, i % 2, 128 * n:128 * n + 128]
                                dve.wait_ge(weighed, i + 1)
                                dve.wait_ge(got_s[i], 16)
                                if i >= 2:
                                    dve.wait_ge(msg_a, i - 1)
                                    dve.wait_ge(summed, i - 1)
                                dve.tensor_tensor(both[:, i % 2, :], w(1), s0, ALU.mult).then_inc(bp_ready, 1)
                                own.mark(dve.scalar_tensor_tensor(msg[:, i % 2, 0:128], w(0), y0, s0, ALU.mult, ALU.mult))
                                dve.wait_ge(dp_ready, i + 1)
                                own.step(dve.scalar_tensor_tensor(dot[:, i % 2, :], got[:, i, 256:384], edges[:, i, 6:7],
                                                                  dot[:, i % 2, :], ALU.mult, ALU.add))
                                own.mark(dve.scalar_tensor_tensor(
                                    msg[:, i % 2, 640:1024].rearrange("p (m u) -> p m u", m=3),
                                    w(2).unsqueeze(1).to_broadcast((128, 3, 128)), y0,
                                    got[:, i, 128:512].rearrange("p (m u) -> p m u", m=3), ALU.mult, ALU.mult))
                                own.step(dve.scalar_tensor_tensor(dot[:, i % 2, :], got[:, i, 384:512], edges[:, i, 7:8],
                                                                  dot[:, i % 2, :], ALU.mult, ALU.add))
                                own.step(dve.tensor_tensor(msg[:, i % 2, 128:256], w(3), dot[:, i % 2, :], ALU.mult))
                                dve.engine_nop().then_inc(w_used, 1)
                                dve.engine_nop().then_inc(msg_v, 1)
                            if i >= 1:
                                t = i - 1
                                at = dve.value_load(tile_base[0:1, bass.ds(g * GE + t, 1)], min_val=0, max_val=NT - 1)
                                dve.wait_ge(summed, t + 1)
                                if t:
                                    dve.wait_ge(added, t)
                                dst = acc[:, bass.ds(at, 1), :].rearrange("p a b -> p (a b)")
                                dve.tensor_tensor(dst, dst, pm[0:TN, 2 * (t % 2):2 * (t % 2) + 2, :]
                                                  .rearrange("p a b -> p (a b)"), ALU.add).then_inc(added, 1)
                        dve.wait_ge(added, GE)
        acc_t = sb("g1_acct", [128, 2, 8, TN])
        x = sb("g1_x", [TN, NT, D])
        p8 = ctx.enter_context(nc.psum_tensor(f"g1_pt_{nc.next_id()}", [128, 4, 512], F32))
        po = ctx.enter_context(nc.psum_tensor(f"g1_po_{nc.next_id()}", [128, 2, 512], F32))
        gain = SILU_GAIN / 8 / 16 / 10
        with stage(nc, "loaded", "turned", "copied", "summed", "added", "stored") as (
                block, loaded, turned, copied, summed, added, stored):
            @block.sync
            def _(sp):
                sp.dma_start(x[:, :, :], tiles_of(x_d)).then_inc(loaded, 16)
                for i in range(NT):
                    sp.wait_ge(added, i + 1)
                    sp.dma_start(tiles_of(out_d)[:, i, :], x[:, i, :]).then_inc(stored, 16)
                sp.wait_ge(stored, 16 * NT)

            @block.tensor
            def _(pe):
                for i in range(NT):
                    if i >= 2:
                        pe.wait_ge(copied, i - 1)
                    for k in range(8):
                        ins = pe.transpose(p8[:, 2 * (i % 2) + k // 4, TN * (k % 4):TN * (k % 4) + TN],
                                           acc[:, i, 128 * k:128 * k + 128], c.ident[0:TN, 0:TN])
                    ins.then_inc(turned, 1)
                    pe.wait_ge(copied, i + 1)
                    if i >= 2:
                        pe.wait_ge(added, i - 1)
                    for o, (a, b) in enumerate(((0, 1), (2, 5), (3, 6), (4, 7))):
                        for n, k in enumerate((a, b)):
                            ins = pe.matmul(po[0:TN, i % 2, 128 * o:128 * o + 128], acc_t[:, i % 2, k, :],
                                            wo[:, min(o, 1), n, :], start=(n == 0), stop=(n == 1))
                    ins.then_inc(summed, 1)

            @block.scalar
            def _(act):
                for i in range(NT):
                    act.wait_ge(turned, i + 1)
                    if i >= 2:
                        act.wait_ge(summed, i - 1)
                    for k in range(8):
                        ins = act.activation(acc_t[:, i % 2, k, :], p8[:, 2 * (i % 2) + k // 4, TN * (k % 4):TN * (k % 4) + TN],
                                             ACT.Copy, scale=gain * (3 ** -0.5 if k == 1 else 1.0))
                    ins.then_inc(copied, 1)

            @block.vector
            def _(dve):
                dve.wait_ge(loaded, 16)
                for i in range(NT):
                    dve.wait_ge(summed, i + 1)
                    dve.tensor_tensor(x[:, i, 0:128], x[:, i, 0:128], po[0:TN, i % 2, 0:128], ALU.add)
                    xm = x[:, i, 128:512].rearrange("p (v m) -> p m v", m=3)
                    dve.tensor_tensor(xm, xm, po[0:TN, i % 2, 128:512].rearrange("p (m v) -> p m v", m=3),
                                      ALU.add).then_inc(added, 1)


def pick_experts(nc, c, x_d, w1_d, w2_d, b2_d, picked):
    with ExitStack() as ctx:
        sb = lambda name, shape, dt=F32: ctx.enter_context(nc.sbuf_tensor(f"{name}_{nc.next_id()}", shape, dt))
        x = sb("ro_x", [TN, NT, D])
        w1 = sb("ro_w1", [128, DC, 128])
        w2 = sb("ro_w2", [128, 8])
        b2 = sb("ro_b2", [1, 8])
        pooled = sb("ro_pool", [128, DC])
        hid = sb("ro_h", [128, 1])
        row = sb("ro_row", [1, 4, 8])
        top = sb("ro_top", [1, 2, 8])
        idx = sb("ro_idx", [1, 2, 8], U32)
        pad = sb("ro_pad", [1, 2, 8])
        ps = ctx.enter_context(nc.psum_tensor(f"ro_ps_{nc.next_id()}", [128, 3, 512], F32))
        with stage(nc, "loaded", "own", "pool_sum", "pool_ready", "h_sum", "h_ready", "l_sum", "shifted", "exps") as (
                block, loaded, own_s, pool_sum, pool_ready, h_sum, h_ready, l_sum, shifted, exps):
            @block.sync
            def _(sp):
                sp.dma_start(x[:, :, :], tiles_of(x_d)).then_inc(loaded, 16)
                sp.dma_start(w1[:, :, :], w1_d).then_inc(loaded, 16)
                sp.dma_start(w2[:, :], w2_d).then_inc(loaded, 16)
                sp.dma_start(b2[:, :], b2_d).then_inc(loaded, 16)

            @block.tensor
            def _(pe):
                pe.wait_ge(loaded, 64)
                for k in range(DC):
                    for i in range(NT):
                        ins = pe.matmul(ps[:, 0, k:k + 1], x[:, i, 128 * k:128 * k + 128], c.mean_col[0:TN, :],
                                        start=(i == 0), stop=(i == NT - 1))
                ins.then_inc(pool_sum, 1)
                pe.wait_ge(pool_ready, 1)
                for k in range(DC):
                    ins = pe.matmul(ps[:, 1, 0:1], w1[:, k, :], pooled[:, k:k + 1], start=(k == 0), stop=(k == DC - 1))
                ins.then_inc(h_sum, 1)
                pe.wait_ge(h_ready, 1)
                pe.matmul(ps[0:1, 2, 0:8], hid[:, :], w2[:, :], start=True, stop=True).then_inc(l_sum, 1)

            @block.scalar
            def _(act):
                act.wait_ge(h_sum, 1)
                act.activation(hid[:, :], ps[:, 1, 0:1], ACT.Gelu, bias=c.pcol[:, PCOL["rt_b1"]]).then_inc(h_ready, 1)
                act.wait_ge(shifted, 1)
                act.activation(row[:, 1, :], row[:, 0, :], ACT.Exp).then_inc(exps, 1)

            @block.vector
            def _(dve):
                own = Chain(dve, own_s)
                own.mark(dve.memset(pad[:, :, :], -1.0))
                dve.wait_ge(pool_sum, 1)
                dve.tensor_copy(pooled[:, :], ps[:, 0, 0:DC]).then_inc(pool_ready, 1)
                dve.wait_ge(l_sum, 1)
                dve.wait_ge(loaded, 64)
                own.step(dve.tensor_tensor(row[:, 2, :], ps[0:1, 2, 0:8], b2[:, :], ALU.add))
                own.step(dve.tensor_reduce(row[:, 3, 0:1], row[:, 2, :], AX, ALU.max))
                dve.tensor_scalar(row[:, 0, :], row[:, 2, :], row[:, 3, 0:1], None, ALU.subtract).then_inc(shifted, 1)
                dve.wait_ge(exps, 1)
                own.step(dve.tensor_reduce(row[:, 3, 1:2], row[:, 1, :], AX, ALU.add))
                own.step(dve.reciprocal(row[:, 3, 2:3], row[:, 3, 1:2]))
                for n in range(2):
                    own.mark(dve.tensor_scalar(pad[:, n, 0:4], row[:, 1, 4 * n:4 * n + 4], row[:, 3, 2:3], None, ALU.mult))
                own.join()
                for n in range(2):
                    own.mark(dve.max(top[:, n, :], pad[:, n, :]))
                own.join()
                for n in range(2):
                    own.mark(dve.max_index(idx[:, n, :], top[:, n, :], pad[:, n, :]))
                own.join()
                own.step(dve.tensor_copy(picked[:, :], idx[:, :, 0]))


def program(nc, a, out, debug=None):
    dram = lambda name, shape, dt=F32: nc.dram_tensor(name, shape, dt, kind="Internal").ap()
    rows = lambda name: dram(name, [N, D])
    kview = lambda w: w.rearrange("(k p) o -> p k o", p=128)
    c = Core()
    with ExitStack() as ctx:
        sb = lambda name, shape, dt=F32: ctx.enter_context(nc.sbuf_tensor(name, shape, dt))
        c.pcol_d = a["pcol"]
        c.pcol = sb("pcol", [128, NPCOL])
        c.ident = sb("ident", [128, 128])
        c.lower = sb("lower", [128, 128], BF16)
        c.ones = sb("ones", [128, 128], BF16)
        c.causal = sb("causal", [TN, TN])
        c.mean_col = sb("mean_col", [128, 1])
        c.iota_i = sb("iota_i", [128, 256], I32)
        c.node_i = sb("node_i", [128, NT], I32)
        c.iota = sb("iota", [128, 256])
        c.node = sb("node", [128, NT])
        base0 = sb("base0", [1, NS], I32)
        base1 = sb("base1", [1, NS], I32)
        picked = sb("picked", [1, 2], I32)
        col = lambda n: c.pcol[:, PCOL[n]]
        make_constants(nc, c)

        table0, table1 = dram("table0", [128 * NS, ROW]), dram("table1", [128 * NS, ROW])
        sort = lambda key, other, table, base: sort_edges(
            nc, c, a[key], a[other], a["edge_weight"], a["edge_attr_4"], a["edge_attr_8"], table, base)
        sort("src", "dst", table0, base0)
        sort("dst", "src", table1, base1)
        support, x1 = rows("support"), rows("x1")
        with nc.sbuf_tensor("n0_t", [128, DC, N], F32) as n_t:
            normalize(nc, c, a["x"], targets=[(n_t, None, None)])
            project_tokens(nc, c, n_t, DC, kview(a["L0_gnn_weight"]), support)
        graph_sum0(nc, c, table0, base0, support, a["x"], a["L0_gnn_bias"], x1)

        xa, x2, z2, x3 = rows("xa"), rows("x2"), rows("z2"), rows("x3")
        moe_bias, y_moe = rows("moe_bias"), dram("y_moe", [EXPERTS, CAP, D])
        with nc.sbuf_tensor("s0_t", [128, DC, N], F32) as s_t, nc.sbuf_tensor("o0_t", [128, DC, N], F32) as o_t:
            normalize(nc, c, x1, first_out=xa, double=True, targets=[(s_t, col("ln1_g"), col("ln1_b"))])
            pairs = [lambda e, j, w=a[f"L0_ffn_w{n}"]: kview(w)[:, :, bass.ds(j * 128, 128)] for n in "qkv"]
            attention(nc, c, s_t, s_t, o_t, *pairs, None, None, None)
            project_tokens(nc, c, o_t, DC, kview(a["L0_ffn_wo"]), x2, residuals=[xa])
            normalize(nc, c, x2, last_out=z2, targets=[(s_t, col("ln2_g"), col("ln2_b"))])
            with nc.sbuf_tensor("slot_tok", [CAP, EXPERTS], F32) as slot_tok, \
                    nc.sbuf_tensor("y_row", [TN, 2, NT], F32) as y_row, nc.sbuf_tensor("gate", [TN, 2, NT], F32) as gate:
                route_tokens(nc, c, s_t, kview(a["L0_ffn_wr"]), a["L0_ffn_b2"], slot_tok, y_row, gate, moe_bias)
                run_experts(nc, c, z2, slot_tok, a["L0_ffn_w1"], a["L0_ffn_w2"], y_moe)
                combine_experts(nc, c, y_moe, y_row, gate, [x2, x1, moe_bias], x3)

        nodes, x4 = rows("nodes"), rows("x4")
        h_d = dram("h_edges", [GROUPS, 128, GE // 2 * TE])
        edge_mlp(nc, c, table1, [a[f"L1_gnn_W_mlp{n}"] for n in (1, 2, 3)], h_d)
        with nc.sbuf_tensor("n1_t", [128, DC, N], F32) as n_t:
            normalize(nc, c, x3, targets=[(n_t, None, None)],
                      column=lambda k: slice(0, 128) if k == 0 else slice(128 + k - 1, 512, 3))
            up_project(nc, c, n_t, [a["L1_gnn_W_up0"], a["L1_gnn_W_up1"]], nodes)
        graph_sum1(nc, c, table1, base1, nodes, h_d, a["L1_gnn_W_mlp4"], a["L1_gnn_W_out0"], a["L1_gnn_W_out1"], x3, x4)

        xc, x5 = rows("xc"), rows("x5")
        with ExitStack() as acts:
            sa = lambda name: acts.enter_context(nc.sbuf_tensor(name, [128, DC, N], F32))
            with ExitStack() as mid:
                s_t = sa("s1_t")
                t_t, o_t = (mid.enter_context(nc.sbuf_tensor(n, [128, DC, N], F32)) for n in ("t1_t", "o1_t"))
                normalize(nc, c, x4, first_out=xc, double=True,
                          targets=[(s_t, col("ns_w"), col("ns_b")), (t_t, col("nt_w"), col("nt_b"))])
                pick_experts(nc, c, xc, kview(a["router_w1"]), a["router_w2"], a["router_b2"], picked)
                spatial, temporal = picked[0:1, 0:1], picked[0:1, 1:2]

                ek = lambda w, e: w[bass.ds(e, 1), :, :].rearrange("e (k p) o -> p (e k) o", p=128)
                wpair = lambda w, n=0: (lambda e, j: ek(w, e)[:, :, bass.ds(j * 128 + D * n, 128)])
                bcol = lambda b, n=0: (lambda e, j: b[bass.ds(e, 1), bass.ds(j * 128 + D * n, 128)].rearrange("e (p o) -> (e p) o", o=1))
                brow = lambda b, n=0: (lambda e, j: b[bass.ds(e, 1), bass.ds(j * 128 + D * n, 128)])
                all_w = lambda w: (lambda e: ek(w, e))
                all_b = lambda b: (lambda e: b[bass.ds(e, 1), :, :].rearrange("e p c -> (e p) c"))
                attention(nc, c, t_t, t_t, o_t, wpair(a["tq_w"]), wpair(a["tk_w"]), wpair(a["tv_w"]),
                          bcol(a["tq_brow"]), bcol(a["tk_brow"]), brow(a["tv_brow"]), causal=True, pick=temporal)
                project_features(nc, c, o_t, all_w(a["tp_w"]), all_b(a["tp_b"]), DC, t_t, residual_t=t_t, pick=temporal)
                sw, sbr = a["sp_in_w"], a["sp_in_brow"]
                attention(nc, c, s_t, s_t, o_t, wpair(sw, 0), wpair(sw, 1), wpair(sw, 2),
                          bcol(sbr, 0), bcol(sbr, 1), brow(sbr, 2), pick=spatial)
                project_features(nc, c, o_t, all_w(a["sp_out_w"]), all_b(a["sp_out_b"]), DC, s_t, pick=spatial)
                cw, cbr = a["cross_in_w"], a["cross_in_brow"]
                zero = lambda f: (lambda e, j: f(0, j))
                attention(nc, c, s_t, t_t, o_t, zero(wpair(cw, 0)), zero(wpair(cw, 1)), zero(wpair(cw, 2)),
                          zero(bcol(cbr, 0)), zero(bcol(cbr, 1)), zero(brow(cbr, 2)))
                project_tokens(nc, c, o_t, DC, kview(a["cross_out_w"]), x5, bias_d=a["cross_out_b"], residuals=[xc])
            with nc.sbuf_tensor("h1_t", [128, MLP // 128, N], F32) as h_t:
                normalize(nc, c, x5, targets=[(s_t, col("nm_w"), col("nm_b"))])
                project_features(nc, c, s_t, lambda e: kview(a["mlp_w1"]), lambda e: a["mlp_b1"], MLP // 128, h_t,
                                 func=ACT.Gelu)
                project_tokens(nc, c, h_t, MLP // 128, kview(a["mlp_w2"]), out, bias_d=a["mlp_b2"],
                               residuals=[x5, x4])


def kernel(**inputs):
    import concourse.bacc as bacc
    from concourse.bass_utils import run_bass_kernel_spmd as run

    g = {k: np.asarray(v) for k, v in inputs.items()}
    f = {k[7:]: v for k, v in g.items() if k.startswith("L1_ffn_")}
    cols = lambda v: v.reshape(-1, 128).T
    ecols = lambda v: v.reshape(v.shape[0], -1, 128).transpose(0, 2, 1)
    packed = {"ln1_g": cols(g["L0_ffn_ln1_g"]), "ln1_b": cols(g["L0_ffn_ln1_b"]),
              "ln2_g": cols(g["L0_ffn_ln2_g"]), "ln2_b": cols(g["L0_ffn_ln2_b"]),
              "ns_w": cols(f["norm_s_w"]), "ns_b": cols(f["norm_s_b"]),
              "nt_w": cols(f["norm_t_w"]), "nt_b": cols(f["norm_t_b"]),
              "nm_w": cols(f["norm_mlp_w"]), "nm_b": cols(f["norm_mlp_b"]),
              "co_b": cols(f["cross_out_b"]), "mlp_b1": cols(f["mlp_b1"]), "rt_b1": cols(f["router_b1"]),
              "moe_b1": g["L0_ffn_b1"].reshape(EXPERTS * 2, 128).T}
    arrays = {"pcol": np.concatenate([packed[n] for n in PCOL], axis=1)}
    for n in ("x", "src", "dst", "edge_attr_4", "edge_attr_8", "edge_weight", "L0_gnn_weight", "L0_ffn_wq", "L0_ffn_wk",
              "L0_ffn_wv", "L0_ffn_wo", "L0_ffn_wr", "L0_ffn_w1", "L0_ffn_w2", "L0_ffn_b2", "L1_gnn_W_up0",
              "L1_gnn_W_up1", "L1_gnn_W_mlp1", "L1_gnn_W_mlp2", "L1_gnn_W_mlp3", "L1_gnn_W_mlp4", "L1_gnn_W_out0",
              "L1_gnn_W_out1"):
        arrays[n] = g[n]
    arrays["L0_gnn_bias"] = g["L0_gnn_bias"].reshape(1, D)
    for n in ("sp_in", "sp_out", "tq", "tk", "tv", "tp"):
        arrays[f"{n}_w"] = f[f"{n}_w"].transpose(0, 2, 1)
    for n in ("sp_out", "tp"):
        arrays[f"{n}_b"] = ecols(f[f"{n}_b"])
    for n in ("tq", "tk", "tv", "sp_in"):
        arrays[f"{n}_brow"] = f[f"{n}_b"]
    arrays["cross_in_w"] = f["cross_in_w"].T[None]
    arrays["cross_in_brow"] = f["cross_in_b"][None]
    arrays["cross_out_w"], arrays["cross_out_b"] = f["cross_out_w"].T, f["cross_out_b"][None]
    arrays["mlp_w1"], arrays["mlp_b1"] = f["mlp_w1"].T, cols(f["mlp_b1"])
    arrays["mlp_w2"], arrays["mlp_b2"] = f["mlp_w2"].T, f["mlp_b2"][None]
    arrays["router_w1"], arrays["router_w2"], arrays["router_b2"] = f["router_w1"].T, f["router_w2"].T, f["router_b2"][None]
    arrays = {k: np.ascontiguousarray(v) for k, v in arrays.items()}

    nc = bacc.Bacc("TRN2", target_bir_lowering=False, num_devices=1)
    aps = {k: nc.dram_tensor(f"in_{k}", v.shape, mybir.dt.from_np(v.dtype), kind="ExternalInput").ap()
           for k, v in arrays.items()}
    out = nc.dram_tensor("out_0", (N, D), F32, kind="ExternalOutput").ap()
    program(nc, aps, out)
    r = run(nc, [{f"in_{k}": v for k, v in arrays.items()}], core_ids=[0])
    return r.results[0]["out_0"]
```

```python
from contextlib import ExitStack, contextmanager

import numpy as np

import concourse.bass as bass
from concourse import mybir

F32 = mybir.dt.float32
BF16 = mybir.dt.bfloat16
I32 = mybir.dt.int32
U32 = mybir.dt.uint32
ALU = mybir.AluOpType
ACT = mybir.ActivationFunctionType
AX = mybir.AxisListType.X

N = 1250
D = 512
TN = 125
NT = N // TN
DC = D // 128
E = 20000
EC = E // TN
TE = 128
GE = 14
GL = 3 * GE
GROUPS = -(-((E + NT * (TE - 1)) // TE) // GE)
assert GROUPS % 3 == 0
NS = GE * GROUPS
TURNS = NS // GL
RING = 8
ROW = 16
HEADS = 8
HD = D // HEADS
EXPERTS = 64
CAP = 2 * (N * 2 // EXPERTS)
CAPW = 96
FF = 256
MLP = 4 * D
EPS = 1e-5
SILU_GAIN = 1.679177
COLS = [slice(0, 512), slice(512, 1024), slice(1024, N)]

PCOL = {}
_at = 0
for _n, _w in (("ln1_g", 4), ("ln1_b", 4), ("ln2_g", 4), ("ln2_b", 4), ("ns_w", 4), ("ns_b", 4),
               ("nt_w", 4), ("nt_b", 4), ("nm_w", 4), ("nm_b", 4), ("co_b", 4), ("mlp_b1", 16),
               ("rt_b1", 1), ("moe_b1", EXPERTS * FF // 128)):
    PCOL[_n] = slice(_at, _at + _w)
    _at += _w
NPCOL = _at


class Core:
    pass


@contextmanager
def stage(nc, *names):
    sems = [nc.alloc_semaphore(f"{n}_{nc.next_id()}") for n in names]
    with nc.Block() as block:
        yield (block, *sems)
    nc.clear_and_free_semaphores(sems)
    nc.all_engine_barrier()


class Chain:

    def __init__(self, eng, sem):
        self.eng, self.sem, self.n = eng, sem, 0

    def mark(self, ins):
        self.n += 1
        ins.then_inc(self.sem, 1)

    def step(self, ins):
        self.mark(ins)
        self.eng.wait_ge(self.sem, self.n)

    def join(self):
        self.eng.wait_ge(self.sem, self.n)


def tiles_of(dram):
    return dram.rearrange("(i p) d -> p i d", p=TN)


def make_constants(nc, c):
    with stage(nc, "made", "loaded") as (block, made, loaded):
        @block.sync
        def _(sp):
            sp.dma_start(c.pcol[:, :], c.pcol_d).then_inc(loaded, 16)
            sp.wait_ge(loaded, 16)

        @block.gpsimd
        def _(pool):
            own = Chain(pool, made)
            pool.memset(c.ident[:, :], 0.0).then_inc(made, 1)
            pool.memset(c.lower[:, :], 1.0).then_inc(made, 1)
            pool.memset(c.ones[:, :], 1.0).then_inc(made, 1)
            pool.memset(c.causal[:, :], 0.0).then_inc(made, 1)
            pool.memset(c.mean_col[:, :], 1.0 / N).then_inc(made, 1)
            pool.iota(c.iota_i[:, :], [[1, 256]], base=0, channel_multiplier=0).then_inc(made, 1)
            pool.iota(c.node_i[:, :], [[TN, NT]], base=0, channel_multiplier=1).then_inc(made, 1)
            own.n = 7
            own.join()
            own.mark(pool.affine_select(out=c.ident[:, :], in_=c.ident[:, :], compare_op=ALU.not_equal,
                                        fill=1.0, base=0, pattern=[[-1, 128]], channel_multiplier=1))
            own.mark(pool.affine_select(out=c.lower[:, :], in_=c.lower[:, :], compare_op=ALU.is_gt,
                                        fill=0.0, base=0, pattern=[[1, 128]], channel_multiplier=-1))
            own.mark(pool.affine_select(out=c.causal[:, :], in_=c.causal[:, :], compare_op=ALU.is_ge,
                                        fill=-3.0e38, base=0, pattern=[[-1, TN]], channel_multiplier=1))
            own.mark(pool.tensor_copy(c.iota[:, :], c.iota_i[:, :]))
            own.mark(pool.tensor_copy(c.node[:, :], c.node_i[:, :]))
            own.join()


def normalize(nc, c, src, first_out=None, last_out=None, double=False, targets=(), column=None):
    column = column or (lambda k: slice(128 * k, 128 * k + 128))
    with ExitStack() as ctx:
        sb = lambda name, shape, dt=F32: ctx.enter_context(nc.sbuf_tensor(f"{name}_{nc.next_id()}", shape, dt))
        x = sb("ln_x", [TN, NT, D])
        y = sb("ln_y", [TN, NT, D])
        z = sb("ln_z", [TN, NT, D]) if double else y
        stats = sb("ln_stats", [TN, NT, 6])
        mv = sb("ln_mv", [TN, NT, 2])
        root = sb("ln_root", [TN, NT])
        ps = ctx.enter_context(nc.psum_tensor(f"ln_ps_{nc.next_id()}", [128, 4, 512], F32))
        passes = [(x, y), (y, z)] if double else [(x, y)]
        with stage(nc, "loaded", "loaded2", "own", "var", "rooted", "normed", "turned", "copied", "stored", "copied2") as (
                block, loaded, loaded2, own_s, var, rooted, normed, turned, copied, stored, copied2):
            halves = [slice(0, NT // 2), slice(NT // 2, NT)]

            @block.sync
            def _(sp):
                for s, h in zip((loaded, loaded2), halves):
                    sp.dma_start(x[:, h, :], tiles_of(src)[:, h, :]).then_inc(s, 16)
                n = 0
                if first_out is not None:
                    sp.wait_ge(normed, NT)
                    sp.dma_start(tiles_of(first_out), y[:, :, :]).then_inc(stored, 16)
                    n += 16
                if last_out is not None:
                    sp.wait_ge(normed, NT * len(passes))
                    sp.dma_start(tiles_of(last_out), z[:, :, :]).then_inc(stored, 16)
                    n += 16
                if n:
                    sp.wait_ge(stored, n)

            @block.vector
            def _(dve):
                own = Chain(dve, own_s)
                for k, (a, b) in enumerate(passes):
                    for i in range(NT):
                        if k == 0:
                            dve.wait_ge(loaded if i < NT // 2 else loaded2, 16)
                        own.mark(dve.bn_stats(stats[:, i, :], a[:, i, :]))
                    own.join()
                    for i in range(NT):
                        own.mark(dve.bn_aggr(mv[:, i, :], stats[:, i, :]))
                    own.join()
                    own.mark(dve.tensor_scalar(root[:, :], mv[:, :, 1], EPS, None, ALU.add))
                    own.join()
                    dve.engine_nop().then_inc(var, 1)
                    dve.wait_ge(rooted, k + 1)
                    own.step(dve.reciprocal(root[:, :], root[:, :]))
                    for i in range(NT):
                        dve.tensor_scalar(b[:, i, :], a[:, i, :], mv[:, i, 0:1], root[:, i:i + 1],
                                          ALU.subtract, ALU.mult).then_inc(normed, 1)
                    dve.wait_ge(normed, NT * (k + 1))
                if len(targets) > 1:
                    d, g, b = targets[1]
                    for i in range(NT):
                        dve.wait_ge(copied, i + 1)
                        for k in range(DC):
                            ins = dve.tensor_scalar(d[:, k, TN * i:TN * i + TN], ps[:, i % 4, TN * k:TN * k + TN],
                                                    g[:, k:k + 1], b[:, k:k + 1], ALU.mult, ALU.add)
                        ins.then_inc(copied2, 1)

            @block.scalar
            def _(act):
                for k in range(len(passes)):
                    act.wait_ge(var, k + 1)
                    act.activation(root[:, :], root[:, :], ACT.Sqrt).then_inc(rooted, 1)
                if targets:
                    d, g, b = targets[0]
                    for i in range(NT):
                        act.wait_ge(turned, i + 1)
                        if g is None:
                            ins = act.activation(d[:, :, TN * i:TN * i + TN],
                                                 ps[:, i % 4, 0:DC * TN].rearrange("p (k n) -> p k n", k=DC), ACT.Copy)
                        else:
                            for k in range(DC):
                                ins = act.activation(d[:, k, TN * i:TN * i + TN], ps[:, i % 4, TN * k:TN * k + TN],
                                                     ACT.Identity, bias=b[:, k:k + 1], scale=g[:, k:k + 1])
                        ins.then_inc(copied, 1)

            @block.tensor
            def _(pe):
                if targets:
                    for i in range(NT):
                        pe.wait_ge(normed, NT * (len(passes) - 1) + i + 1)
                        if i >= 4:
                            pe.wait_ge(copied, i - 3)
                            if len(targets) > 1:
                                pe.wait_ge(copied2, i - 3)
                        for k in range(DC):
                            ins = pe.transpose(ps[:, i % 4, TN * k:TN * k + TN], z[:, i, column(k)], c.ident[0:TN, 0:TN])
                        ins.then_inc(turned, 1)


def project_tokens(nc, c, src_t, nk, w_d, out_d, bias_d=None, residuals=(), width=D, scale=None):
    with ExitStack() as ctx:
        sb = lambda name, shape, dt=F32: ctx.enter_context(nc.sbuf_tensor(f"{name}_{nc.next_id()}", shape, dt))
        w = sb("pt_w", [128, nk, width])
        res = [sb("pt_res", [TN, 2, width]) for _ in residuals]
        y = sb("pt_y", [TN, 2, width])
        bias = sb("pt_bias", [TN, width]) if bias_d is not None else None
        ps = ctx.enter_context(nc.psum_tensor(f"pt_ps_{nc.next_id()}", [128, 4, 512], F32))
        with stage(nc, "weights", "res0", "res1", "summed", "added", "st0", "st1", "own") as (
                block, weights, res0, res1, summed, added, st0, st1, own_s):
            res_in = (res0, res1)
            st = (st0, st1)
            per = 16 * len(residuals)

            @block.sync
            def _(sp):
                for k in range(0, nk, 4):
                    sp.dma_start(w[:, k:k + 4, :], w_d[:, k:k + 4, :]).then_inc(weights, 16)
                if bias is not None:
                    sp.dma_start(bias[:, :], bias_d.to_broadcast((TN, width)) if bias_d.shape[0] == 1 else bias_d).then_inc(weights, 16)
                for i in range(NT + 1):
                    if i < NT and residuals:
                        if i >= 2:
                            sp.wait_ge(added, i - 1)
                        for r, d in zip(res, residuals):
                            sp.dma_start(r[:, i % 2, :], tiles_of(d)[:, i, :]).then_inc(res_in[i % 2], 16)
                    if i >= 1:
                        sp.wait_ge(added, i)
                        sp.dma_start(tiles_of(out_d)[:, i - 1, :], y[:, (i - 1) % 2, :]).then_inc(st[(i - 1) % 2], 16)
                for s in st:
                    sp.wait_ge(s, 16 * NT // 2)

            @block.tensor
            def _(pe):
                pe.wait_ge(weights, 16 * (nk // 4 + (bias is not None)))
                for i in range(NT):
                    if i >= 4:
                        pe.wait_ge(added, i - 3)
                    for k in range(nk):
                        ins = pe.matmul(ps[0:TN, i % 4, 0:width], src_t[:, k, TN * i:TN * i + TN], w[:, k, :],
                                        start=(k == 0), stop=(k == nk - 1))
                    ins.then_inc(summed, 1)

            @block.vector
            def _(dve):
                own = Chain(dve, own_s)
                dve.wait_ge(weights, 16 * (nk // 4 + (bias is not None)))
                for i in range(NT):
                    dve.wait_ge(summed, i + 1)
                    if residuals:
                        dve.wait_ge(res_in[i % 2], per * (i // 2 + 1))
                    if i >= 2:
                        dve.wait_ge(st[i % 2], 16 * (i // 2))
                    terms = ([bias[:, :]] if bias is not None else []) + [r[:, i % 2, :] for r in res]
                    cur = ps[0:TN, i % 4, 0:width]
                    out = y[:, i % 2, :]
                    if not terms:
                        ins = dve.tensor_copy(out, cur)
                    for n, t in enumerate(terms):
                        ins = dve.tensor_tensor(out, cur, t, ALU.add)
                        cur = out
                        if n < len(terms) - 1:
                            own.step(ins)
                    ins.then_inc(added, 1)


def project_features(nc, c, src_t, w_d, bias_d, nout, dst_t, residual_t=None, func=None, pick=None):
    with ExitStack() as ctx:
        sb = lambda name, shape, dt=F32: ctx.enter_context(nc.sbuf_tensor(f"{name}_{nc.next_id()}", shape, dt))
        w = sb("pf_w", [128, DC, 128 * nout])
        bias = sb("pf_bias", [128, nout])
        ps = ctx.enter_context(nc.psum_tensor(f"pf_ps_{nc.next_id()}", [128, 6, 512], F32))
        units = [(o, s) for o in range(nout) for s in COLS]
        with stage(nc, "weights", "summed", "done") as (block, weights, summed, done):
            @block.sync
            def _(sp):
                e = sp.value_load(pick, min_val=0, max_val=3) if pick is not None else None
                sp.dma_start(w[:, :, :], w_d(e)).then_inc(weights, 16)
                sp.dma_start(bias[:, :], bias_d(e)).then_inc(weights, 16)
                sp.wait_ge(weights, 32)

            @block.tensor
            def _(pe):
                pe.wait_ge(weights, 32)
                for u, (o, s) in enumerate(units):
                    if u >= 6:
                        pe.wait_ge(done, u - 5)
                    for k in range(DC):
                        ins = pe.matmul(ps[:, u % 6, 0:s.stop - s.start], w[:, k, 128 * o:128 * o + 128],
                                        src_t[:, k, s], start=(k == 0), stop=(k == DC - 1))
                    ins.then_inc(summed, 1)

            if func is None:
                @block.vector
                def _(dve):
                    dve.wait_ge(weights, 32)
                    for u, (o, s) in enumerate(units):
                        dve.wait_ge(summed, u + 1)
                        cur = ps[:, u % 6, 0:s.stop - s.start]
                        if residual_t is None:
                            ins = dve.tensor_scalar(dst_t[:, o, s], cur, bias[:, o:o + 1], None, ALU.add)
                        else:
                            ins = dve.scalar_tensor_tensor(dst_t[:, o, s], cur, bias[:, o:o + 1],
                                                           residual_t[:, o, s], ALU.add, ALU.add)
                        ins.then_inc(done, 1)
            else:
                @block.scalar
                def _(act):
                    act.wait_ge(weights, 32)
                    for u, (o, s) in enumerate(units):
                        act.wait_ge(summed, u + 1)
                        act.activation(dst_t[:, o, s], ps[:, u % 6, 0:s.stop - s.start], func,
                                       bias=bias[:, o:o + 1]).then_inc(done, 1)


def attention(nc, c, q_src, kv_src, out_t, wq_d, wk_d, wv_d, bq_d, bk_d, bv_d, causal=False, pick=None):
    biased = bq_d is not None
    F32R = mybir.dt.float32r
    with ExitStack() as ctx:
        sb = lambda name, shape, dt=F32: ctx.enter_context(nc.sbuf_tensor(f"{name}_{nc.next_id()}", shape, dt))
        wq, wk, wv = (sb(f"at_w{n}", [128, DC, 128]) for n in "qkv")
        bq, bk = sb("at_bq", [128, 1]), sb("at_bk", [128, 1])
        bv = sb("at_bv", [TN, 128])
        q_two = [sb(f"at_q{h}", [128, N], F32R) for h in range(2)]
        k_hi = [sb(f"at_kh{h}", [128, N], F32R) for h in range(2)]
        k_lo = [sb(f"at_kl{h}", [128, N], F32R) for h in range(2)]
        v = sb("at_v", [TN, NT, 128])
        p = sb("at_p", [TN, 2, N])
        p_t = sb("at_pt", [TN, 2, NT, TN])
        o = sb("at_o", [TN, NT, 128])
        neg_max = sb("at_max", [TN, 2 * NT])
        total = sb("at_sum", [TN, 2 * NT])
        inverse = sb("at_inv", [TN, 2 * NT])
        pscore = ctx.enter_context(nc.psum_tensor(f"at_ps_{nc.next_id()}", [128, 5, 512], F32))
        pturn = ctx.enter_context(nc.psum_tensor(f"at_pt_{nc.next_id()}", [128, 2, 512], F32))
        pout = ctx.enter_context(nc.psum_tensor(f"at_po_{nc.next_id()}", [128, 512], F32))
        TAIL = N - 1024
        flat = pscore[:, :, :].rearrange("p a b -> p (a b)")
        score = [flat[:, 0:N], flat[:, 5 * 512 - N:5 * 512]]
        pieces = [[(0, 512), (512, 1024), (1024, N)], [(TAIL, TAIL + 512), (TAIL + 512, N), (0, TAIL)]]
        units = [(h, i) for h in range(2) for i in range(NT)]
        NU = len(units)
        keys = [(i + 1 if causal else NT) for _, i in units]
        parts = [-(-n // 4) for n in keys]
        upto = lambda u: sum(parts[:u])
        every = [(u, n) for u in range(NU) for n in range(parts[u])]
        with_part = lambda n, u: sum(q > n for q in parts[:u])
        NW = 96 if biased else 48
        q_bank = [pscore[:, n, :] for n in range(3)]
        k_bank = [pscore[:, 3, :], pscore[:, 4, :], pscore[:, 2, :]]
        v_bank = [pturn[:, 0, :], pturn[:, 1, :], pout]

        def load_pair(sp, e, pair, sem):
            for dst, src in ((wq, wq_d), (wk, wk_d), (wv, wv_d)):
                sp.dma_start(dst[:, :, :], src(e, pair)).then_inc(sem, 16)
            if biased:
                sp.dma_start(bq[:, :], bq_d(e, pair)).then_inc(sem, 16)
                sp.dma_start(bk[:, :], bk_d(e, pair)).then_inc(sem, 16)
                sp.dma_start(bv[:, :], bv_d(e, pair).to_broadcast((TN, 128))).then_inc(sem, 16)

        def scale_q(pool, loaded, scaled):
            pool.wait_ge(loaded, NW)
            pool.tensor_scalar(wq[:, :, :], wq[:, :, :], HD ** -0.5, None, ALU.mult).then_inc(scaled, 1)
            pool.wait_ge(scaled, 1)
            if biased:
                pool.tensor_scalar(bq[:, :], bq[:, :], HD ** -0.5, None, ALU.mult).then_inc(scaled, 1)
                pool.wait_ge(scaled, 2)

        with stage(nc, "zeroed", "loaded", "scaled") as (block, zeroed, loaded, scaled):
            if not biased:
                @block.vector
                def _(dve):
                    for b in (bq, bk, bv):
                        dve.memset(b[:, :], 0.0).then_inc(zeroed, 1)
                    dve.wait_ge(zeroed, 3)

            @block.sync
            def _(sp):
                e = sp.value_load(pick, min_val=0, max_val=3) if pick is not None else None
                load_pair(sp, e, 0, loaded)

            @block.gpsimd
            def _(pool):
                scale_q(pool, loaded, scaled)

        with nc.Fori(0, HEADS // 2) as pair:
            with stage(nc, "loaded", "scaled", "q_sum", "k_sum", "v_sum", "q_hi", "q_lo", "k_high", "k_low", "v_done",
                       "scored", "masked", "max_ready", "exp_done", "turned", "part0", "part1", "part2", "pv_done",
                       "inv_done", "o_ready", "o_turned", "o_stored") as (
                    block, loaded, scaled, q_sum, k_sum, v_sum, q_hi, q_lo, k_high, k_low, v_done, scored, masked,
                    max_ready, exp_done, turned, part0, part1, part2, pv_done, inv_done, o_ready, o_turned, o_stored):
                part_done = (part0, part1, part2)

                @block.sync
                def _(sp):
                    e = sp.value_load(pick, min_val=0, max_val=3) if pick is not None else None
                    sp.wait_ge(v_sum, NT)
                    sp.wait_ge(q_hi, 6)
                    sp.wait_ge(q_lo, 6)
                    sp.wait_ge(k_high, 12)
                    sp.wait_ge(k_low, 12)
                    sp.wait_ge(v_done, 3)
                    load_pair(sp, e, (pair + 1) % (HEADS // 2), loaded)

                @block.gpsimd
                def _(pool):
                    scale_q(pool, loaded, scaled)

                @block.tensor
                def _(pe):
                    def project(w, src, dst, s, ready):
                        for k in range(DC):
                            ins = pe.matmul(dst[:, 0:s.stop - s.start], w[:, k, :], src[:, k, s],
                                            start=(k == 0), stop=(k == DC - 1))
                        ins.then_inc(ready, 1)

                    for n, s in enumerate(COLS):
                        project(wq, q_src, q_bank[n], s, q_sum)
                    for n in range(2):
                        project(wk, kv_src, k_bank[n], COLS[n], k_sum)
                    for i in range(NT):
                        for k in range(DC):
                            ins = pe.matmul(v_bank[i // 4][0:TN, 128 * (i % 4):128 * (i % 4) + 128],
                                            kv_src[:, k, TN * i:TN * i + TN], wv[:, k, :],
                                            start=(k == 0), stop=(k == DC - 1))
                        ins.then_inc(v_sum, 1)
                    pe.wait_ge(q_hi, 6)
                    pe.wait_ge(q_lo, 6)
                    project(wk, kv_src, k_bank[2], COLS[2], k_sum)
                    pe.wait_ge(k_high, 12)
                    pe.wait_ge(k_low, 12)
                    pe.wait_ge(v_done, 3)

                    def score_part(u, n):
                        h, i = units[u]
                        w = TN * keys[u] + TN * keys[u] % 2
                        there = [(a, min(b, w)) for a, b in pieces[u % 2] if a < w]
                        if n >= len(there):
                            return
                        a, b = there[n]
                        if u >= 2 and n == 0:
                            pe.wait_ge(exp_done, u - 1)
                        if u >= 1 and a == (0 if u % 2 else 1024):
                            pe.wait_ge(exp_done, u)
                        for m, k in enumerate((k_hi[h], k_lo[h])):
                            ins = pe.matmul(score[u % 2][0:TN, a:b], q_two[h][:, TN * i:TN * i + TN], k[:, a:b],
                                            start=(m == 0), stop=(m == 1))
                        if n == len(there) - 1:
                            ins.then_inc(scored, 1)

                    def turn_part(u, n):
                        if n >= parts[u]:
                            return
                        if n == 0:
                            pe.wait_ge(exp_done, u + 1)
                        g = upto(u) + n
                        if g >= 2:
                            v_, m = every[g - 2]
                            pe.wait_ge(part_done[m], with_part(m, v_ + 1))
                        for j in range(4 * n, min(4 * n + 4, keys[u])):
                            ins = pe.transpose(pturn[0:TN, g % 2, TN * (j % 4):TN * (j % 4) + TN],
                                               p[:, u % 2, TN * j:TN * j + TN], c.ident[0:TN, 0:TN])
                        ins.then_inc(turned, 1)

                    for u in range(NU + 3):
                        for n in range(3):
                            if 2 <= u < NU + 2:
                                turn_part(u - 2, n)
                            if u < NU:
                                score_part(u, n)
                        if u >= 3:
                            t = u - 3
                            h, i = units[t]
                            for n in range(parts[t]):
                                pe.wait_ge(part_done[n], with_part(n, t + 1))
                            if t >= 1:
                                pe.wait_ge(o_ready, t)
                            for j in range(keys[t]):
                                ins = pe.matmul(pout[0:TN, 0:HD], p_t[:, t % 2, j, :],
                                                v[:, j, HD * h:HD * h + HD], start=(j == 0), stop=(j == keys[t] - 1))
                            ins.then_inc(pv_done, 1)
                    pe.wait_ge(o_ready, NU)
                    for i in range(NT):
                        ins = pe.transpose(pscore[:, i // 4, TN * (i % 4):TN * (i % 4) + TN], o[:, i, :],
                                           c.ident[0:TN, 0:TN])
                        if i % 4 == 3 or i == NT - 1:
                            ins.then_inc(o_turned, 1)

                def copy_part(eng, u, n, copy):
                    if not 0 <= u < NU or n >= parts[u]:
                        return
                    if u >= 2:
                        eng.wait_ge(pv_done, u - 1)
                    eng.wait_ge(turned, upto(u) + n + 1)
                    m = min(4, keys[u] - 4 * n)
                    copy(p_t[:, u % 2, 4 * n:4 * n + m, :],
                         pturn[0:TN, (upto(u) + n) % 2, 0:TN * m].rearrange("p (a b) -> p a b", b=TN)).then_inc(part_done[n], 1)

                @block.scalar
                def _(act):
                    for n, s in enumerate(COLS):
                        act.wait_ge(q_sum, n + 1)
                        for h in range(2):
                            r = slice(64 * h, 64 * h + 64)
                            act.activation(q_two[h][r, s], q_bank[n][r, 0:s.stop - s.start], ACT.Identity,
                                           bias=bq[r, 0:1]).then_inc(q_hi, 1)
                    for n, s in enumerate(COLS):
                        act.wait_ge(k_sum, n + 1)
                        for h in range(2):
                            r = slice(64 * h, 64 * h + 64)
                            for to in (r, slice(64 - 64 * h, 128 - 64 * h)):
                                act.activation(k_hi[h][to, s], k_bank[n][r, 0:s.stop - s.start], ACT.Identity,
                                               bias=bk[r, 0:1]).then_inc(k_high, 1)
                    for u in range(NU + 2):
                        if 1 <= u <= NU:
                            t = u - 1
                            act.wait_ge(max_ready, t + 1)
                            if t >= 2:
                                act.wait_ge(turned, upto(t - 1))
                            w = TN * keys[t]
                            act.activation(p[:, t % 2, 0:w], score[t % 2][0:TN, 0:w], ACT.Exp,
                                           bias=neg_max[:, t:t + 1], accum_out=total[:, t:t + 1]).then_inc(exp_done, 1)
                        for n in (0, 2):
                            copy_part(act, u - 2, n, lambda out, in_: act.activation(out, in_, ACT.Copy))
                    for n in range(3):
                        act.wait_ge(o_turned, n + 1)
                        w = min(4 * TN, N - 4 * TN * n)
                        act.activation(out_t[:, bass.ds(pair, 1), 4 * TN * n:4 * TN * n + w]
                                       .rearrange("p a n -> p (a n)"), pscore[:, n, 0:w], ACT.Copy).then_inc(o_stored, 1)
                    act.wait_ge(o_stored, 3)

                @block.vector
                def _(dve):
                    for n, s in enumerate(COLS):
                        for h in range(2):
                            r, other = slice(64 * h, 64 * h + 64), slice(64 - 64 * h, 128 - 64 * h)
                            dve.wait_ge(q_hi, 2 * n + 2)
                            dve.scalar_tensor_tensor(q_two[h][other, s], q_bank[n][r, 0:s.stop - s.start], bq[r, 0:1],
                                                     q_two[h][r, s].bitcast(F32), ALU.add, ALU.subtract).then_inc(q_lo, 1)
                    for n, s in enumerate(COLS):
                        for h in range(2):
                            r, other = slice(64 * h, 64 * h + 64), slice(64 - 64 * h, 128 - 64 * h)
                            dve.wait_ge(k_high, 4 * n + 4)
                            for to in (r, other):
                                dve.scalar_tensor_tensor(k_lo[h][to, s], k_bank[n][r, 0:s.stop - s.start],
                                                         bk[r, 0:1], k_hi[h][r, s].bitcast(F32), ALU.add, ALU.subtract)\
                                    .then_inc(k_low, 1)
                    for n in range(3):
                        m = min(4, NT - 4 * n)
                        dve.wait_ge(v_sum, 4 * n + m)
                        src = v_bank[n][0:TN, 0:128 * m]
                        dve.tensor_tensor(v[:, 4 * n:4 * n + m, :], src.rearrange("p (a b) -> p a b", b=128),
                                          bv[:, :].unsqueeze(1).to_broadcast((TN, m, 128)), ALU.add).then_inc(v_done, 1)
                    for u in range(NU + 3):
                        copy_part(dve, u - 2, 1, dve.tensor_copy)
                        if u < NU:
                            w = TN * keys[u]
                            dve.wait_ge(scored, u + 1)
                            if causal:
                                diag = score[u % 2][0:TN, w - TN:w]
                                dve.tensor_tensor(diag, diag, c.causal[:, :], ALU.add).then_inc(masked, 1)
                                dve.wait_ge(masked, u + 1)
                            dve.tensor_reduce(neg_max[:, u:u + 1], score[u % 2][0:TN, 0:w], AX, ALU.max, negate=True)\
                                .then_inc(max_ready, 1)
                        if u >= 3:
                            t = u - 3
                            h, i = units[t]
                            dve.wait_ge(exp_done, t + 1)
                            dve.reciprocal(inverse[:, t:t + 1], total[:, t:t + 1]).then_inc(inv_done, 1)
                            dve.wait_ge(inv_done, t + 1)
                            dve.wait_ge(pv_done, t + 1)
                            dve.tensor_scalar(o[:, i, HD * h:HD * h + HD], pout[0:TN, 0:HD],
                                              inverse[:, t:t + 1], None, ALU.mult).then_inc(o_ready, 1)


def sort_edges(nc, c, key_d, other_d, w_d, a4_d, a8_d, table_d, tile_base):
    with ExitStack() as ctx:
        sb = lambda name, shape, dt=F32: ctx.enter_context(nc.sbuf_tensor(f"{name}_{nc.next_id()}", shape, dt))
        key = sb("so_key", [TN, EC], I32)
        rows = sb("so_rows", [TN, EC, ROW])
        rows_i = rows[:, :, :].bitcast(I32)
        other = sb("so_other", [TN, EC], I32)
        w = sb("so_w", [TN, EC])
        a4 = sb("so_a4", [TN, EC * 4])
        a8 = sb("so_a8", [TN, EC * 8])
        zero = sb("so_zero", [128, NS * ROW])
        keyf = sb("so_keyf", [TN, EC])
        bucket = sb("so_bucket", [TN, EC])
        oh = sb("so_oh", [TN, NT, EC], BF16)
        flat = sb("so_flat", [128, NT * EC])
        run = sb("so_run", [128, NT * EC])
        start = sb("so_start", [128, NT + 1])
        count = sb("so_count", [128, NT])
        count_i = sb("so_counti", [128, NT], I32)
        ntile = sb("so_ntile", [128, NT])
        off = sb("so_off", [128, NT])
        delta = sb("so_delta", [128, NT])
        val = sb("so_val", [TN, NT, EC])
        slot = sb("so_slot", [TN, EC])
        slot_i = sb("so_sloti", [TN, EC], I32)
        part_i = sb("so_parti", [TN, EC], I32)
        tile_i = sb("so_tilei", [TN, EC], I32)
        base = sb("so_base", [128, NS])
        ps = ctx.enter_context(nc.psum_tensor(f"so_ps_{nc.next_id()}", [128, 8, 512], F32))
        B = 3 * EC
        banks = [(n, 3 * n, min(3, NT - 3 * n)) for n in range(-(-NT // 3))]
        row3 = lambda d: d.rearrange("(p t) c -> p (t c)", p=TN)
        with stage(nc, "loaded", "own", "zeroed", "hot", "counted", "placed", "filled", "sent") as (
                block, loaded, own_s, zeroed, hot, counted, placed, filled, sent):
            @block.sync
            def _(sp):
                sp.dma_start(key[:, :], key_d.rearrange("(p t) -> p t", p=TN)).then_inc(loaded, 16)
                sp.dma_start(other[:, :], other_d.rearrange("(p t) -> p t", p=TN)).then_inc(loaded, 16)
                sp.dma_start(w[:, :], w_d.rearrange("(p t) -> p t", p=TN)).then_inc(loaded, 16)
                sp.dma_start(a4[:, :], row3(a4_d)).then_inc(loaded, 16)
                sp.dma_start(a8[:, :], row3(a8_d)).then_inc(loaded, 16)
                sp.wait_ge(zeroed, 1)
                sp.dma_start(table_d.rearrange("(p t) c -> p (t c)", p=128), zero[:, :]).then_inc(filled, 16)
                sp.wait_ge(filled, 16)

            @block.tensor
            def _(pe):
                pe.wait_ge(hot, NT)
                for n, j, m in banks:
                    pe.matmul(ps[:, n, 0:m * EC], c.ones[0:TN, :], oh[:, j:j + m, :].rearrange("p a b -> p (a b)"),
                              start=True, stop=True).then_inc(counted, 1)
                for n, j, m in banks:
                    pe.matmul(ps[0:TN, 4 + n, 0:m * EC], c.lower[0:TN, 0:TN],
                              oh[:, j:j + m, :].rearrange("p a b -> p (a b)"), start=True, stop=True).then_inc(counted, 1)

            @block.vector
            def _(dve):
                dve.memset(zero[:, :], 0.0).then_inc(zeroed, 1)
                own = Chain(dve, own_s)
                dve.wait_ge(loaded, 80)
                own.mark(dve.tensor_copy(rows_i[:, :, 0], other[:, :]))
                own.mark(dve.tensor_copy(rows[:, :, 2], w[:, :]))
                own.mark(dve.memset(rows[:, :, 3], 0.0))
                own.mark(dve.tensor_copy(rows[:, :, 4:8], a4[:, :].rearrange("p (t c) -> p t c", c=4)))
                own.mark(dve.tensor_copy(rows[:, :, 8:16], a8[:, :].rearrange("p (t c) -> p t c", c=8)))
                own.step(dve.tensor_copy(keyf[:, :], key[:, :]))
                own.step(dve.tensor_scalar(bucket[:, :], keyf[:, :], float(TN), None, ALU.is_ge))
                for j in range(2, NT):
                    own.step(dve.scalar_tensor_tensor(bucket[:, :], keyf[:, :], float(TN * j), bucket[:, :],
                                                      ALU.is_ge, ALU.add))
                own.mark(dve.scalar_tensor_tensor(rows[:, :, 1], bucket[:, :], -float(TN), keyf[:, :],
                                                  ALU.mult, ALU.add))
                for j in range(NT):
                    dve.tensor_scalar(oh[:, j, :], bucket[:, :], float(j), None, ALU.is_equal).then_inc(hot, 1)
                for n, j, m in banks:
                    dve.wait_ge(counted, n + 1)
                    own.mark(dve.tensor_copy(flat[:, j * EC:(j + m) * EC], ps[:, n, 0:m * EC]))
                own.join()
                own.step(dve.tensor_tensor_scan(run[:, :], flat[:, :], flat[:, :], 0.0, ALU.add, ALU.bypass))
                own.mark(dve.memset(start[:, 0:1], 0.0))
                own.mark(dve.tensor_copy(start[:, 1:NT + 1],
                                         run[:, :].rearrange("p (j t) -> p j t", j=NT)[:, :, EC - 1]))
                own.join()
                own.mark(dve.tensor_tensor(run[:, :], run[:, :], flat[:, :], ALU.subtract))
                own.step(dve.tensor_tensor(count[:, :], start[:, 1:NT + 1], start[:, 0:NT], ALU.subtract))
                own.step(dve.tensor_scalar(count_i[:, :], count[:, :], float(TE - 1), None, ALU.add))
                own.step(dve.tensor_scalar(count_i[:, :], count_i[:, :], TE.bit_length() - 1, None,
                                           ALU.arith_shift_right))
                own.step(dve.tensor_copy(ntile[:, :], count_i[:, :]))
                own.step(dve.tensor_tensor_scan(off[:, :], ntile[:, :], ntile[:, :], 0.0, ALU.add, ALU.bypass))
                own.step(dve.tensor_tensor(off[:, :], off[:, :], ntile[:, :], ALU.subtract))
                own.step(dve.scalar_tensor_tensor(delta[:, :], off[:, :], float(TE), start[:, 0:NT],
                                                  ALU.mult, ALU.subtract))
                own.step(dve.tensor_scalar(base[:, :], c.iota[:, 0:NS], off[:, 1:2], None, ALU.is_ge))
                for j in range(2, NT):
                    own.step(dve.scalar_tensor_tensor(base[:, :], c.iota[:, 0:NS], off[:, j:j + 1], base[:, :],
                                                      ALU.is_ge, ALU.add))
                own.mark(dve.tensor_copy(tile_base[:, :], base[0:1, :]))
                dve.wait_ge(counted, 8)
                for n, j, m in banks:
                    own.mark(dve.tensor_tensor(val[:, j:j + m, :].rearrange("p a b -> p (a b)"),
                                               run[0:TN, j * EC:(j + m) * EC], ps[0:TN, 4 + n, 0:m * EC], ALU.add))
                own.join()
                for j in range(NT):
                    own.mark(dve.scalar_tensor_tensor(val[:, j, :], val[:, j, :], delta[0:TN, j:j + 1], oh[:, j, :],
                                                      ALU.add, ALU.mult))
                own.join()
                own.step(dve.tensor_reduce(slot[:, :], val[:, :, :].rearrange("p j t -> p t j"), AX, ALU.add))
                own.step(dve.tensor_copy(slot_i[:, :], slot[:, :]))
                own.mark(dve.tensor_scalar(part_i[:, :], slot_i[:, :], TE - 1, None, ALU.bitwise_and))
                own.mark(dve.tensor_scalar(tile_i[:, :], slot_i[:, :], TE.bit_length() - 1, None, ALU.arith_shift_right))
                own.join()
                dve.scalar_tensor_tensor(slot_i[:, :], part_i[:, :], float(NS), tile_i[:, :],
                                         ALU.mult, ALU.add).then_inc(placed, 1)

            @block.gpsimd
            def _(pool):
                pool.wait_ge(placed, 1)
                pool.wait_ge(filled, 16)
                for t in range(EC):
                    pool.indirect_dma_start(table_d, bass.IndirectOffsetOnAxis(ap=slot_i[:, t:t + 1], axis=0),
                                            rows[:, t, :], None).then_inc(sent, 16)
                pool.wait_ge(sent, 16 * EC)


def graph_sum0(nc, c, table_d, tile_base, support_d, x_d, bias_d, out_d):
    with ExitStack() as ctx:
        sb = lambda name, shape, dt=F32: ctx.enter_context(nc.sbuf_tensor(f"{name}_{nc.next_id()}", shape, dt))
        acc = sb("g0_acc", [TN, NT, D])
        bias = sb("g0_bias", [TN, D])
        edges = sb("g0_edges", [128, GL, ROW])
        got = sb("g0_got", [128, RING, D])
        hot = sb("g0_hot", [128, GL, TN])
        ps = ctx.enter_context(nc.psum_tensor(f"g0_ps_{nc.next_id()}", [128, 4, 512], F32))
        with stage(nc, "loaded", "own") as (block, loaded, own_s):
            @block.sync
            def _(sp):
                sp.dma_start(acc[:, :, :], tiles_of(x_d)).then_inc(loaded, 16)
                sp.dma_start(bias[:, :], bias_d.to_broadcast((TN, D))).then_inc(loaded, 16)

            @block.vector
            def _(dve):
                dve.wait_ge(loaded, 32)
                for i in range(NT):
                    dve.tensor_tensor(acc[:, i, :], acc[:, i, :], bias[:, :], ALU.add).then_inc(own_s, 1)
                dve.wait_ge(own_s, NT)
        table = table_d.rearrange("(p t) c -> p t c", p=128)
        with nc.Fori(0, TURNS) as g:
            with stage(nc, "loaded", "hot_ready", "summed", "added", *(f"got{i}" for i in range(RING))) as (
                    block, loaded, hot_ready, summed, added, *got_s):
                @block.sync
                def _(sp):
                    sp.dma_start(edges[:, :, :], table[:, bass.ds(g * GL, GL), :]).then_inc(loaded, 16)
                    sp.wait_ge(loaded, 16)

                @block.gpsimd
                def _(pool):
                    pool.wait_ge(loaded, 16)
                    ids = edges[:, :, :].bitcast(I32)
                    for i in range(GL):
                        if i >= RING:
                            pool.wait_ge(summed, i - RING + 1)
                        pool.indirect_dma_start(got[:, i % RING, :], None, support_d,
                                                bass.IndirectOffsetOnAxis(ap=ids[:, i, 0:1], axis=0))\
                            .then_inc(got_s[i % RING], 16)

                @block.vector
                def _(dve):
                    dve.wait_ge(loaded, 16)
                    for i in range(GL + 4):
                        if i < GL:
                            dve.tensor_scalar(hot[:, i, :], c.iota[:, 0:TN], edges[:, i, 1:2], edges[:, i, 2:3],
                                              ALU.is_equal, ALU.mult).then_inc(hot_ready, 1)
                        if i >= 4:
                            t = i - 4
                            at = dve.value_load(tile_base[0:1, bass.ds(g * GL + t, 1)], min_val=0, max_val=NT - 1)
                            dve.wait_ge(summed, t + 1)
                            if t:
                                dve.wait_ge(added, t)
                            dst = acc[:, bass.ds(at, 1), :].rearrange("p a b -> p (a b)")
                            dve.tensor_tensor(dst, dst, ps[0:TN, t % 4, :], ALU.add).then_inc(added, 1)
                    dve.wait_ge(added, GL)

                @block.tensor
                def _(pe):
                    for i in range(GL):
                        pe.wait_ge(hot_ready, i + 1)
                        pe.wait_ge(got_s[i % RING], 16 * (i // RING + 1))
                        if i >= 4:
                            pe.wait_ge(added, i - 3)
                        pe.matmul(ps[0:TN, i % 4, :], hot[:, i, :], got[:, i % RING, :], start=True, stop=True)\
                            .then_inc(summed, 1)
        with stage(nc, "stored") as (block, stored):
            @block.sync
            def _(sp):
                sp.dma_start(tiles_of(out_d), acc[:, :, :]).then_inc(stored, 16)
                sp.wait_ge(stored, 16)


def route_tokens(nc, c, xn_t, wr_d, b2_d, slot_tok, y_row, gate, moe_bias_d):
    with ExitStack() as ctx:
        sb = lambda name, shape, dt=F32: ctx.enter_context(nc.sbuf_tensor(f"{name}_{nc.next_id()}", shape, dt))
        wr = sb("rt_w", [128, DC, EXPERTS])
        b2 = sb("rt_b2", [EXPERTS, D])
        logit = sb("rt_logit", [TN, NT, EXPERTS])
        probs = sb("rt_probs", [TN, NT, EXPERTS])
        small = sb("rt_small", [TN, 4, NT])
        top = sb("rt_top", [TN, NT, 8])
        idx = sb("rt_idx", [TN, NT, 8], U32)
        expert = sb("rt_expert", [TN, 2, NT])
        hot = sb("rt_hot", [TN, 2, NT, EXPERTS], BF16)
        both = sb("rt_both", [TN, NT, EXPERTS], BF16)
        before = sb("rt_before", [TN, NT, EXPERTS])
        mine = sb("rt_mine", [TN, NT, EXPERTS])
        pos = sb("rt_pos", [TN, 2, NT])
        keep = sb("rt_keep", [TN, 2, NT])
        place = sb("rt_place", [TN, 2, NT, CAP])
        named = sb("rt_named", [TN, 2, NT, EXPERTS])
        spread = sb("rt_spread", [TN, NT, EXPERTS])
        spread_t = sb("rt_spreadt", [EXPERTS, NT, TN])
        yb = sb("rt_yb", [TN, NT, D])
        ps = ctx.enter_context(nc.psum_tensor(f"rt_ps_{nc.next_id()}", [128, 8, 512], F32))
        with stage(nc, "loaded", "own", "logits", "shifted", "exps", "hot_ready", "ranked", "named_ready", "tokens",
                   "spread_ready", "turned", "copied", "biased", "kept", "stored") as (
                block, loaded, own_s, logits, shifted, exps, hot_ready, ranked, named_ready, tokens, spread_ready,
                turned, copied, biased, kept, stored):
            @block.sync
            def _(sp):
                sp.dma_start(wr[:, :, :], wr_d).then_inc(loaded, 16)
                sp.dma_start(b2[:, :], b2_d).then_inc(loaded, 16)
                sp.wait_ge(kept, NT)
                sp.dma_start(tiles_of(moe_bias_d), yb[:, :, :]).then_inc(stored, 16)
                sp.wait_ge(stored, 16)

            @block.tensor
            def _(pe):
                pe.wait_ge(loaded, 32)
                for i in range(NT):
                    for k in range(DC):
                        ins = pe.matmul(ps[0:TN, i // 8, EXPERTS * (i % 8):EXPERTS * (i % 8) + EXPERTS],
                                        xn_t[:, k, TN * i:TN * i + TN], wr[:, k, :], start=(k == 0), stop=(k == DC - 1))
                    ins.then_inc(logits, 1)
                pe.wait_ge(hot_ready, 1)
                for i in range(NT):
                    dst = ps[0:TN, 2 + i // 8, EXPERTS * (i % 8):EXPERTS * (i % 8) + EXPERTS]
                    for j in range(i):
                        pe.matmul(dst, c.ones[0:TN, 0:TN], both[:, j, :], start=(j == 0), stop=False)
                    pe.matmul(dst, c.lower[0:TN, 0:TN], both[:, i, :], start=(i == 0), stop=True).then_inc(ranked, 1)
                pe.wait_ge(named_ready, 1)
                for n in range(2 * NT):
                    ins = pe.matmul(ps[0:CAP, 4, 0:EXPERTS], place[:, n % 2, n // 2, :], named[:, n % 2, n // 2, :],
                                    start=(n == 0), stop=(n == 2 * NT - 1))
                ins.then_inc(tokens, 1)
                pe.wait_ge(spread_ready, 1)
                for i in range(NT):
                    pe.transpose(ps[0:EXPERTS, 5, 0:TN], spread[:, i, :],
                                 c.ident[0:TN, 0:TN]).then_inc(turned, 1)
                    pe.wait_ge(copied, i + 1)
                    if i >= 2:
                        pe.wait_ge(kept, i - 1)
                    pe.matmul(ps[0:TN, 6 + i % 2, :], spread_t[:, i, :], b2[:, :], start=True, stop=True).then_inc(biased, 1)

            @block.scalar
            def _(act):
                act.wait_ge(shifted, 1)
                act.activation(probs[:, :, :], logit[:, :, :], ACT.Exp).then_inc(exps, 1)
                for i in range(NT):
                    act.wait_ge(turned, i + 1)
                    act.activation(spread_t[:, i, :], ps[0:EXPERTS, 5, 0:TN], ACT.Copy)\
                        .then_inc(copied, 1)
                    act.wait_ge(biased, i + 1)
                    act.activation(yb[:, i, :], ps[0:TN, 6 + i % 2, :], ACT.Copy).then_inc(kept, 1)

            @block.vector
            def _(dve):
                own = Chain(dve, own_s)
                peak, total, inv, pair = (small[:, n, :] for n in range(4))
                bc = lambda a, n: a.unsqueeze(2).to_broadcast((TN, NT, n))
                dve.wait_ge(logits, NT)
                for i in range(0, NT, 8):
                    m = min(8, NT - i)
                    own.mark(dve.tensor_copy(logit[:, i:i + m, :], ps[0:TN, i // 8, 0:EXPERTS * m]
                                             .rearrange("p (a b) -> p a b", b=EXPERTS)))
                own.join()
                own.step(dve.tensor_reduce(peak, logit[:, :, :], AX, ALU.max))
                dve.tensor_tensor(logit[:, :, :], logit[:, :, :], bc(peak, EXPERTS), ALU.subtract).then_inc(shifted, 1)
                dve.wait_ge(exps, 1)
                own.step(dve.tensor_reduce(total, probs[:, :, :], AX, ALU.add))
                own.step(dve.reciprocal(inv, total))
                own.step(dve.tensor_tensor(probs[:, :, :], probs[:, :, :], bc(inv, EXPERTS), ALU.mult))
                for i in range(NT):
                    own.mark(dve.max(top[:, i, :], probs[:, i, :]))
                own.join()
                for i in range(NT):
                    own.mark(dve.max_index(idx[:, i, :], top[:, i, :], probs[:, i, :]))
                own.step(dve.tensor_tensor(pair, top[:, :, 0], top[:, :, 1], ALU.add))
                own.step(dve.reciprocal(pair, pair))
                for k in range(2):
                    own.mark(dve.tensor_copy(expert[:, k, :], idx[:, :, k]))
                    own.mark(dve.tensor_tensor(gate[:, k, :], top[:, :, k], pair, ALU.mult))
                own.join()
                for k in range(2):
                    for i in range(NT):
                        own.mark(dve.tensor_scalar(hot[:, k, i, :], c.iota[0:TN, 0:EXPERTS], expert[:, k, i:i + 1],
                                                   None, ALU.is_equal))
                own.join()
                dve.tensor_tensor(both[:, :, :], hot[:, 0, :, :], hot[:, 1, :, :], ALU.add).then_inc(hot_ready, 1)
                dve.wait_ge(ranked, NT)
                for i in range(0, NT, 8):
                    m = min(8, NT - i)
                    own.mark(dve.tensor_copy(before[:, i:i + m, :], ps[0:TN, 2 + i // 8, 0:EXPERTS * m]
                                             .rearrange("p (a b) -> p a b", b=EXPERTS)))
                own.join()
                for k in range(2):
                    own.step(dve.tensor_tensor(mine[:, :, :], before[:, :, :], hot[:, k, :, :], ALU.mult))
                    own.step(dve.tensor_reduce(pos[:, k, :], mine[:, :, :], AX, ALU.add))
                for k in range(2):
                    for i in range(NT):
                        own.mark(dve.tensor_scalar(place[:, k, i, :], c.iota[0:TN, 0:CAP], pos[:, k, i:i + 1], None,
                                                   ALU.is_equal))
                        own.mark(dve.tensor_scalar(named[:, k, i, :], c.iota[0:TN, 0:EXPERTS], expert[:, k, i:i + 1],
                                                   c.node[0:TN, i:i + 1], ALU.is_equal, ALU.mult))
                own.join()
                dve.engine_nop().then_inc(named_ready, 1)
                own.step(dve.tensor_scalar(keep[:, :, :], pos[:, :, :], float(CAP), None, ALU.is_lt))
                own.mark(dve.tensor_tensor(gate[:, :, :], gate[:, :, :], keep[:, :, :], ALU.mult))
                own.step(dve.tensor_scalar(pos[:, :, :], pos[:, :, :], float(CAP - 1), None, ALU.min))
                own.step(dve.scalar_tensor_tensor(y_row[:, :, :], expert[:, :, :], float(CAP), pos[:, :, :],
                                                  ALU.mult, ALU.add))
                for i in range(NT):
                    own.mark(dve.tensor_scalar(spread[:, i, :], c.iota[0:TN, 0:EXPERTS], expert[:, 0, i:i + 1],
                                               gate[:, 0, i:i + 1], ALU.is_equal, ALU.mult))
                    own.mark(dve.tensor_scalar(mine[:, i, :], c.iota[0:TN, 0:EXPERTS], expert[:, 1, i:i + 1],
                                               gate[:, 1, i:i + 1], ALU.is_equal, ALU.mult))
                own.join()
                dve.tensor_tensor(spread[:, :, :], spread[:, :, :], mine[:, :, :], ALU.add).then_inc(spread_ready, 1)
                dve.wait_ge(tokens, 1)
                own.step(dve.tensor_copy(slot_tok[:, :], ps[0:CAP, 4, 0:EXPERTS]))


def run_experts(nc, c, z_d, slot_tok, w1_d, w2_d, y_d):
    TURN, SLOTS, XS = 16, 8, 4
    MC = FF // 128
    with ExitStack() as ctx:
        sb = lambda name, shape, dt=F32: ctx.enter_context(nc.sbuf_tensor(f"{name}_{nc.next_id()}", shape, dt))
        w1 = sb("mo_w1", [128, SLOTS, DC, FF])
        w2 = sb("mo_w2", [128, SLOTS, MC, D])
        ids = sb("mo_ids", [CAP, EXPERTS], I32)
        ids_now = sb("mo_idsnow", [CAP, TURN], I32)
        b1_now = sb("mo_b1", [128, TURN * MC])
        x = sb("mo_x", [CAP, XS, D])
        x_t = sb("mo_xt", [128, 2, DC, CAPW])
        h_t = sb("mo_ht", [128, 2, MC, CAPW])
        y = sb("mo_y", [CAP, 2, D])
        pt = ctx.enter_context(nc.psum_tensor(f"mo_pt_{nc.next_id()}", [128, 2, 512], F32))
        ph = ctx.enter_context(nc.psum_tensor(f"mo_ph_{nc.next_id()}", [128, 2, 512], F32))
        py = ctx.enter_context(nc.psum_tensor(f"mo_py_{nc.next_id()}", [128, 2, 512], F32))
        w1_v = w1_d.rearrange("e (k p) f -> p e k f", p=128)
        w2_v = w2_d.rearrange("e (k p) f -> p e k f", p=128)

        def load_expert(sp, slot, e, sem):
            for dst, src in ((w1, w1_v), (w2, w2_v)):
                sp.dma_start(dst[:, slot, :, :], src[:, bass.ds(e, 1), :, :].rearrange("p e k f -> p (e k) f")).then_inc(sem, 16)

        with stage(nc, "ready", "loaded") as (block, ready, loaded):
            @block.vector
            def _(dve):
                dve.tensor_copy(ids[:, :], slot_tok[:, :]).then_inc(ready, 1)
                dve.memset(x_t[:, :, :, :], 0.0).then_inc(ready, 1)
                dve.wait_ge(ready, 2)

            @block.sync
            def _(sp):
                for e in range(SLOTS):
                    load_expert(sp, e, e, loaded)
                sp.wait_ge(loaded, 32 * SLOTS)

        def turn(g, last):
            with stage(nc, "now_ready", "turned", "xt_ready", "h_sum", "h_ready", "y_sum", "y_ready", "y0", "y1",
                       *(f"x{i}" for i in range(XS)), *(f"w{i}" for i in range(SLOTS))) as (
                    block, now_ready, turned, xt_ready, h_sum, h_ready, y_sum, y_ready, y0, y1, *more):
                stores, x_in, w_in = (y0, y1), more[:XS], more[XS:]
                loads = TURN - SLOTS if last else TURN

                @block.sync
                def _(sp):
                    for e in range(loads):
                        sp.wait_ge(y_sum, e + 1)
                        load_expert(sp, e % SLOTS, g * TURN + (e + SLOTS), w_in[e % SLOTS])
                    for s in range(SLOTS):
                        sp.wait_ge(w_in[s], 32 * (loads // SLOTS))

                @block.gpsimd
                def _(pool):
                    pool.wait_ge(now_ready, 1)
                    for e in range(TURN + XS):
                        if e < TURN:
                            if e >= XS:
                                pool.wait_ge(turned, e - XS + 1)
                            pool.indirect_dma_start(x[:, e % XS, :], None, z_d,
                                                    bass.IndirectOffsetOnAxis(ap=ids_now[:, e:e + 1], axis=0))\
                                .then_inc(x_in[e % XS], 16)
                        if e >= XS:
                            f = e - XS
                            pool.wait_ge(y_ready, f + 1)
                            pool.dma_start(y_d[bass.ds(g * TURN + f, 1), :, :].rearrange("e s d -> (e s) d"),
                                           y[:, f % 2, :]).then_inc(stores[f % 2], 16)
                    for s in stores:
                        pool.wait_ge(s, 16 * TURN // 2)

                @block.tensor
                def _(pe):
                    for e in range(TURN + 2):
                        if e < TURN:
                            pe.wait_ge(x_in[e % XS], 16 * (e // XS + 1))
                            if e >= 2:
                                pe.wait_ge(xt_ready, e - 1)
                            for k in range(DC):
                                ins = pe.transpose(pt[:, e % 2, 128 * k:128 * k + CAP], x[:, e % XS, 128 * k:128 * k + 128],
                                                   c.ident[0:CAP, 0:CAP])
                            ins.then_inc(turned, 1)
                        if 1 <= e <= TURN:
                            f = e - 1
                            if f >= SLOTS:
                                pe.wait_ge(w_in[f % SLOTS], 32 * (f // SLOTS))
                            pe.wait_ge(xt_ready, f + 1)
                            if f >= 2:
                                pe.wait_ge(h_ready, f - 1)
                            for m in range(MC):
                                for k in range(DC):
                                    ins = pe.matmul(ph[:, f % 2, 128 * m:128 * m + CAPW],
                                                    w1[:, f % SLOTS, k, 128 * m:128 * m + 128],
                                                    x_t[:, f % 2, k, :], start=(k == 0), stop=(k == DC - 1))
                            ins.then_inc(h_sum, 1)
                        if e >= 2:
                            f = e - 2
                            pe.wait_ge(h_ready, f + 1)
                            if f >= 2:
                                pe.wait_ge(y_ready, f - 1)
                            for m in range(MC):
                                ins = pe.matmul(py[0:CAP, f % 2, :], h_t[:, f % 2, m, 0:CAP],
                                                w2[:, f % SLOTS, m, :], start=(m == 0), stop=(m == MC - 1))
                            ins.then_inc(y_sum, 1)

                @block.scalar
                def _(act):
                    act.wait_ge(now_ready, 2)
                    for e in range(TURN + 1):
                        if e < TURN:
                            act.wait_ge(turned, e + 1)
                            if e >= 2:
                                act.wait_ge(h_sum, e - 1)
                            for k in range(DC):
                                ins = act.activation(x_t[:, e % 2, k, 0:CAP], pt[:, e % 2, 128 * k:128 * k + CAP], ACT.Identity,
                                                     bias=c.pcol[:, PCOL["ln2_b"]][:, k:k + 1],
                                                     scale=c.pcol[:, PCOL["ln2_g"]][:, k:k + 1])
                            ins.then_inc(xt_ready, 1)
                        if e >= 1:
                            f = e - 1
                            act.wait_ge(h_sum, f + 1)
                            if f >= 2:
                                act.wait_ge(y_sum, f - 1)
                            for m in range(MC):
                                ins = act.activation(h_t[:, f % 2, m, :], ph[:, f % 2, 128 * m:128 * m + CAPW],
                                                     ACT.Gelu_apprx_tanh, bias=b1_now[:, MC * f + m:MC * f + m + 1])
                            ins.then_inc(h_ready, 1)

                @block.vector
                def _(dve):
                    dve.tensor_copy(ids_now[:, :], ids[:, bass.ds(g * TURN, TURN)]).then_inc(now_ready, 1)
                    dve.tensor_copy(b1_now[:, :], c.pcol[:, PCOL["moe_b1"]][:, bass.ds(g * (TURN * MC), TURN * MC)])\
                        .then_inc(now_ready, 1)
                    for f in range(TURN):
                        dve.wait_ge(y_sum, f + 1)
                        if f >= 2:
                            dve.wait_ge(stores[f % 2], 16 * (f // 2))
                        dve.tensor_copy(y[:, f % 2, :], py[0:CAP, f % 2, :]).then_inc(y_ready, 1)

        with nc.Fori(0, EXPERTS // TURN - 1) as g:
            turn(g, False)
        turn(EXPERTS // TURN - 1, True)


def combine_experts(nc, c, y_d, y_row, gate, parts, out_d):
    with ExitStack() as ctx:
        sb = lambda name, shape, dt=F32: ctx.enter_context(nc.sbuf_tensor(f"{name}_{nc.next_id()}", shape, dt))
        ids = sb("cb_ids", [TN, 2, NT], I32)
        got = sb("cb_got", [TN, 2, NT, D])
        acc = sb("cb_acc", [TN, NT, D])
        part = sb("cb_part", [TN, 2, NT, D])
        rows = y_d.rearrange("e s d -> (e s) d")
        with stage(nc, "ready", "loaded", "loaded1", "got0", "got1", "own", "stored") as (
                block, ready, loaded, loaded1, got0, got1, own_s, stored):
            @block.sync
            def _(sp):
                sp.dma_start(acc[:, :, :], tiles_of(parts[0])).then_inc(loaded, 16)
                for n, d in enumerate(parts[1:]):
                    sp.dma_start(part[:, n, :, :], tiles_of(d)).then_inc(loaded, 16)
                for i in range(NT):
                    sp.wait_ge(own_s, 1 + 4 * (i + 1))
                    sp.dma_start(tiles_of(out_d)[:, i, :], acc[:, i, :]).then_inc(stored, 16)
                sp.wait_ge(stored, 16 * NT)

            @block.gpsimd
            def _(pool):
                pool.wait_ge(ready, 1)
                for i in range(NT):
                    for k in range(2):
                        pool.indirect_dma_start(got[:, k, i, :], None, rows,
                                                bass.IndirectOffsetOnAxis(ap=ids[:, k, i:i + 1], axis=0))\
                            .then_inc((got0, got1)[k], 16)

            @block.vector
            def _(dve):
                own = Chain(dve, own_s)
                dve.tensor_copy(ids[:, :, :], y_row[:, :, :]).then_inc(ready, 1)
                own.n = 1
                dve.engine_nop().then_inc(own_s, 1)
                dve.wait_ge(loaded, 16 * len(parts))
                dve.wait_ge(got0, 16 * NT)
                dve.wait_ge(got1, 16 * NT)
                for i in range(NT):
                    for n in range(2):
                        own.step(dve.tensor_tensor(acc[:, i, :], acc[:, i, :], part[:, n, i, :], ALU.add))
                    for k in range(2):
                        own.step(dve.scalar_tensor_tensor(acc[:, i, :], got[:, k, i, :], gate[:, k, i:i + 1],
                                                          acc[:, i, :], ALU.mult, ALU.add))


def edge_mlp(nc, c, table_d, w_d, h_d):
    HG = GE // 2
    W = HG * TE
    HW = W // 2
    with ExitStack() as ctx:
        sb = lambda name, shape, dt=F32: ctx.enter_context(nc.sbuf_tensor(f"{name}_{nc.next_id()}", shape, dt))
        edges = sb("em_edges", [128, NS, ROW])
        attr = sb("em_attr", [128, NS, 8])
        w1 = sb("em_w1", [GE * 8, HG, 128])
        w23 = sb("em_w23", [128, 2, 128])
        a_t = sb("em_at", [GE * 8, 2, TE])
        h = sb("em_h", [128, 3, 2, W])
        ps = ctx.enter_context(nc.psum_tensor(f"em_ps_{nc.next_id()}", [128, 8, 512], F32))
        with stage(nc, "zeroed", "loaded", "wts", "packed") as (block, zeroed, loaded, wts, packed):
            @block.vector
            def _(dve):
                dve.memset(w1[:, :, :], 0.0).then_inc(zeroed, 1)
                dve.memset(w23[:, :, :], 0.0).then_inc(zeroed, 1)
                dve.wait_ge(loaded, 16)
                dve.tensor_copy(attr[:, :, :], edges[:, :, 8:16]).then_inc(packed, 1)
                dve.wait_ge(packed, 1)

            @block.sync
            def _(sp):
                sp.dma_start(edges[:, :, :], table_d.rearrange("(p t) c -> p t c", p=128)).then_inc(loaded, 16)
                sp.wait_ge(zeroed, 2)
                for i in range(HG):
                    sp.dma_start(w1[8 * i:8 * i + 8, i, 0:64], w_d[0]).then_inc(wts, 16)
                    sp.dma_start(w1[8 * (i + HG):8 * (i + HG) + 8, i, 64:128], w_d[0]).then_inc(wts, 16)
                for n in range(2):
                    sp.dma_start(w23[0:64, n, 0:64], w_d[1 + n]).then_inc(wts, 16)
                    sp.dma_start(w23[64:128, n, 64:128], w_d[1 + n]).then_inc(wts, 16)
                sp.wait_ge(wts, 16 * (2 * HG + 4))
        with stage(nc, "turned", "copied", "s1", "s2", "s3", "a1", "a2", "a3", "st0", "st1") as (
                block, turned, copied, s1, s2, s3, a1, a2, a3, st0, st1):
            s, a, st = (s1, s2, s3), (a1, a2, a3), (st0, st1)
            @block.tensor
            def _(pe):
                for g in range(GROUPS + 3):
                    if g < GROUPS:
                        if g >= 2:
                            pe.wait_ge(copied, g - 1)
                        pe.transpose(ps[0:GE * 8, 6 + g % 2, 0:TE], attr[:, g * GE:(g + 1) * GE, :]
                                     .rearrange("p t c -> p (t c)"), c.ident[:, :]).then_inc(turned, 1)
                    for layer in range(3):
                        t = g - 1 - layer
                        if not 0 <= t < GROUPS:
                            continue
                        if layer == 0:
                            pe.wait_ge(copied, t + 1)
                        else:
                            pe.wait_ge(a[layer - 1], 2 * (t + 1))
                        if t >= 1:
                            pe.wait_ge(a[layer], 2 * t)
                        for half in range(2):
                            dst = ps[:, 2 * layer + half, :]
                            if layer == 0:
                                for i in range(HG):
                                    lo, hi = max(i * TE, half * HW), min((i + 1) * TE, (half + 1) * HW)
                                    if lo < hi:
                                        ins = pe.matmul(dst[:, lo - half * HW:hi - half * HW], w1[:, i, :],
                                                        a_t[:, t % 2, lo - i * TE:hi - i * TE], start=True, stop=True)
                            else:
                                ins = pe.matmul(dst[:, 0:HW], w23[:, layer - 1, :],
                                                h[:, layer - 1, t % 2, half * HW:(half + 1) * HW], start=True, stop=True)
                            ins.then_inc(s[layer], 1)

            @block.vector
            def _(dve):
                for g in range(GROUPS):
                    dve.wait_ge(turned, g + 1)
                    if g >= 2:
                        dve.wait_ge(s1, 2 * (g - 1))
                    dve.tensor_copy(a_t[:, g % 2, :], ps[0:GE * 8, 6 + g % 2, 0:TE]).then_inc(copied, 1)

            @block.scalar
            def _(act):
                for g in range(GROUPS + 3):
                    for layer in range(3):
                        t = g - 1 - layer
                        if not 0 <= t < GROUPS:
                            continue
                        if t >= 2:
                            if layer < 2:
                                act.wait_ge(s[layer + 1], 2 * (t - 1))
                            else:
                                act.wait_ge(st[t % 2], 16 * (t // 2))
                        for half in range(2):
                            act.wait_ge(s[layer], 2 * t + half + 1)
                            act.activation(h[:, layer, t % 2, half * HW:(half + 1) * HW],
                                           ps[:, 2 * layer + half, 0:HW], ACT.Silu,
                                           scale=(8 ** -0.5, SILU_GAIN / 8, SILU_GAIN / 8)[layer]).then_inc(a[layer], 1)

            @block.sync
            def _(sp):
                for g in range(GROUPS):
                    sp.wait_ge(a3, 2 * (g + 1))
                    sp.dma_start(h_d[g, :, :], h[:, 2, g % 2, :]).then_inc(st[g % 2], 16)
                for x in st:
                    sp.wait_ge(x, 16 * GROUPS // 2)


def up_project(nc, c, x_t, up_d, out_d):
    with ExitStack() as ctx:
        sb = lambda name, shape, dt=F32: ctx.enter_context(nc.sbuf_tensor(f"{name}_{nc.next_id()}", shape, dt))
        up = sb("up_w", [128, 2, 128])
        y = sb("up_y", [TN, NT, D])
        ps = ctx.enter_context(nc.psum_tensor(f"up_ps_{nc.next_id()}", [128, 4, 512], F32))
        with stage(nc, "loaded", "summed", "copied", "stored") as (block, loaded, summed, copied, stored):
            @block.sync
            def _(sp):
                for n in range(2):
                    sp.dma_start(up[:, n, :], up_d[n]).then_inc(loaded, 16)
                sp.wait_ge(copied, NT)
                sp.dma_start(tiles_of(out_d), y[:, :, :]).then_inc(stored, 16)
                sp.wait_ge(stored, 16)

            @block.tensor
            def _(pe):
                pe.wait_ge(loaded, 32)
                for i in range(NT):
                    if i >= 4:
                        pe.wait_ge(copied, i - 3)
                    for k in range(4):
                        ins = pe.matmul(ps[0:TN, i % 4, 128 * k:128 * k + 128], x_t[:, k, TN * i:TN * i + TN],
                                        up[:, min(k, 1), :], start=True, stop=True)
                    ins.then_inc(summed, 1)

            @block.scalar
            def _(act):
                for i in range(NT):
                    act.wait_ge(summed, i + 1)
                    act.activation(y[:, i, :], ps[0:TN, i % 4, :], ACT.Copy, scale=128 ** -0.5).then_inc(copied, 1)


def graph_sum1(nc, c, table_d, tile_base, nodes_d, h_d, w4_d, out0_d, out1_d, x_d, out_d):
    HG = GE // 2
    with ExitStack() as ctx:
        sb = lambda name, shape, dt=F32: ctx.enter_context(nc.sbuf_tensor(f"{name}_{nc.next_id()}", shape, dt))
        acc = sb("g1_acc", [TN, NT, 2 * D])
        w4 = sb("g1_w4", [128, 2, D])
        wo = sb("g1_wo", [128, 2, 2, 128])
        with ExitStack() as inner:
            sb2 = lambda name, shape, dt=F32: inner.enter_context(nc.sbuf_tensor(f"{name}_{nc.next_id()}", shape, dt))
            edges = sb2("g1_edges", [128, GL, ROW])
            h = sb2("g1_h", [128, GL // GE, HG * TE])
            got = sb2("g1_got", [128, RING, D])
            hot = sb2("g1_hot", [128, 3, 2, TN])
            w = sb2("g1_w", [128, 2, D])
            dot = sb2("g1_dot", [128, 2, 128])
            both = sb2("g1_both", [128, 3, 128])
            msg = sb2("g1_msg", [128, 3, 2 * D])
            pw = inner.enter_context(nc.psum_tensor(f"g1_pw_{nc.next_id()}", [128, 2, 512], F32))
            pm = inner.enter_context(nc.psum_tensor(f"g1_pm_{nc.next_id()}", [128, 4, 512], F32))
            with stage(nc, "loaded", "own") as (block, loaded, own_s):
                @block.vector
                def _(dve):
                    dve.memset(acc[:, :, :], 0.0).then_inc(own_s, 1)
                    dve.memset(w4[:, :, :], 0.0).then_inc(own_s, 1)
                    dve.wait_ge(own_s, 2)

                @block.sync
                def _(sp):
                    for n in range(2):
                        sp.dma_start(wo[:, 0, n, :], out0_d[128 * n:128 * n + 128, :]).then_inc(loaded, 16)
                        sp.dma_start(wo[:, 1, n, :], out1_d[128 * n:128 * n + 128, :]).then_inc(loaded, 16)
                    sp.wait_ge(own_s, 2)
                    sp.dma_start(w4[0:64, 0, :], w4_d).then_inc(loaded, 16)
                    sp.dma_start(w4[64:128, 1, :], w4_d).then_inc(loaded, 16)
                    sp.wait_ge(loaded, 96)
            table = table_d.rearrange("(p t) c -> p t c", p=128)
            with nc.Fori(0, TURNS) as g:
                with stage(nc, "loaded", "h_in", "hot_ready", "weighed", "w_copied", "bp_ready", "dp_ready", "msg_v",
                           "msg_a", "msg_p", "own", "summed", "added", *(f"got{i}" for i in range(RING))) as (
                        block, loaded, h_in, hot_ready, weighed, w_copied, bp_ready, dp_ready, msg_v, msg_a, msg_p,
                        own_s, summed, added, *got_s):
                    def got_wait(eng, i):
                        eng.wait_ge(got_s[i % RING], 16 * (i // RING + 1))

                    @block.sync
                    def _(sp):
                        sp.dma_start(edges[:, :, :], table[:, bass.ds(g * GL, GL), :]).then_inc(loaded, 16)
                        sp.dma_start(h[:, :, :], h_d[bass.ds(g * (GL // GE), GL // GE), :, :]
                                     .rearrange("g p n -> p g n")).then_inc(h_in, 16)
                        sp.wait_ge(loaded, 16)
                        sp.wait_ge(h_in, 16)

                    @block.gpsimd
                    def _(pool):
                        pool.wait_ge(loaded, 16)
                        ids = edges[:, :, :].bitcast(I32)
                        for i in range(GL + RING - 2):
                            if i < GL:
                                if i >= RING:
                                    pool.wait_ge(msg_v, i - RING + 1)
                                    pool.wait_ge(msg_p, i - RING + 1)
                                pool.indirect_dma_start(got[:, i % RING, :], None, nodes_d,
                                                        bass.IndirectOffsetOnAxis(ap=ids[:, i, 0:1], axis=0))\
                                    .then_inc(got_s[i % RING], 16)
                            if i >= RING - 2:
                                t = i - RING + 2
                                if t >= 3:
                                    pool.wait_ge(summed, t - 2)
                                pool.tensor_scalar(hot[:, t % 3, 0, :], c.iota[:, 0:TN], edges[:, t, 1:2],
                                                   edges[:, t, 4:5], ALU.is_equal, ALU.mult).then_inc(hot_ready, 1)
                                pool.tensor_scalar(hot[:, t % 3, 1, :], c.iota[:, 0:TN], edges[:, t, 1:2], None,
                                                   ALU.is_equal).then_inc(hot_ready, 1)
                                pool.wait_ge(w_copied, t + 1)
                                got_wait(pool, t)
                                pool.tensor_tensor(
                                    msg[:, t % 3, 128:512].rearrange("p (m u) -> p m u", m=3),
                                    w[:, t % 2, 256:384].unsqueeze(1).to_broadcast((128, 3, 128)),
                                    got[:, t % RING, 128:512].rearrange("p (m u) -> p m u", m=3),
                                    ALU.mult).then_inc(msg_p, 1)

                    @block.tensor
                    def _(pe):
                        pe.wait_ge(h_in, 16)
                        for i in range(GL + 2):
                            if i < GL:
                                if i >= 2:
                                    pe.wait_ge(w_copied, i - 1)
                                r = i % GE
                                col = TE * (r % HG)
                                pe.matmul(pw[:, i % 2, :], h[:, i // GE, col:col + TE], w4[:, r // HG, :],
                                          start=True, stop=True).then_inc(weighed, 1)
                            if i >= 2:
                                t = i - 2
                                pe.wait_ge(hot_ready, 2 * t + 2)
                                pe.wait_ge(msg_v, t + 1)
                                pe.wait_ge(msg_a, t + 1)
                                pe.wait_ge(msg_p, t + 1)
                                if t >= 2:
                                    pe.wait_ge(added, t - 1)
                                for n in range(2):
                                    ins = pe.matmul(pm[0:TN, 2 * (t % 2) + n, :], hot[:, t % 3, n, :],
                                                    msg[:, t % 3, 512 * n:512 * n + 512], start=True, stop=True)
                                ins.then_inc(summed, 1)

                    @block.scalar
                    def _(act):
                        act.wait_ge(loaded, 16)
                        for i in range(GL + 1):
                            if i < GL:
                                act.wait_ge(weighed, i + 1)
                                if i >= 2:
                                    act.wait_ge(msg_v, i - 1)
                                    act.wait_ge(msg_p, i - 1)
                                act.activation(w[:, i % 2, :], pw[:, i % 2, :], ACT.Copy).then_inc(w_copied, 1)
                                got_wait(act, i)
                                act.activation(dot[:, i % 2, :], got[:, i % RING, 128:256], ACT.Copy,
                                               scale=edges[:, i, 5:6]).then_inc(dp_ready, 1)
                            if i >= 1:
                                t = i - 1
                                act.wait_ge(bp_ready, t + 1)
                                if t >= 3:
                                    act.wait_ge(summed, t - 2)
                                for m in range(3):
                                    ins = act.activation(msg[:, t % 3, 640 + 128 * m:768 + 128 * m], both[:, t % 3, :],
                                                         ACT.Copy, scale=edges[:, t, 5 + m:6 + m])
                                ins.then_inc(msg_a, 1)

                    @block.vector
                    def _(dve):
                        own = Chain(dve, own_s)
                        dve.wait_ge(loaded, 16)

                        def add(t, n):
                            if n == 0:
                                dve.wait_ge(summed, t + 1)
                                if t:
                                    dve.wait_ge(added, t)
                            dst = acc[:, bass.ds(at[0], 1), 512 * n:512 * n + 512].rearrange("p a b -> p (a b)")
                            ins = dve.tensor_tensor(dst, dst, pm[0:TN, 2 * (t % 2) + n, :], ALU.add)
                            if n == 1:
                                ins.then_inc(added, 1)

                        at = [None]
                        for i in range(GL + 3):
                            t = i - 3
                            if t >= 0:
                                at[0] = dve.value_load(tile_base[0:1, bass.ds(g * GL + t, 1)], min_val=0, max_val=NT - 1)
                            if i < GL:
                                s0 = got[:, i % RING, 0:128]
                                dve.wait_ge(w_copied, i + 1)
                                got_wait(dve, i)
                                if i >= 3:
                                    dve.wait_ge(msg_a, i - 2)
                                    dve.wait_ge(summed, i - 2)
                                dve.tensor_tensor(both[:, i % 3, :], w[:, i % 2, 128:256], s0, ALU.mult).then_inc(bp_ready, 1)
                                own.mark(dve.tensor_tensor(msg[:, i % 3, 0:128], w[:, i % 2, 0:128], s0, ALU.mult))
                                dve.wait_ge(dp_ready, i + 1)
                                own.mark(dve.scalar_tensor_tensor(dot[:, i % 2, :], got[:, i % RING, 256:384],
                                                                  edges[:, i, 6:7], dot[:, i % 2, :], ALU.mult, ALU.add))
                            if t >= 0:
                                add(t, 0)
                            if i < GL:
                                own.join()
                                own.mark(dve.scalar_tensor_tensor(dot[:, i % 2, :], got[:, i % RING, 384:512],
                                                                  edges[:, i, 7:8], dot[:, i % 2, :], ALU.mult, ALU.add))
                            if t >= 0:
                                add(t, 1)
                            if i < GL:
                                own.join()
                                dve.tensor_tensor(msg[:, i % 3, 512:640], w[:, i % 2, 384:512], dot[:, i % 2, :],
                                                  ALU.mult).then_inc(msg_v, 1)
                        dve.wait_ge(added, GL)
        acc_t = sb("g1_acct", [128, 2, 8, TN])
        x = sb("g1_x", [TN, NT, D])
        p8 = ctx.enter_context(nc.psum_tensor(f"g1_pt_{nc.next_id()}", [128, 4, 512], F32))
        po = ctx.enter_context(nc.psum_tensor(f"g1_po_{nc.next_id()}", [128, 2, 512], F32))
        gain = SILU_GAIN / 8 / 16 / 10
        with stage(nc, "loaded", "turned", "copied", "summed", "added", "stored") as (
                block, loaded, turned, copied, summed, added, stored):
            @block.sync
            def _(sp):
                sp.dma_start(x[:, :, :], tiles_of(x_d)).then_inc(loaded, 16)
                for i in range(NT):
                    sp.wait_ge(added, i + 1)
                    sp.dma_start(tiles_of(out_d)[:, i, :], x[:, i, :]).then_inc(stored, 16)
                sp.wait_ge(stored, 16 * NT)

            @block.tensor
            def _(pe):
                for i in range(NT):
                    if i >= 2:
                        pe.wait_ge(copied, i - 1)
                    for k in range(8):
                        ins = pe.transpose(p8[:, 2 * (i % 2) + k // 4, TN * (k % 4):TN * (k % 4) + TN],
                                           acc[:, i, 128 * k:128 * k + 128], c.ident[0:TN, 0:TN])
                    ins.then_inc(turned, 1)
                    pe.wait_ge(copied, i + 1)
                    if i >= 2:
                        pe.wait_ge(added, i - 1)
                    for o, (a, b) in enumerate(((0, 4), (5, 1), (6, 2), (7, 3))):
                        for n, k in enumerate((a, b)):
                            ins = pe.matmul(po[0:TN, i % 2, 128 * o:128 * o + 128], acc_t[:, i % 2, k, :],
                                            wo[:, min(o, 1), n, :], start=(n == 0), stop=(n == 1))
                    ins.then_inc(summed, 1)

            @block.scalar
            def _(act):
                for i in range(NT):
                    act.wait_ge(turned, i + 1)
                    if i >= 2:
                        act.wait_ge(summed, i - 1)
                    for k in range(8):
                        ins = act.activation(acc_t[:, i % 2, k, :], p8[:, 2 * (i % 2) + k // 4, TN * (k % 4):TN * (k % 4) + TN],
                                             ACT.Copy, scale=gain * (3 ** -0.5 if k == 4 else 1.0))
                    ins.then_inc(copied, 1)

            @block.vector
            def _(dve):
                dve.wait_ge(loaded, 16)
                for i in range(NT):
                    dve.wait_ge(summed, i + 1)
                    dve.tensor_tensor(x[:, i, 0:128], x[:, i, 0:128], po[0:TN, i % 2, 0:128], ALU.add)
                    xm = x[:, i, 128:512].rearrange("p (v m) -> p m v", m=3)
                    dve.tensor_tensor(xm, xm, po[0:TN, i % 2, 128:512].rearrange("p (m v) -> p m v", m=3),
                                      ALU.add).then_inc(added, 1)


def pick_experts(nc, c, x_d, w1_d, w2_d, b2_d, picked):
    with ExitStack() as ctx:
        sb = lambda name, shape, dt=F32: ctx.enter_context(nc.sbuf_tensor(f"{name}_{nc.next_id()}", shape, dt))
        x = sb("ro_x", [TN, NT, D])
        w1 = sb("ro_w1", [128, DC, 128])
        w2 = sb("ro_w2", [128, 8])
        b2 = sb("ro_b2", [1, 8])
        pooled = sb("ro_pool", [128, DC])
        hid = sb("ro_h", [128, 1])
        row = sb("ro_row", [1, 4, 8])
        top = sb("ro_top", [1, 2, 8])
        idx = sb("ro_idx", [1, 2, 8], U32)
        pad = sb("ro_pad", [1, 2, 8])
        ps = ctx.enter_context(nc.psum_tensor(f"ro_ps_{nc.next_id()}", [128, 3, 512], F32))
        with stage(nc, "loaded", "own", "pool_sum", "pool_ready", "h_sum", "h_ready", "l_sum", "shifted", "exps") as (
                block, loaded, own_s, pool_sum, pool_ready, h_sum, h_ready, l_sum, shifted, exps):
            @block.sync
            def _(sp):
                sp.dma_start(x[:, :, :], tiles_of(x_d)).then_inc(loaded, 16)
                sp.dma_start(w1[:, :, :], w1_d).then_inc(loaded, 16)
                sp.dma_start(w2[:, :], w2_d).then_inc(loaded, 16)
                sp.dma_start(b2[:, :], b2_d).then_inc(loaded, 16)

            @block.tensor
            def _(pe):
                pe.wait_ge(loaded, 64)
                for k in range(DC):
                    for i in range(NT):
                        ins = pe.matmul(ps[:, 0, k:k + 1], x[:, i, 128 * k:128 * k + 128], c.mean_col[0:TN, :],
                                        start=(i == 0), stop=(i == NT - 1))
                ins.then_inc(pool_sum, 1)
                pe.wait_ge(pool_ready, 1)
                for k in range(DC):
                    ins = pe.matmul(ps[:, 1, 0:1], w1[:, k, :], pooled[:, k:k + 1], start=(k == 0), stop=(k == DC - 1))
                ins.then_inc(h_sum, 1)
                pe.wait_ge(h_ready, 1)
                pe.matmul(ps[0:1, 2, 0:8], hid[:, :], w2[:, :], start=True, stop=True).then_inc(l_sum, 1)

            @block.scalar
            def _(act):
                act.wait_ge(h_sum, 1)
                act.activation(hid[:, :], ps[:, 1, 0:1], ACT.Gelu, bias=c.pcol[:, PCOL["rt_b1"]]).then_inc(h_ready, 1)
                act.wait_ge(shifted, 1)
                act.activation(row[:, 1, :], row[:, 0, :], ACT.Exp).then_inc(exps, 1)

            @block.vector
            def _(dve):
                own = Chain(dve, own_s)
                own.mark(dve.memset(pad[:, :, :], -1.0))
                dve.wait_ge(pool_sum, 1)
                dve.tensor_copy(pooled[:, :], ps[:, 0, 0:DC]).then_inc(pool_ready, 1)
                dve.wait_ge(l_sum, 1)
                dve.wait_ge(loaded, 64)
                own.step(dve.tensor_tensor(row[:, 2, :], ps[0:1, 2, 0:8], b2[:, :], ALU.add))
                own.step(dve.tensor_reduce(row[:, 3, 0:1], row[:, 2, :], AX, ALU.max))
                dve.tensor_scalar(row[:, 0, :], row[:, 2, :], row[:, 3, 0:1], None, ALU.subtract).then_inc(shifted, 1)
                dve.wait_ge(exps, 1)
                own.step(dve.tensor_reduce(row[:, 3, 1:2], row[:, 1, :], AX, ALU.add))
                own.step(dve.reciprocal(row[:, 3, 2:3], row[:, 3, 1:2]))
                for n in range(2):
                    own.mark(dve.tensor_scalar(pad[:, n, 0:4], row[:, 1, 4 * n:4 * n + 4], row[:, 3, 2:3], None, ALU.mult))
                own.join()
                for n in range(2):
                    own.mark(dve.max(top[:, n, :], pad[:, n, :]))
                own.join()
                for n in range(2):
                    own.mark(dve.max_index(idx[:, n, :], top[:, n, :], pad[:, n, :]))
                own.join()
                own.step(dve.tensor_copy(picked[:, :], idx[:, :, 0]))


def program(nc, a, out, debug=None):
    dram = lambda name, shape, dt=F32: nc.dram_tensor(name, shape, dt, kind="Internal").ap()
    rows = lambda name: dram(name, [N, D])
    kview = lambda w: w.rearrange("(k p) o -> p k o", p=128)
    c = Core()
    with ExitStack() as ctx:
        sb = lambda name, shape, dt=F32: ctx.enter_context(nc.sbuf_tensor(name, shape, dt))
        c.pcol_d = a["pcol"]
        c.pcol = sb("pcol", [128, NPCOL])
        c.ident = sb("ident", [128, 128])
        c.lower = sb("lower", [128, 128], BF16)
        c.ones = sb("ones", [128, 128], BF16)
        c.causal = sb("causal", [TN, TN])
        c.mean_col = sb("mean_col", [128, 1])
        c.iota_i = sb("iota_i", [128, 256], I32)
        c.node_i = sb("node_i", [128, NT], I32)
        c.iota = sb("iota", [128, 256])
        c.node = sb("node", [128, NT])
        base0 = sb("base0", [1, NS], I32)
        base1 = sb("base1", [1, NS], I32)
        picked = sb("picked", [1, 2], I32)
        col = lambda n: c.pcol[:, PCOL[n]]
        make_constants(nc, c)

        table0, table1 = dram("table0", [128 * NS, ROW]), dram("table1", [128 * NS, ROW])
        sort = lambda key, other, table, base: sort_edges(
            nc, c, a[key], a[other], a["edge_weight"], a["edge_attr_4"], a["edge_attr_8"], table, base)
        sort("src", "dst", table0, base0)
        sort("dst", "src", table1, base1)
        support, x1 = rows("support"), rows("x1")
        with nc.sbuf_tensor("n0_t", [128, DC, N], F32) as n_t:
            normalize(nc, c, a["x"], targets=[(n_t, None, None)])
            project_tokens(nc, c, n_t, DC, kview(a["L0_gnn_weight"]), support)
        graph_sum0(nc, c, table0, base0, support, a["x"], a["L0_gnn_bias"], x1)

        xa, x2, z2, x3 = rows("xa"), rows("x2"), rows("z2"), rows("x3")
        moe_bias, y_moe = rows("moe_bias"), dram("y_moe", [EXPERTS, CAP, D])
        with nc.sbuf_tensor("s0_t", [128, DC, N], F32) as s_t, nc.sbuf_tensor("o0_t", [128, DC, N], F32) as o_t:
            normalize(nc, c, x1, first_out=xa, double=True, targets=[(s_t, col("ln1_g"), col("ln1_b"))])
            pairs = [lambda e, j, w=a[f"L0_ffn_w{n}"]: kview(w)[:, :, bass.ds(j * 128, 128)] for n in "qkv"]
            attention(nc, c, s_t, s_t, o_t, *pairs, None, None, None)
            project_tokens(nc, c, o_t, DC, kview(a["L0_ffn_wo"]), x2, residuals=[xa])
            normalize(nc, c, x2, last_out=z2, targets=[(s_t, col("ln2_g"), col("ln2_b"))])
            with nc.sbuf_tensor("slot_tok", [CAP, EXPERTS], F32) as slot_tok, \
                    nc.sbuf_tensor("y_row", [TN, 2, NT], F32) as y_row, nc.sbuf_tensor("gate", [TN, 2, NT], F32) as gate:
                route_tokens(nc, c, s_t, kview(a["L0_ffn_wr"]), a["L0_ffn_b2"], slot_tok, y_row, gate, moe_bias)
                run_experts(nc, c, z2, slot_tok, a["L0_ffn_w1"], a["L0_ffn_w2"], y_moe)
                combine_experts(nc, c, y_moe, y_row, gate, [x2, x1, moe_bias], x3)

        nodes, x4 = rows("nodes"), rows("x4")
        h_d = dram("h_edges", [GROUPS, 128, GE // 2 * TE])
        edge_mlp(nc, c, table1, [a[f"L1_gnn_W_mlp{n}"] for n in (1, 2, 3)], h_d)
        with nc.sbuf_tensor("n1_t", [128, DC, N], F32) as n_t:
            normalize(nc, c, x3, targets=[(n_t, None, None)],
                      column=lambda k: slice(0, 128) if k == 0 else slice(128 + k - 1, 512, 3))
            up_project(nc, c, n_t, [a["L1_gnn_W_up0"], a["L1_gnn_W_up1"]], nodes)
        graph_sum1(nc, c, table1, base1, nodes, h_d, a["L1_gnn_W_mlp4"], a["L1_gnn_W_out0"], a["L1_gnn_W_out1"], x3, x4)

        xc, x5 = rows("xc"), rows("x5")
        with ExitStack() as acts:
            sa = lambda name: acts.enter_context(nc.sbuf_tensor(name, [128, DC, N], F32))
            with ExitStack() as mid:
                s_t = sa("s1_t")
                t_t, o_t = (mid.enter_context(nc.sbuf_tensor(n, [128, DC, N], F32)) for n in ("t1_t", "o1_t"))
                normalize(nc, c, x4, first_out=xc, double=True,
                          targets=[(s_t, col("ns_w"), col("ns_b")), (t_t, col("nt_w"), col("nt_b"))])
                pick_experts(nc, c, xc, kview(a["router_w1"]), a["router_w2"], a["router_b2"], picked)
                spatial, temporal = picked[0:1, 0:1], picked[0:1, 1:2]

                ek = lambda w, e: w[bass.ds(e, 1), :, :].rearrange("e (k p) o -> p (e k) o", p=128)
                wpair = lambda w, n=0: (lambda e, j: ek(w, e)[:, :, bass.ds(j * 128 + D * n, 128)])
                bcol = lambda b, n=0: (lambda e, j: b[bass.ds(e, 1), bass.ds(j * 128 + D * n, 128)].rearrange("e (p o) -> (e p) o", o=1))
                brow = lambda b, n=0: (lambda e, j: b[bass.ds(e, 1), bass.ds(j * 128 + D * n, 128)])
                all_w = lambda w: (lambda e: ek(w, e))
                all_b = lambda b: (lambda e: b[bass.ds(e, 1), :, :].rearrange("e p c -> (e p) c"))
                attention(nc, c, t_t, t_t, o_t, wpair(a["tq_w"]), wpair(a["tk_w"]), wpair(a["tv_w"]),
                          bcol(a["tq_brow"]), bcol(a["tk_brow"]), brow(a["tv_brow"]), causal=True, pick=temporal)
                project_features(nc, c, o_t, all_w(a["tp_w"]), all_b(a["tp_b"]), DC, t_t, residual_t=t_t, pick=temporal)
                sw, sbr = a["sp_in_w"], a["sp_in_brow"]
                attention(nc, c, s_t, s_t, o_t, wpair(sw, 0), wpair(sw, 1), wpair(sw, 2),
                          bcol(sbr, 0), bcol(sbr, 1), brow(sbr, 2), pick=spatial)
                project_features(nc, c, o_t, all_w(a["sp_out_w"]), all_b(a["sp_out_b"]), DC, s_t, pick=spatial)
                cw, cbr = a["cross_in_w"], a["cross_in_brow"]
                zero = lambda f: (lambda e, j: f(0, j))
                attention(nc, c, s_t, t_t, o_t, zero(wpair(cw, 0)), zero(wpair(cw, 1)), zero(wpair(cw, 2)),
                          zero(bcol(cbr, 0)), zero(bcol(cbr, 1)), zero(brow(cbr, 2)))
                project_tokens(nc, c, o_t, DC, kview(a["cross_out_w"]), x5, bias_d=a["cross_out_b"], residuals=[xc])
            with nc.sbuf_tensor("h1_t", [128, MLP // 128, N], F32) as h_t:
                normalize(nc, c, x5, targets=[(s_t, col("nm_w"), col("nm_b"))])
                project_features(nc, c, s_t, lambda e: kview(a["mlp_w1"]), lambda e: a["mlp_b1"], MLP // 128, h_t,
                                 func=ACT.Gelu)
                project_tokens(nc, c, h_t, MLP // 128, kview(a["mlp_w2"]), out, bias_d=a["mlp_b2"],
                               residuals=[x5, x4])


def kernel(**inputs):
    import concourse.bacc as bacc
    from concourse.bass_utils import run_bass_kernel_spmd as run

    g = {k: np.asarray(v) for k, v in inputs.items()}
    f = {k[7:]: v for k, v in g.items() if k.startswith("L1_ffn_")}
    cols = lambda v: v.reshape(-1, 128).T
    ecols = lambda v: v.reshape(v.shape[0], -1, 128).transpose(0, 2, 1)
    packed = {"ln1_g": cols(g["L0_ffn_ln1_g"]), "ln1_b": cols(g["L0_ffn_ln1_b"]),
              "ln2_g": cols(g["L0_ffn_ln2_g"]), "ln2_b": cols(g["L0_ffn_ln2_b"]),
              "ns_w": cols(f["norm_s_w"]), "ns_b": cols(f["norm_s_b"]),
              "nt_w": cols(f["norm_t_w"]), "nt_b": cols(f["norm_t_b"]),
              "nm_w": cols(f["norm_mlp_w"]), "nm_b": cols(f["norm_mlp_b"]),
              "co_b": cols(f["cross_out_b"]), "mlp_b1": cols(f["mlp_b1"]), "rt_b1": cols(f["router_b1"]),
              "moe_b1": g["L0_ffn_b1"].reshape(EXPERTS * 2, 128).T}
    arrays = {"pcol": np.concatenate([packed[n] for n in PCOL], axis=1)}
    for n in ("x", "src", "dst", "edge_attr_4", "edge_attr_8", "edge_weight", "L0_gnn_weight", "L0_ffn_wq", "L0_ffn_wk",
              "L0_ffn_wv", "L0_ffn_wo", "L0_ffn_wr", "L0_ffn_w1", "L0_ffn_w2", "L0_ffn_b2", "L1_gnn_W_up0",
              "L1_gnn_W_up1", "L1_gnn_W_mlp1", "L1_gnn_W_mlp2", "L1_gnn_W_mlp3", "L1_gnn_W_mlp4", "L1_gnn_W_out0",
              "L1_gnn_W_out1"):
        arrays[n] = g[n]
    arrays["L0_gnn_bias"] = g["L0_gnn_bias"].reshape(1, D)
    for n in ("sp_in", "sp_out", "tq", "tk", "tv", "tp"):
        arrays[f"{n}_w"] = f[f"{n}_w"].transpose(0, 2, 1)
    for n in ("sp_out", "tp"):
        arrays[f"{n}_b"] = ecols(f[f"{n}_b"])
    for n in ("tq", "tk", "tv", "sp_in"):
        arrays[f"{n}_brow"] = f[f"{n}_b"]
    arrays["cross_in_w"] = f["cross_in_w"].T[None]
    arrays["cross_in_brow"] = f["cross_in_b"][None]
    arrays["cross_out_w"], arrays["cross_out_b"] = f["cross_out_w"].T, f["cross_out_b"][None]
    arrays["mlp_w1"], arrays["mlp_b1"] = f["mlp_w1"].T, cols(f["mlp_b1"])
    arrays["mlp_w2"], arrays["mlp_b2"] = f["mlp_w2"].T, f["mlp_b2"][None]
    arrays["router_w1"], arrays["router_w2"], arrays["router_b2"] = f["router_w1"].T, f["router_w2"].T, f["router_b2"][None]
    arrays = {k: np.ascontiguousarray(v) for k, v in arrays.items()}

    nc = bacc.Bacc("TRN2", target_bir_lowering=False, num_devices=1)
    aps = {k: nc.dram_tensor(f"in_{k}", v.shape, mybir.dt.from_np(v.dtype), kind="ExternalInput").ap()
           for k, v in arrays.items()}
    out = nc.dram_tensor("out_0", (N, D), F32, kind="ExternalOutput").ap()
    program(nc, aps, out)
    r = run(nc, [{f"in_{k}": v for k, v in arrays.items()}], core_ids=[0])
    return r.results[0]["out_0"]
```

```python
from contextlib import ExitStack, contextmanager

import numpy as np

import concourse.bass as bass
from concourse import mybir

F32 = mybir.dt.float32
BF16 = mybir.dt.bfloat16
I32 = mybir.dt.int32
U32 = mybir.dt.uint32
ALU = mybir.AluOpType
ACT = mybir.ActivationFunctionType
AX = mybir.AxisListType.X

N = 1250
D = 512
TN = 125
NT = N // TN
DC = D // 128
E = 20000
EC = E // TN
TE = 128
GE = 14
GL = 6 * GE
GROUPS = -(-((E + NT * (TE - 1)) // TE) // GE)
assert GROUPS % 6 == 0
NS = GE * GROUPS
TURNS = NS // GL
RING = 8
ROW = 16
HEADS = 8
HD = D // HEADS
EXPERTS = 64
CAP = 2 * (N * 2 // EXPERTS)
CAPW = 96
FF = 256
MLP = 4 * D
EPS = 1e-5
SILU_GAIN = 1.679177
COLS = [slice(0, 512), slice(512, 1024), slice(1024, N)]

PCOL = {}
_at = 0
for _n, _w in (("ln1_g", 4), ("ln1_b", 4), ("ln2_g", 4), ("ln2_b", 4), ("ns_w", 4), ("ns_b", 4),
               ("nt_w", 4), ("nt_b", 4), ("nm_w", 4), ("nm_b", 4), ("mlp_b1", 16),
               ("rt_b1", 1), ("moe_b1", EXPERTS * FF // 128)):
    PCOL[_n] = slice(_at, _at + _w)
    _at += _w
NPCOL = _at


class Core:
    pass


@contextmanager
def stage(nc, *names):
    sems = [nc.alloc_semaphore(f"{n}_{nc.next_id()}") for n in names]
    with nc.Block() as block:
        yield (block, *sems)
    nc.clear_and_free_semaphores(sems)
    nc.all_engine_barrier()


class Chain:

    def __init__(self, eng, sem):
        self.eng, self.sem, self.n = eng, sem, 0

    def mark(self, ins):
        self.n += 1
        ins.then_inc(self.sem, 1)

    def step(self, ins):
        self.mark(ins)
        self.eng.wait_ge(self.sem, self.n)

    def join(self):
        self.eng.wait_ge(self.sem, self.n)


def tiles_of(dram):
    return dram.rearrange("(i p) d -> p i d", p=TN)


def make_constants(nc, c):
    with stage(nc, "made", "loaded") as (block, made, loaded):
        @block.sync
        def _(sp):
            sp.dma_start(c.pcol[:, :], c.pcol_d).then_inc(loaded, 16)
            sp.wait_ge(loaded, 16)

        @block.gpsimd
        def _(pool):
            own = Chain(pool, made)
            pool.memset(c.ident[:, :], 0.0).then_inc(made, 1)
            pool.memset(c.lower[:, :], 1.0).then_inc(made, 1)
            pool.memset(c.ones[:, :], 1.0).then_inc(made, 1)
            pool.memset(c.causal[:, :], 0.0).then_inc(made, 1)
            pool.memset(c.mean_col[:, :], 1.0 / N).then_inc(made, 1)
            pool.iota(c.iota_i[:, :], [[1, 256]], base=0, channel_multiplier=0).then_inc(made, 1)
            pool.iota(c.node_i[:, :], [[TN, NT]], base=0, channel_multiplier=1).then_inc(made, 1)
            own.n = 7
            own.join()
            own.mark(pool.affine_select(out=c.ident[:, :], in_=c.ident[:, :], compare_op=ALU.not_equal,
                                        fill=1.0, base=0, pattern=[[-1, 128]], channel_multiplier=1))
            own.mark(pool.affine_select(out=c.lower[:, :], in_=c.lower[:, :], compare_op=ALU.is_gt,
                                        fill=0.0, base=0, pattern=[[1, 128]], channel_multiplier=-1))
            own.mark(pool.affine_select(out=c.causal[:, :], in_=c.causal[:, :], compare_op=ALU.is_ge,
                                        fill=-3.0e38, base=0, pattern=[[-1, 2 * TN]], channel_multiplier=1))
            own.mark(pool.tensor_copy(c.iota[:, :], c.iota_i[:, :]))
            own.mark(pool.tensor_copy(c.node[:, :], c.node_i[:, :]))
            own.join()


def normalize(nc, c, src, x=None, first_out=None, last_out=None, double=False, targets=(), column=None,
              send=None, columns=()):
    column = column or (lambda k: slice(128 * k, 128 * k + 128))
    with ExitStack() as ctx:
        sb = lambda name, shape, dt=F32: ctx.enter_context(nc.sbuf_tensor(f"{name}_{nc.next_id()}", shape, dt))
        ready = x is not None
        x = x if ready else sb("ln_x", [TN, NT, D])
        y = sb("ln_y", [TN, NT, D])
        z = sb("ln_z", [TN, NT, D]) if double else y
        stats = sb("ln_stats", [TN, NT, 6])
        mv = sb("ln_mv", [TN, NT, 2])
        root = sb("ln_root", [TN, NT])
        ps = ctx.enter_context(nc.psum_tensor(f"ln_ps_{nc.next_id()}", [128, 4, 512], F32))
        passes = [(x, y), (y, z)] if double else [(x, y)]
        with stage(nc, "loaded", "loaded2", "own", "var", "rooted", "normed", "turned", "copied", "stored", "copied2",
                   "sent") as (
                block, loaded, loaded2, own_s, var, rooted, normed, turned, copied, stored, copied2, sent):
            if send is not None:
                @block.gpsimd
                def _(pool):
                    send_edges(pool, send, columns, sent)

            halves = [slice(0, NT // 2), slice(NT // 2, NT)]

            @block.sync
            def _(sp):
                n = 0
                if not ready:
                    for s, h in zip((loaded, loaded2), halves):
                        sp.dma_start(x[:, h, :], tiles_of(src)[:, h, :]).then_inc(s, 16)
                elif src is not None:
                    sp.dma_start(tiles_of(src), x[:, :, :]).then_inc(stored, 16)
                    n += 16
                if first_out is not None:
                    sp.wait_ge(normed, NT)
                    sp.dma_start(tiles_of(first_out), y[:, :, :]).then_inc(stored, 16)
                    n += 16
                if last_out is not None:
                    sp.wait_ge(normed, NT * len(passes))
                    sp.dma_start(tiles_of(last_out), z[:, :, :]).then_inc(stored, 16)
                    n += 16
                if n:
                    sp.wait_ge(stored, n)

            @block.vector
            def _(dve):
                own = Chain(dve, own_s)
                for k, (a, b) in enumerate(passes):
                    for i in range(NT):
                        if k == 0 and not ready:
                            dve.wait_ge(loaded if i < NT // 2 else loaded2, 16)
                        own.mark(dve.bn_stats(stats[:, i, :], a[:, i, :]))
                    own.join()
                    for i in range(NT):
                        own.mark(dve.bn_aggr(mv[:, i, :], stats[:, i, :]))
                    own.join()
                    own.mark(dve.tensor_scalar(root[:, :], mv[:, :, 1], EPS, None, ALU.add))
                    own.join()
                    dve.engine_nop().then_inc(var, 1)
                    dve.wait_ge(rooted, k + 1)
                    own.step(dve.reciprocal(root[:, :], root[:, :]))
                    for i in range(NT):
                        dve.tensor_scalar(b[:, i, :], a[:, i, :], mv[:, i, 0:1], root[:, i:i + 1],
                                          ALU.subtract, ALU.mult).then_inc(normed, 1)
                    dve.wait_ge(normed, NT * (k + 1))
                if len(targets) > 1:
                    d, g, b = targets[1]
                    for i in range(NT):
                        dve.wait_ge(copied, i + 1)
                        for k in range(DC):
                            ins = dve.tensor_scalar(d[:, k, TN * i:TN * i + TN], ps[:, i % 4, TN * k:TN * k + TN],
                                                    g[:, k:k + 1], b[:, k:k + 1], ALU.mult, ALU.add)
                        ins.then_inc(copied2, 1)

            @block.scalar
            def _(act):
                for k in range(len(passes)):
                    act.wait_ge(var, k + 1)
                    act.activation(root[:, :], root[:, :], ACT.Sqrt).then_inc(rooted, 1)
                if targets:
                    d, g, b = targets[0]
                    for i in range(NT):
                        act.wait_ge(turned, i + 1)
                        if g is None:
                            ins = act.activation(d[:, :, TN * i:TN * i + TN],
                                                 ps[:, i % 4, 0:DC * TN].rearrange("p (k n) -> p k n", k=DC), ACT.Copy)
                        else:
                            for k in range(DC):
                                ins = act.activation(d[:, k, TN * i:TN * i + TN], ps[:, i % 4, TN * k:TN * k + TN],
                                                     ACT.Identity, bias=b[:, k:k + 1], scale=g[:, k:k + 1])
                        ins.then_inc(copied, 1)

            @block.tensor
            def _(pe):
                if targets:
                    for i in range(NT):
                        pe.wait_ge(normed, NT * (len(passes) - 1) + i + 1)
                        if i >= 4:
                            pe.wait_ge(copied, i - 3)
                            if len(targets) > 1:
                                pe.wait_ge(copied2, i - 3)
                        for k in range(DC):
                            ins = pe.transpose(ps[:, i % 4, TN * k:TN * k + TN], z[:, i, column(k)], c.ident[0:TN, 0:TN])
                        ins.then_inc(turned, 1)


def project_tokens(nc, c, src_t, nk, w_d, out_d, bias_d=None, residuals=(), width=D, send=None, columns=(), y=None):
    with ExitStack() as ctx:
        sb = lambda name, shape, dt=F32: ctx.enter_context(nc.sbuf_tensor(f"{name}_{nc.next_id()}", shape, dt))
        w = sb("pt_w", [128, nk, width])
        res = [sb("pt_res", [TN, 2, width]) for _ in residuals]
        keep = y is not None
        y = y if keep else sb("pt_y", [TN, 2, width])
        bias = sb("pt_bias", [TN, width]) if bias_d is not None else None
        ps = ctx.enter_context(nc.psum_tensor(f"pt_ps_{nc.next_id()}", [128, 4, 512], F32))
        with stage(nc, "weights", "res0", "res1", "summed", "added", "st0", "st1", "own", "sent") as (
                block, weights, res0, res1, summed, added, st0, st1, own_s, sent):
            if send is not None:
                @block.gpsimd
                def _(pool):
                    send_edges(pool, send, columns, sent)

            res_in = (res0, res1)
            st = (st0, st1)
            per = 16 * len(residuals)

            @block.sync
            def _(sp):
                for k in range(0, nk, 4):
                    sp.dma_start(w[:, k:k + 4, :], w_d[:, k:k + 4, :]).then_inc(weights, 16)
                if bias is not None:
                    sp.dma_start(bias[:, :], bias_d.to_broadcast((TN, width))).then_inc(weights, 16)
                for i in range(NT + 1):
                    if i < NT and residuals:
                        if i >= 2:
                            sp.wait_ge(added, i - 1)
                        for r, d in zip(res, residuals):
                            sp.dma_start(r[:, i % 2, :], tiles_of(d)[:, i, :]).then_inc(res_in[i % 2], 16)
                    if i >= 1 and not keep:
                        sp.wait_ge(added, i)
                        sp.dma_start(tiles_of(out_d)[:, i - 1, :], y[:, (i - 1) % 2, :]).then_inc(st[(i - 1) % 2], 16)
                for s in () if keep else st:
                    sp.wait_ge(s, 16 * NT // 2)

            @block.tensor
            def _(pe):
                pe.wait_ge(weights, 16 * (nk // 4 + (bias is not None)))
                for i in range(NT):
                    if i >= 4:
                        pe.wait_ge(added, i - 3)
                    for k in range(nk):
                        ins = pe.matmul(ps[0:TN, i % 4, 0:width], src_t[:, k, TN * i:TN * i + TN], w[:, k, :],
                                        start=(k == 0), stop=(k == nk - 1))
                    ins.then_inc(summed, 1)

            @block.vector
            def _(dve):
                own = Chain(dve, own_s)
                dve.wait_ge(weights, 16 * (nk // 4 + (bias is not None)))
                for i in range(NT):
                    dve.wait_ge(summed, i + 1)
                    if residuals:
                        dve.wait_ge(res_in[i % 2], per * (i // 2 + 1))
                    if i >= 2 and not keep:
                        dve.wait_ge(st[i % 2], 16 * (i // 2))
                    terms = ([bias[:, :]] if bias is not None else []) + [r[:, i % 2, :] for r in res]
                    cur = ps[0:TN, i % 4, 0:width]
                    out = y[:, i if keep else i % 2, :]
                    if not terms:
                        ins = dve.tensor_copy(out, cur)
                    for n, t in enumerate(terms):
                        ins = dve.tensor_tensor(out, cur, t, ALU.add)
                        cur = out
                        if n < len(terms) - 1:
                            own.step(ins)
                    ins.then_inc(added, 1)


def project_features(nc, c, src_t, w_d, bias_d, nout, dst_t, residual_t=None, pick=None):
    with ExitStack() as ctx:
        sb = lambda name, shape, dt=F32: ctx.enter_context(nc.sbuf_tensor(f"{name}_{nc.next_id()}", shape, dt))
        w = sb("pf_w", [128, DC, 128 * nout])
        bias = sb("pf_bias", [128, nout])
        ps = ctx.enter_context(nc.psum_tensor(f"pf_ps_{nc.next_id()}", [128, 6, 512], F32))
        units = [(o, s) for o in range(nout) for s in COLS]
        with stage(nc, "weights", "summed", "done") as (block, weights, summed, done):
            @block.sync
            def _(sp):
                e = sp.value_load(pick, min_val=0, max_val=3) if pick is not None else None
                sp.dma_start(w[:, :, :], w_d(e)).then_inc(weights, 16)
                sp.dma_start(bias[:, :], bias_d(e)).then_inc(weights, 16)
                sp.wait_ge(weights, 32)

            @block.tensor
            def _(pe):
                pe.wait_ge(weights, 32)
                for u, (o, s) in enumerate(units):
                    if u >= 6:
                        pe.wait_ge(done, u - 5)
                    for k in range(DC):
                        ins = pe.matmul(ps[:, u % 6, 0:s.stop - s.start], w[:, k, 128 * o:128 * o + 128],
                                        src_t[:, k, s], start=(k == 0), stop=(k == DC - 1))
                    ins.then_inc(summed, 1)

            @block.vector
            def _(dve):
                dve.wait_ge(weights, 32)
                for u, (o, s) in enumerate(units):
                    dve.wait_ge(summed, u + 1)
                    cur = ps[:, u % 6, 0:s.stop - s.start]
                    if residual_t is None:
                        ins = dve.tensor_scalar(dst_t[:, o, s], cur, bias[:, o:o + 1], None, ALU.add)
                    else:
                        ins = dve.scalar_tensor_tensor(dst_t[:, o, s], cur, bias[:, o:o + 1],
                                                       residual_t[:, o, s], ALU.add, ALU.add)
                    ins.then_inc(done, 1)


def mlp(nc, c, src_t, w1_d, w2_d, b1, b2_d, parts, out_d):
    F32R = mybir.dt.float32r
    groups = [range(0, 6), range(6, NT)]
    OC = MLP // 128
    CH = [(g, o) for g in range(len(groups)) for o in range(OC)]
    first = lambda g: groups[g][0] * TN
    pieces = [[(0, 500), (500, 750)], [(0, 500)]]
    GN = len(groups[0]) * TN
    with ExitStack() as ctx:
        sb = lambda name, shape, dt=F32: ctx.enter_context(nc.sbuf_tensor(f"{name}_{nc.next_id()}", shape, dt))
        s_hi, s_lo = (sb(f"ml_s{n}", [128, DC, N], F32R) for n in range(2))
        w1 = sb("ml_w1", [128, 2, DC, 128])
        w2 = sb("ml_w2", [128, 2, D])
        w1_hi, w1_lo = (sb(f"ml_w1{n}", [128, 3, DC, 128], F32R) for n in range(2))
        w2_hi, w2_lo = (sb(f"ml_w2{n}", [128, 3, D], F32R) for n in range(2))
        h = sb("ml_h", [128, 2, GN])
        h_hi, h_lo = (sb(f"ml_h{n}", [128, 2, GN], F32R) for n in range(2))
        res = sb("ml_res", [TN, NT, D])
        part = sb("ml_part", [TN, NT, D])
        b2 = sb("ml_b2", [TN, D])
        ph = ctx.enter_context(nc.psum_tensor(f"ml_ph_{nc.next_id()}", [128, 2, 512], F32))
        py = ctx.enter_context(nc.psum_tensor(f"ml_py_{nc.next_id()}", [128, 6, 512], F32))
        with stage(nc, "w_in0", "w_in1", "parts_in", "with_part", "with_bias", "s_high", "s_low", "w_high", "w_low",
                   "h_sum", "h_made", "h_high", "h_low", "y_sum", "finished", "stored") as (
                block, w_in0, w_in1, parts_in, with_part, with_bias, s_high, s_low, w_high, w_low, h_sum, h_made,
                h_high, h_low, y_sum, finished, stored):
            w_in = (w_in0, w_in1)

            @block.sync
            def _(sp):
                def load(n):
                    o = CH[n][1]
                    sp.dma_start(w1[:, n % 2, :, :], w1_d[:, :, 128 * o:128 * o + 128]).then_inc(w_in[n % 2], 16)
                    sp.dma_start(w2[:, n % 2, :], w2_d[:, o, :]).then_inc(w_in[n % 2], 16)

                load(0)
                load(1)
                sp.dma_start(res[:, :, :], tiles_of(parts[0])).then_inc(parts_in, 16)
                sp.dma_start(part[:, :, :], tiles_of(parts[1])).then_inc(parts_in, 16)
                sp.dma_start(b2[:, :], b2_d.to_broadcast((TN, D))).then_inc(parts_in, 16)
                for n in range(2, len(CH)):
                    sp.wait_ge(w_high, 2 * (n - 1))
                    sp.wait_ge(w_low, 2 * (n - 1))
                    load(n)
                    if n == OC + 2:
                        for i in groups[0]:
                            sp.wait_ge(finished, i + 1)
                            sp.dma_start(tiles_of(out_d)[:, i, :], res[:, i, :]).then_inc(stored, 16)
                for i in groups[1]:
                    sp.wait_ge(finished, i + 1)
                    sp.dma_start(tiles_of(out_d)[:, i, :], res[:, i, :]).then_inc(stored, 16)
                sp.wait_ge(stored, 16 * NT)

            @block.gpsimd
            def _(pool):
                pool.wait_ge(parts_in, 48)
                for i in range(NT):
                    pool.tensor_tensor(res[:, i, :], res[:, i, :], part[:, i, :], ALU.add).then_inc(with_part, 1)
                    pool.wait_ge(with_part, i + 1)
                    pool.tensor_tensor(res[:, i, :], res[:, i, :], b2[:, :], ALU.add).then_inc(with_bias, 1)
                    pool.wait_ge(with_bias, i + 1)

            @block.tensor
            def _(pe):
                pe.wait_ge(s_high, DC)
                pe.wait_ge(s_low, DC)
                for n in range(len(CH) + 1):
                    if n < len(CH):
                        g, o = CH[n]
                        pe.wait_ge(w_high, 2 * n + 2)
                        pe.wait_ge(w_low, 2 * n + 2)
                        if n >= 1:
                            pe.wait_ge(h_made, n)
                        for m, (a, b) in enumerate(pieces[g]):
                            terms = [(w, x, k) for w, x in ((w1_hi, s_hi), (w1_hi, s_lo), (w1_lo, s_hi)) for k in range(DC)]
                            for t, (w, x, k) in enumerate(terms):
                                ins = pe.matmul(ph[:, m, 0:b - a], w[:, n % 3, k, :], x[:, k, first(g) + a:first(g) + b],
                                                start=(t == 0), stop=(t == len(terms) - 1))
                        ins.then_inc(h_sum, 1)
                    if n >= 1:
                        v = n - 1
                        g, o = CH[v]
                        pe.wait_ge(h_high, v + 1)
                        pe.wait_ge(h_low, v + 1)
                        if o == 0 and g == 1:
                            pe.wait_ge(finished, len(groups[0]))
                        for i in range(len(groups[g])):
                            terms = ((h_hi, w2_hi), (h_hi, w2_lo), (h_lo, w2_hi))
                            for t, (x, w) in enumerate(terms):
                                ins = pe.matmul(py[0:TN, i, :], x[:, v % 2, TN * i:TN * i + TN], w[:, v % 3, :],
                                                start=(o == 0 and t == 0), stop=(o == OC - 1 and t == 2))
                        ins.then_inc(y_sum, 1)

            @block.scalar
            def _(act):
                def split(n):
                    act.wait_ge(w_in[n % 2], 32 * (n // 2 + 1))
                    if n >= 3:
                        act.wait_ge(y_sum, n - 2)
                    act.activation(w1_hi[:, n % 3, :, :], w1[:, n % 2, :, :], ACT.Copy).then_inc(w_high, 1)
                    act.activation(w2_hi[:, n % 3, :], w2[:, n % 2, :], ACT.Copy).then_inc(w_high, 1)

                for k in range(DC):
                    act.activation(s_hi[:, k, :], src_t[:, k, :], ACT.Copy).then_inc(s_high, 1)
                split(0)
                for n, (g, o) in enumerate(CH):
                    if n + 1 < len(CH):
                        split(n + 1)
                    act.wait_ge(h_sum, n + 1)
                    if n >= 2:
                        act.wait_ge(h_low, n - 1)
                    for m, (a, b) in enumerate(pieces[g]):
                        ins = act.activation(h[:, n % 2, a:b], ph[:, m, 0:b - a], ACT.Gelu, bias=b1[:, o:o + 1])
                    ins.then_inc(h_made, 1)

            @block.vector
            def _(dve):
                def split(n):
                    dve.wait_ge(w_high, 2 * n + 2)
                    if n >= 3:
                        dve.wait_ge(y_sum, n - 2)
                    dve.tensor_tensor(w1_lo[:, n % 3, :, :], w1[:, n % 2, :, :], w1_hi[:, n % 3, :, :].bitcast(F32),
                                      ALU.subtract).then_inc(w_low, 1)
                    dve.tensor_tensor(w2_lo[:, n % 3, :], w2[:, n % 2, :], w2_hi[:, n % 3, :].bitcast(F32),
                                      ALU.subtract).then_inc(w_low, 1)

                def finish(g):
                    dve.wait_ge(y_sum, OC * (g + 1))
                    for i, t in enumerate(groups[g]):
                        dve.wait_ge(with_bias, t + 1)
                        dve.tensor_tensor(res[:, t, :], res[:, t, :], py[0:TN, i, :], ALU.add).then_inc(finished, 1)

                for k in range(DC):
                    dve.wait_ge(s_high, k + 1)
                    dve.tensor_tensor(s_lo[:, k, :], src_t[:, k, :], s_hi[:, k, :].bitcast(F32), ALU.subtract)\
                        .then_inc(s_low, 1)
                split(0)
                for n, (g, o) in enumerate(CH):
                    if n + 1 < len(CH):
                        split(n + 1)
                    w = pieces[g][-1][1]
                    dve.wait_ge(h_made, n + 1)
                    if n >= 2:
                        dve.wait_ge(y_sum, n - 1)
                    dve.tensor_copy(h_hi[:, n % 2, 0:w], h[:, n % 2, 0:w]).then_inc(h_high, 1)
                    dve.wait_ge(h_high, n + 1)
                    dve.tensor_tensor(h_lo[:, n % 2, 0:w], h[:, n % 2, 0:w], h_hi[:, n % 2, 0:w].bitcast(F32),
                                      ALU.subtract).then_inc(h_low, 1)
                    if n == OC:
                        finish(0)
                finish(1)


def attention(nc, c, q_src, kv_src, out_t, wq_d, wk_d, wv_d, bq_d, bk_d, bv_d, causal=False, pick=None, send=None):
    biased = bq_d is not None
    F32R = mybir.dt.float32r
    with ExitStack() as ctx:
        sb = lambda name, shape, dt=F32: ctx.enter_context(nc.sbuf_tensor(f"{name}_{nc.next_id()}", shape, dt))
        wq, wk, wv = (sb(f"at_w{n}", [128, DC, 128]) for n in "qkv")
        bias_all = sb("at_ball", [128, 3, HEADS // 2])
        bias = sb("at_bias", [128, 3])
        bq, bk, bv = (bias[:, n:n + 1] for n in range(3))
        q_two = [sb(f"at_q{h}", [128, N], F32R) for h in range(2)]
        k_hi = [sb(f"at_kh{h}", [128, N], F32R) for h in range(2)]
        k_lo = [sb(f"at_kl{h}", [128, N], F32R) for h in range(2)]
        v_two = sb("at_v", [TN, NT, 2, 2, HD], F32R)
        p = sb("at_p", [TN, 2, N])
        p_hi = sb("at_phi", [TN, 2, NT, 2 * TN], F32R)
        p_lo = sb("at_plo", [TN, 2, NT, 2 * TN], F32R)
        sums = sb("at_sums", [128, 2, 3, 2 * TN])
        whole = sb("at_whole", [128, 2 * TN])
        diag = sb("at_diag", [TN, 4, TN])
        ones = sb("at_ones", [TN, 128])
        neg_max = sb("at_max", [TN, 2 * NT])
        total = sb("at_sum", [TN, 2 * NT])
        inverse = sb("at_inv", [TN, 2 * NT])
        if send is not None:
            table_d, rows, slots = send
            SEND = EC // (HEADS // 2)
            rows_now = sb("at_rows", [TN, SEND, ROW])
            slots_now = sb("at_slots", [TN, SEND], I32)
        pscore = ctx.enter_context(nc.psum_tensor(f"at_ps_{nc.next_id()}", [128, 5, 512], F32))
        pturn = ctx.enter_context(nc.psum_tensor(f"at_pt_{nc.next_id()}", [128, 2, 512], F32))
        pout = ctx.enter_context(nc.psum_tensor(f"at_po_{nc.next_id()}", [128, 512], F32))
        TAIL = N - 1024
        flat = pscore[:, :, :].rearrange("p a b -> p (a b)")
        score = [flat[:, 0:N], flat[:, 5 * 512 - N:5 * 512]]
        pieces = [[(0, 512), (512, 1024), (1024, N)], [(TAIL, TAIL + 512), (TAIL + 512, N), (0, TAIL)]]
        units = [(h, i) for m in range(0, NT, 2) for h in range(2) for i in (m, m + 1)]
        NU = len(units)
        keys = [(i // 2 * 2 + 2 if causal else NT) for _, i in units]
        parts = [-(-n // 4) for n in keys]
        upto = lambda u: sum(parts[:u])
        q_bank = [pscore[:, n, :] for n in range(3)]
        k_bank = [pscore[:, 3, :], pscore[:, 4, :], pscore[:, 0, :]]
        v_bank = [pturn[:, 0, :], pturn[:, 1, :], pout]

        def load(sp, e, pair, which, sem):
            for dst, src in which:
                sp.dma_start(dst[:, :, :], src(e, pair)).then_inc(sem, 16)

        def project(pe, w, src, dst, s, ready):
            for k in range(DC):
                ins = pe.matmul(dst[:, 0:s.stop - s.start], w[:, k, :], src[:, k, s], start=(k == 0), stop=(k == DC - 1))
            ins.then_inc(ready, 1)

        def q_high(act, banks, q_sum, q_hi):
            for n in banks:
                s = COLS[n]
                act.wait_ge(q_sum, n + 1)
                for h in range(2):
                    r = slice(64 * h, 64 * h + 64)
                    act.activation(q_two[h][r, s], q_bank[n][r, 0:s.stop - s.start], ACT.Identity,
                                   bias=bq[r, 0:1]).then_inc(q_hi, 1)

        def k_highs(act, k_sum, k_high, k_high_too):
            for n, s in enumerate(COLS):
                act.wait_ge(k_sum, n + 1)
                for h in range(2):
                    r = slice(64 * h, 64 * h + 64)
                    act.activation(k_hi[h][r, s], k_bank[n][r, 0:s.stop - s.start], ACT.Identity,
                                   bias=bk[r, 0:1]).then_inc(k_high, 1)
                for h in range(2):
                    act.wait_ge(k_high, 2 * n + h + 1)
                    act.activation(k_hi[h][64 - 64 * h:128 - 64 * h, s], k_hi[h][64 * h:64 * h + 64, s], ACT.Copy)\
                        .then_inc(k_high_too, 1)

        def q_low(dve, banks, q_hi, q_lo):
            for n in banks:
                s = COLS[n]
                for h in range(2):
                    r, other = slice(64 * h, 64 * h + 64), slice(64 - 64 * h, 128 - 64 * h)
                    dve.wait_ge(q_hi, 2 * n + 2)
                    dve.scalar_tensor_tensor(q_two[h][other, s], q_bank[n][r, 0:s.stop - s.start], bq[r, 0:1],
                                             q_two[h][r, s].bitcast(F32), ALU.add, ALU.subtract).then_inc(q_lo, 1)

        def k_lows(dve, q_lo, k_high, k_low, k_low_too):
            for n, s in enumerate(COLS):
                dve.wait_ge(k_high, 2 * n + 2)
                for h in range(2):
                    r = slice(64 * h, 64 * h + 64)
                    dve.scalar_tensor_tensor(k_lo[h][r, s], k_bank[n][r, 0:s.stop - s.start], bk[r, 0:1],
                                             k_hi[h][r, s].bitcast(F32), ALU.add, ALU.subtract).then_inc(k_low, 1)
                for h in range(2):
                    dve.wait_ge(k_low, 2 * n + h + 1)
                    dve.tensor_copy(k_lo[h][64 - 64 * h:128 - 64 * h, s], k_lo[h][64 * h:64 * h + 64, s])\
                        .then_inc(k_low_too, 1)
            dve.wait_ge(q_lo, 6)
            dve.wait_ge(k_low_too, 6)

        def scale_q(pool, loaded, scaled):
            pool.wait_ge(loaded, 32)
            pool.tensor_scalar(wq[:, :, :], wq[:, :, :], HD ** -0.5, None, ALU.mult).then_inc(scaled, 1)
            pool.wait_ge(scaled, 1)

        with stage(nc, "filled", "loaded", "v_loaded", "bias_in", "scaled", "bias_set", "q_sum", "k_sum", "q_hi", "q_lo",
                   "k_high", "k_low", "k_high_too", "k_low_too") as (
                block, filled, loaded, v_loaded, bias_in, scaled, bias_set, q_sum, k_sum, q_hi, q_lo, k_high, k_low,
                k_high_too, k_low_too):
            @block.vector
            def _(dve):
                dve.memset(ones[:, :], 1.0).then_inc(filled, 1)
                if not biased:
                    dve.memset(bias_all[:, :, :], 0.0).then_inc(filled, 1)
                dve.wait_ge(filled, 1 + (not biased))
                dve.wait_ge(bias_set, 1)
                q_low(dve, range(3), q_hi, q_lo)
                k_lows(dve, q_lo, k_high, k_low, k_low_too)

            @block.scalar
            def _(act):
                act.wait_ge(bias_set, 1)
                q_high(act, range(3), q_sum, q_hi)
                k_highs(act, k_sum, k_high, k_high_too)

            @block.tensor
            def _(pe):
                pe.wait_ge(scaled, 1)
                for n, s in enumerate(COLS):
                    project(pe, wq, q_src, q_bank[n], s, q_sum)
                for n in range(2):
                    project(pe, wk, kv_src, k_bank[n], COLS[n], k_sum)
                pe.wait_ge(q_lo, 2)
                project(pe, wk, kv_src, k_bank[2], COLS[2], k_sum)

            @block.sync
            def _(sp):
                e = sp.value_load(pick, min_val=0, max_val=3) if pick is not None else None
                load(sp, e, 0, ((wq, wq_d), (wk, wk_d)), loaded)
                load(sp, e, 0, ((wv, wv_d),), v_loaded)
                sp.wait_ge(v_loaded, 16)
                if biased:
                    for n, b in enumerate((bq_d, bk_d, bv_d)):
                        sp.dma_start(bias_all[:, n, :], b(e)).then_inc(bias_in, 16)

            @block.gpsimd
            def _(pool):
                scale_q(pool, loaded, scaled)
                if biased:
                    pool.wait_ge(bias_in, 48)
                    pool.tensor_scalar(bias_all[:, 0, :], bias_all[:, 0, :], HD ** -0.5, None, ALU.mult).then_inc(scaled, 1)
                    pool.wait_ge(scaled, 2)
                else:
                    pool.wait_ge(filled, 2)
                pool.tensor_copy(bias[:, :], bias_all[:, :, 0]).then_inc(bias_set, 1)
                pool.wait_ge(bias_set, 1)

        def turn(pair, last):
            with stage(nc, "loaded", "v_loaded", "scaled", "q_sum", "k_sum", "v_sum", "q_hi", "q_lo", "k_high", "k_low", "k_high_too", "k_low_too", "v_high",
                       "v_low", "scored", "masked", "max_ready", "exp_done", "inv_done", "diag_made", "turned", "hi_done", "lo_done",
                       "pv_done", "out_read", "whole_made", "o_done", "last_made", "bias_set", "staged", "sent") as (
                    block, loaded, v_loaded, scaled, q_sum, k_sum, v_sum, q_hi, q_lo, k_high, k_low, k_high_too,
                    k_low_too, v_high, v_low, scored,
                    masked, max_ready, exp_done, inv_done, diag_made, turned, hi_done, lo_done, pv_done, out_read, whole_made,
                    o_done, last_made, bias_set, staged, sent):
                @block.sync
                def _(sp):
                    if last:
                        return
                    e = sp.value_load(pick, min_val=0, max_val=3) if pick is not None else None
                    load(sp, e, pair + 1, ((wq, wq_d), (wk, wk_d)), loaded)
                    sp.wait_ge(v_sum, NT)
                    load(sp, e, pair + 1, ((wv, wv_d),), v_loaded)
                    sp.wait_ge(loaded, 32)
                    sp.wait_ge(v_loaded, 16)

                @block.gpsimd
                def _(pool):
                    pool.tensor_copy(bv, bias_all[:, 2, bass.ds(pair, 1)]).then_inc(bias_set, 1)
                    if not last:
                        pool.tensor_copy(bias[:, 0:2], bias_all[:, 0:2, bass.ds(pair + 1, 1)].rearrange("p n a -> p (n a)"))\
                            .then_inc(bias_set, 1)
                    pool.wait_ge(bias_set, 1 + (not last))
                    if send is not None:
                        pool.tensor_copy(rows_now[:, :, :], rows[:, bass.ds(pair * SEND, SEND), :]).then_inc(staged, 1)
                        pool.tensor_copy(slots_now[:, :], slots[:, bass.ds(pair * SEND, SEND)]).then_inc(staged, 1)
                        pool.wait_ge(staged, 2)

                    def finish(m):
                        pool.wait_ge(out_read, 6 * m + 6)
                        pool.tensor_tensor(whole[:, :], sums[:, m % 2, 0, :], sums[:, m % 2, 1, :], ALU.add)\
                            .then_inc(whole_made, 1)
                        pool.wait_ge(whole_made, (1 + biased) * m + 1)
                        dst = out_t[:, bass.ds(pair, 1), 2 * TN * m:2 * TN * m + 2 * TN].rearrange("p a n -> p (a n)")
                        if biased:
                            pool.tensor_tensor(whole[:, :], whole[:, :], sums[:, m % 2, 2, :], ALU.mult).then_inc(whole_made, 1)
                            pool.wait_ge(whole_made, 2 * m + 2)
                            pool.tensor_tensor(dst, whole[:, :], bv.to_broadcast((128, 2 * TN)), ALU.add).then_inc(o_done, 1)
                        else:
                            pool.tensor_tensor(dst, whole[:, :], sums[:, m % 2, 2, :], ALU.mult).then_inc(o_done, 1)
                        pool.wait_ge(o_done, m + 1)

                    for u in range(NU):
                        if u >= 8 and u % 4 == 0:
                            finish(u // 4 - 2)
                        pool.wait_ge(inv_done, u + 1)
                        if u >= 4:
                            pool.wait_ge(pv_done, (u - 4) // 2 + 1)
                        pool.tensor_scalar(diag[:, u % 4, :], c.ident[0:TN, 0:TN], inverse[:, u:u + 1], None, ALU.mult)\
                            .then_inc(diag_made, 1)
                        pool.wait_ge(diag_made, u + 1)
                        if u == NU // 2 and not last:
                            scale_q(pool, loaded, scaled)
                        if send is not None:
                            for t in range(SEND * u // NU, SEND * (u + 1) // NU):
                                pool.indirect_dma_start(
                                    table_d, bass.IndirectOffsetOnAxis(ap=slots_now[:, t:t + 1], axis=0),
                                    rows_now[:, t, :], None).then_inc(sent, 16)
                    finish(NU // 4 - 2)
                    if send is not None:
                        pool.wait_ge(sent, 16 * SEND)

                @block.tensor
                def _(pe):
                    def project_v(tiles):
                        for i in tiles:
                            for k in range(DC):
                                ins = pe.matmul(v_bank[i // 4][0:TN, 128 * (i % 4):128 * (i % 4) + 128],
                                                kv_src[:, k, TN * i:TN * i + TN], wv[:, k, :],
                                                start=(k == 0), stop=(k == DC - 1))
                            ins.then_inc(v_sum, 1)

                    def score_part(u, n):
                        if not u < NU:
                            return
                        h, i = units[u]
                        w = TN * keys[u]
                        there = [(a, min(b, w)) for a, b in pieces[u % 2] if a < w]
                        if n >= len(there):
                            return
                        a, b = there[n]
                        if u >= 2 and n == 0:
                            pe.wait_ge(exp_done, u - 1)
                        if u >= 1 and a == (0 if u % 2 else 1024):
                            pe.wait_ge(exp_done, u)
                        for m, k in enumerate((k_hi[h], k_lo[h])):
                            ins = pe.matmul(score[u % 2][0:TN, a:b], q_two[h][:, TN * i:TN * i + TN], k[:, a:b],
                                            start=(m == 0), stop=(m == 1))
                        if n == len(there) - 1:
                            ins.then_inc(scored, 1)

                    def turn_part(u, n):
                        if not 0 <= u < NU or n >= parts[u]:
                            return
                        if upto(u) + n < 2:
                            pe.wait_ge(v_high, upto(u) + n + 1)
                            pe.wait_ge(v_low, upto(u) + n + 1)
                        if n == 0:
                            pe.wait_ge(exp_done, u + 1)
                        g = upto(u) + n
                        if g >= 2:
                            pe.wait_ge(lo_done, g - 1)
                        for j in range(4 * n, min(4 * n + 4, keys[u])):
                            ins = pe.transpose(pturn[0:TN, g % 2, TN * (j % 4):TN * (j % 4) + TN],
                                               p[:, u % 2, TN * j:TN * j + TN], c.ident[0:TN, 0:TN])
                        ins.then_inc(turned, 1)

                    def duo_sum(q, half, piece):
                        if not 0 <= q < NU // 2:
                            return
                        h, u = units[2 * q][0], 2 * q + 1
                        if half == 0 and piece == 0:
                            pe.wait_ge(lo_done, upto(u + 1))
                            if q == 0:
                                pe.wait_ge(v_high, 3)
                                pe.wait_ge(v_low, 3)
                            else:
                                pe.wait_ge(out_read, 3 * q)
                            pe.wait_ge(diag_made, 2 * q + 2)
                            for m in range(2):
                                pe.matmul(pout[:, TN * (2 + m):TN * (3 + m)], ones[:, :],
                                          diag[:, (2 * q + m) % 4, :], start=True, stop=True)
                        src = (p_hi, p_lo)[half]
                        cut = keys[u] * 7 // 10
                        for j in (range(cut), range(cut, keys[u]))[piece]:
                            ins = pe.matmul(pout[:, 0:2 * TN], v_two[:, j, h, :, :].rearrange("p a d -> p (a d)"),
                                            src[:, q % 2, j, :], start=(half == 0 and j == 0),
                                            stop=(half == 1 and j == keys[u] - 1))
                        if half == 1 and piece == 1:
                            ins.then_inc(pv_done, 1)

                    for s in range(NU + 4):
                        if s == 2:
                            project_v(range(2, NT))
                        turn_part(s - 2, 0)
                        score_part(s, 0)
                        turn_part(s - 2, 1)
                        duo_sum((s - 4) // 2, s % 2, 0)
                        score_part(s, 1)
                        turn_part(s - 2, 2)
                        duo_sum((s - 4) // 2, s % 2, 1)
                        if s == 1:
                            project_v(range(2))
                        score_part(s, 2)
                        if last:
                            continue
                        if s == NU:
                            pe.wait_ge(scaled, 1)
                            pe.wait_ge(exp_done, NU - 1)
                            project(pe, wq, q_src, q_bank[0], COLS[0], q_sum)
                        if s == NU + 1:
                            project(pe, wq, q_src, q_bank[1], COLS[1], q_sum)
                        if s == NU + 2:
                            pe.wait_ge(exp_done, NU)
                            project(pe, wq, q_src, q_bank[2], COLS[2], q_sum)
                    if not last:
                        for n in range(2):
                            project(pe, wk, kv_src, k_bank[n], COLS[n], k_sum)
                        pe.wait_ge(q_lo, 2)
                        project(pe, wk, kv_src, k_bank[2], COLS[2], k_sum)

                @block.scalar
                def _(act):

                    def high_part(u, n):
                        if not 0 <= u < NU or n >= parts[u]:
                            return
                        if u % 2 == 0 and n == 0 and u >= 4:
                            act.wait_ge(pv_done, u // 2 - 1)
                        g = upto(u) + n
                        act.wait_ge(turned, g + 1)
                        m = min(4, keys[u] - 4 * n)
                        act.activation(p_hi[:, u // 2 % 2, 4 * n:4 * n + m, TN * (u % 2):TN * (u % 2) + TN],
                                       pturn[0:TN, g % 2, 0:TN * m].rearrange("p (a b) -> p a b", b=TN),
                                       ACT.Copy).then_inc(hi_done, 1)

                    for s in range(NU + 4):
                        if s > 2:
                            high_part(s - 2, 0)
                            high_part(s - 2, 1)
                        if 1 <= s <= NU:
                            t = s - 1
                            act.wait_ge(max_ready, t + 1)
                            if t >= 2:
                                act.wait_ge(turned, upto(t - 1))
                            w = TN * keys[t]
                            act.activation(p[:, t % 2, 0:w], score[t % 2][0:TN, 0:w], ACT.Exp,
                                           bias=neg_max[:, t:t + 1], accum_out=total[:, t:t + 1]).then_inc(exp_done, 1)
                        if s == 2:
                            for n in range(3):
                                m = min(4, NT - 4 * n)
                                act.wait_ge(v_sum, 4 * n + m)
                                act.activation(v_two[:, 4 * n:4 * n + m, :, 0, :],
                                               v_bank[n][0:TN, 0:128 * m].rearrange("p (a h d) -> p a h d", a=m, h=2),
                                               ACT.Copy).then_inc(v_high, 1)
                            high_part(0, 0)
                            high_part(0, 1)
                        high_part(s - 2, 2)
                        if s == NU + 3 and not last:
                            act.wait_ge(bias_set, 2)
                            q_high(act, (0, 1), q_sum, q_hi)
                        if s >= 5 and s % 2 == 1:
                            q = (s - 5) // 2
                            act.wait_ge(pv_done, q + 1)
                            if q >= 4:
                                act.wait_ge(o_done, q // 2 - 1)
                            r = slice(HD * units[2 * q][0], HD * units[2 * q][0] + HD)
                            act.activation(sums[r, q // 2 % 2, 0, :], pout[0:HD, 0:2 * TN], ACT.Copy).then_inc(out_read, 1)
                            act.activation(sums[r, q // 2 % 2, 1, :], pout[HD:2 * HD, 0:2 * TN], ACT.Copy).then_inc(out_read, 1)
                            act.activation(sums[r, q // 2 % 2, 2, :], pout[r, 2 * TN:4 * TN], ACT.Copy).then_inc(out_read, 1)
                    if not last:
                        q_high(act, (2,), q_sum, q_hi)
                        k_highs(act, k_sum, k_high, k_high_too)

                @block.vector
                def _(dve):
                    for s in range(NU + 4):
                        if 2 <= s <= NU + 1:
                            dve.wait_ge(exp_done, s - 1)
                            dve.reciprocal(inverse[:, s - 2:s - 1], total[:, s - 2:s - 1]).then_inc(inv_done, 1)
                        if 1 <= s <= NU:
                            u = s - 1
                            w = TN * keys[u]
                            dve.wait_ge(scored, u + 1)
                            if causal:
                                m = TN * (2 - u % 2)
                                late = score[u % 2][0:TN, w - m:w]
                                dve.tensor_tensor(late, late, c.causal[:, 0:m], ALU.add).then_inc(masked, 1)
                                dve.wait_ge(masked, u + 1)
                            dve.tensor_reduce(neg_max[:, u:u + 1], score[u % 2][0:TN, 0:w], AX, ALU.max, negate=True)\
                                .then_inc(max_ready, 1)
                        if s == 2:
                            for n in range(3):
                                m = min(4, NT - 4 * n)
                                dve.wait_ge(v_high, n + 1)
                                dve.tensor_tensor(v_two[:, 4 * n:4 * n + m, :, 1, :],
                                                  v_bank[n][0:TN, 0:128 * m].rearrange("p (a h d) -> p a h d", a=m, h=2),
                                                  v_two[:, 4 * n:4 * n + m, :, 0, :].bitcast(F32), ALU.subtract).then_inc(v_low, 1)
                        u = s - 2
                        for n in range(parts[u] if 0 <= u < NU else 0):
                            g = upto(u) + n
                            dve.wait_ge(hi_done, g + 1)
                            if u % 2 == 0 and n == 0 and u >= 4:
                                dve.wait_ge(pv_done, u // 2 - 1)
                            m = min(4, keys[u] - 4 * n)
                            at = (slice(None), u // 2 % 2, slice(4 * n, 4 * n + m), slice(TN * (u % 2), TN * (u % 2) + TN))
                            dve.tensor_tensor(p_lo[at], pturn[0:TN, g % 2, 0:TN * m].rearrange("p (a b) -> p a b", b=TN),
                                              p_hi[at].bitcast(F32), ALU.subtract).then_inc(lo_done, 1)
                    if not last:
                        q_low(dve, (0, 1), q_hi, q_lo)
                    m = NU // 4 - 1
                    dve.wait_ge(out_read, 6 * m + 6)
                    dve.wait_ge(o_done, m)
                    dve.tensor_tensor(whole[:, :], sums[:, m % 2, 0, :], sums[:, m % 2, 1, :], ALU.add).then_inc(last_made, 1)
                    dve.wait_ge(last_made, 1)
                    dve.tensor_tensor(whole[:, :], whole[:, :], sums[:, m % 2, 2, :], ALU.mult).then_inc(last_made, 1)
                    dve.wait_ge(last_made, 2)
                    dst = out_t[:, bass.ds(pair, 1), 2 * TN * m:2 * TN * m + 2 * TN].rearrange("p a n -> p (a n)")
                    dve.tensor_tensor(dst, whole[:, :], bv.to_broadcast((128, 2 * TN)), ALU.add).then_inc(last_made, 1)
                    dve.wait_ge(last_made, 3)
                    if not last:
                        q_low(dve, (2,), q_hi, q_lo)
                        k_lows(dve, q_lo, k_high, k_low, k_low_too)

        with nc.Fori(0, HEADS // 2 - 1) as pair:
            turn(pair, False)
        turn(HEADS // 2 - 1, True)


def send_edges(pool, send, columns, sent):
    table_d, rows, slots = send
    for t in columns:
        pool.indirect_dma_start(table_d, bass.IndirectOffsetOnAxis(ap=slots[:, t:t + 1], axis=0),
                                rows[:, t, :], None).then_inc(sent, 16)
    pool.wait_ge(sent, 16 * len(columns))


def place_edges(nc, c, key_d, other_d, w_d, a4_d, a8_d, table_d, tile_base, rows, slot_i, send=None, columns=()):
    with ExitStack() as ctx:
        sb = lambda name, shape, dt=F32: ctx.enter_context(nc.sbuf_tensor(f"{name}_{nc.next_id()}", shape, dt))
        key = sb("so_key", [TN, EC], I32)
        rows_i = rows[:, :, :].bitcast(I32)
        other = sb("so_other", [TN, EC], I32)
        w = sb("so_w", [TN, EC])
        a4 = sb("so_a4", [TN, EC * 4])
        a8 = sb("so_a8", [TN, EC * 8])
        zero = sb("so_zero", [128, NS * ROW])
        keyf = sb("so_keyf", [TN, EC])
        bucket = sb("so_bucket", [TN, EC])
        oh = sb("so_oh", [TN, NT, EC], BF16)
        flat = sb("so_flat", [128, NT * EC])
        run = sb("so_run", [128, NT * EC])
        start = sb("so_start", [128, NT + 1])
        count = sb("so_count", [128, NT])
        count_i = sb("so_counti", [128, NT], I32)
        ntile = sb("so_ntile", [128, NT])
        off = sb("so_off", [128, NT])
        delta = sb("so_delta", [128, NT])
        val = sb("so_val", [TN, NT, EC])
        slot = sb("so_slot", [TN, EC])
        part_i = sb("so_parti", [TN, EC], I32)
        tile_i = sb("so_tilei", [TN, EC], I32)
        base = sb("so_base", [128, NS])
        ps = ctx.enter_context(nc.psum_tensor(f"so_ps_{nc.next_id()}", [128, 8, 512], F32))
        B = 3 * EC
        banks = [(n, 3 * n, min(3, NT - 3 * n)) for n in range(-(-NT // 3))]
        row3 = lambda d: d.rearrange("(p t) c -> p (t c)", p=TN)
        with stage(nc, "loaded", "own", "zeroed", "hot", "counted", "placed", "filled", "sent") as (
                block, loaded, own_s, zeroed, hot, counted, placed, filled, sent):
            @block.sync
            def _(sp):
                sp.dma_start(key[:, :], key_d.rearrange("(p t) -> p t", p=TN)).then_inc(loaded, 16)
                sp.dma_start(other[:, :], other_d.rearrange("(p t) -> p t", p=TN)).then_inc(loaded, 16)
                sp.dma_start(w[:, :], w_d.rearrange("(p t) -> p t", p=TN)).then_inc(loaded, 16)
                sp.dma_start(a4[:, :], row3(a4_d)).then_inc(loaded, 16)
                sp.dma_start(a8[:, :], row3(a8_d)).then_inc(loaded, 16)
                sp.wait_ge(zeroed, 1)
                sp.dma_start(table_d.rearrange("(p t) c -> p (t c)", p=128), zero[:, :]).then_inc(filled, 16)
                sp.wait_ge(filled, 16)

            @block.tensor
            def _(pe):
                pe.wait_ge(hot, NT)
                for n, j, m in banks:
                    pe.matmul(ps[:, n, 0:m * EC], c.ones[0:TN, :], oh[:, j:j + m, :].rearrange("p a b -> p (a b)"),
                              start=True, stop=True).then_inc(counted, 1)
                for n, j, m in banks:
                    pe.matmul(ps[0:TN, 4 + n, 0:m * EC], c.lower[0:TN, 0:TN],
                              oh[:, j:j + m, :].rearrange("p a b -> p (a b)"), start=True, stop=True).then_inc(counted, 1)

            @block.vector
            def _(dve):
                dve.memset(zero[:, :], 0.0).then_inc(zeroed, 1)
                own = Chain(dve, own_s)
                dve.wait_ge(loaded, 80)
                own.mark(dve.tensor_copy(rows_i[:, :, 0], other[:, :]))
                own.mark(dve.tensor_copy(rows[:, :, 2], w[:, :]))
                own.mark(dve.memset(rows[:, :, 3], 0.0))
                own.mark(dve.tensor_copy(rows[:, :, 4:8], a4[:, :].rearrange("p (t c) -> p t c", c=4)))
                own.mark(dve.tensor_copy(rows[:, :, 8:16], a8[:, :].rearrange("p (t c) -> p t c", c=8)))
                own.step(dve.tensor_copy(keyf[:, :], key[:, :]))
                own.step(dve.tensor_scalar(bucket[:, :], keyf[:, :], float(TN), None, ALU.is_ge))
                for j in range(2, NT):
                    own.step(dve.scalar_tensor_tensor(bucket[:, :], keyf[:, :], float(TN * j), bucket[:, :],
                                                      ALU.is_ge, ALU.add))
                own.mark(dve.scalar_tensor_tensor(rows[:, :, 1], bucket[:, :], -float(TN), keyf[:, :],
                                                  ALU.mult, ALU.add))
                for j in range(NT):
                    dve.tensor_scalar(oh[:, j, :], bucket[:, :], float(j), None, ALU.is_equal).then_inc(hot, 1)
                for n, j, m in banks:
                    dve.wait_ge(counted, n + 1)
                    own.mark(dve.tensor_copy(flat[:, j * EC:(j + m) * EC], ps[:, n, 0:m * EC]))
                own.join()
                own.step(dve.tensor_tensor_scan(run[:, :], flat[:, :], flat[:, :], 0.0, ALU.add, ALU.bypass))
                own.mark(dve.memset(start[:, 0:1], 0.0))
                own.mark(dve.tensor_copy(start[:, 1:NT + 1],
                                         run[:, :].rearrange("p (j t) -> p j t", j=NT)[:, :, EC - 1]))
                own.join()
                own.mark(dve.tensor_tensor(run[:, :], run[:, :], flat[:, :], ALU.subtract))
                own.step(dve.tensor_tensor(count[:, :], start[:, 1:NT + 1], start[:, 0:NT], ALU.subtract))
                own.step(dve.tensor_scalar(count_i[:, :], count[:, :], float(TE - 1), None, ALU.add))
                own.step(dve.tensor_scalar(count_i[:, :], count_i[:, :], TE.bit_length() - 1, None,
                                           ALU.arith_shift_right))
                own.step(dve.tensor_copy(ntile[:, :], count_i[:, :]))
                own.step(dve.tensor_tensor_scan(off[:, :], ntile[:, :], ntile[:, :], 0.0, ALU.add, ALU.bypass))
                own.step(dve.tensor_tensor(off[:, :], off[:, :], ntile[:, :], ALU.subtract))
                own.step(dve.scalar_tensor_tensor(delta[:, :], off[:, :], float(TE), start[:, 0:NT],
                                                  ALU.mult, ALU.subtract))
                own.step(dve.tensor_scalar(base[:, :], c.iota[:, 0:NS], off[:, 1:2], None, ALU.is_ge))
                for j in range(2, NT):
                    own.step(dve.scalar_tensor_tensor(base[:, :], c.iota[:, 0:NS], off[:, j:j + 1], base[:, :],
                                                      ALU.is_ge, ALU.add))
                own.mark(dve.tensor_copy(tile_base[:, :], base[0:1, :]))
                dve.wait_ge(counted, 8)
                for n, j, m in banks:
                    own.mark(dve.tensor_tensor(val[:, j:j + m, :].rearrange("p a b -> p (a b)"),
                                               run[0:TN, j * EC:(j + m) * EC], ps[0:TN, 4 + n, 0:m * EC], ALU.add))
                own.join()
                for j in range(NT):
                    own.mark(dve.scalar_tensor_tensor(val[:, j, :], val[:, j, :], delta[0:TN, j:j + 1], oh[:, j, :],
                                                      ALU.add, ALU.mult))
                own.join()
                own.step(dve.tensor_reduce(slot[:, :], val[:, :, :].rearrange("p j t -> p t j"), AX, ALU.add))
                own.step(dve.tensor_copy(slot_i[:, :], slot[:, :]))
                own.mark(dve.tensor_scalar(part_i[:, :], slot_i[:, :], TE - 1, None, ALU.bitwise_and))
                own.mark(dve.tensor_scalar(tile_i[:, :], slot_i[:, :], TE.bit_length() - 1, None, ALU.arith_shift_right))
                own.join()
                dve.scalar_tensor_tensor(slot_i[:, :], part_i[:, :], float(NS), tile_i[:, :],
                                         ALU.mult, ALU.add).then_inc(placed, 1)
                dve.wait_ge(placed, 1)

            if send is not None:
                @block.gpsimd
                def _(pool):
                    send_edges(pool, send, columns, sent)


def graph_sum0(nc, c, table_d, tile_base, support_d, x_d, bias_d, acc, send, columns):
    with ExitStack() as ctx:
        sb = lambda name, shape, dt=F32: ctx.enter_context(nc.sbuf_tensor(f"{name}_{nc.next_id()}", shape, dt))
        bias = sb("g0_bias", [TN, D])
        edges = sb("g0_edges", [128, GL, ROW])
        got = sb("g0_got", [128, RING, D])
        hot = sb("g0_hot", [128, GL, TN])
        ps = ctx.enter_context(nc.psum_tensor(f"g0_ps_{nc.next_id()}", [128, 4, 512], F32))
        with stage(nc, "loaded", "own", "sent") as (block, loaded, own_s, sent):
            @block.gpsimd
            def _(pool):
                send_edges(pool, send, columns, sent)

            @block.sync
            def _(sp):
                sp.dma_start(acc[:, :, :], tiles_of(x_d)).then_inc(loaded, 16)
                sp.dma_start(bias[:, :], bias_d.to_broadcast((TN, D))).then_inc(loaded, 16)

            @block.vector
            def _(dve):
                dve.wait_ge(loaded, 32)
                for i in range(NT):
                    dve.tensor_tensor(acc[:, i, :], acc[:, i, :], bias[:, :], ALU.add).then_inc(own_s, 1)
                dve.wait_ge(own_s, NT)
        table = table_d.rearrange("(p t) c -> p t c", p=128)
        with nc.Fori(0, TURNS) as g:
            with stage(nc, "loaded", "hot_ready", "summed", "added", *(f"got{i}" for i in range(RING))) as (
                    block, loaded, hot_ready, summed, added, *got_s):
                @block.sync
                def _(sp):
                    sp.dma_start(edges[:, :, :], table[:, bass.ds(g * GL, GL), :]).then_inc(loaded, 16)
                    sp.wait_ge(loaded, 16)

                @block.gpsimd
                def _(pool):
                    pool.wait_ge(loaded, 16)
                    ids = edges[:, :, :].bitcast(I32)
                    for i in range(GL):
                        if i >= RING:
                            pool.wait_ge(summed, i - RING + 1)
                        pool.indirect_dma_start(got[:, i % RING, :], None, support_d,
                                                bass.IndirectOffsetOnAxis(ap=ids[:, i, 0:1], axis=0))\
                            .then_inc(got_s[i % RING], 16)

                @block.vector
                def _(dve):
                    dve.wait_ge(loaded, 16)
                    for i in range(GL + 4):
                        if i < GL:
                            dve.tensor_scalar(hot[:, i, :], c.iota[:, 0:TN], edges[:, i, 1:2], edges[:, i, 2:3],
                                              ALU.is_equal, ALU.mult).then_inc(hot_ready, 1)
                        if i >= 4:
                            t = i - 4
                            at = dve.value_load(tile_base[0:1, bass.ds(g * GL + t, 1)], min_val=0, max_val=NT - 1)
                            dve.wait_ge(summed, t + 1)
                            if t:
                                dve.wait_ge(added, t)
                            dst = acc[:, bass.ds(at, 1), :].rearrange("p a b -> p (a b)")
                            dve.tensor_tensor(dst, dst, ps[0:TN, t % 4, :], ALU.add).then_inc(added, 1)
                    dve.wait_ge(added, GL)

                @block.tensor
                def _(pe):
                    for i in range(GL):
                        pe.wait_ge(hot_ready, i + 1)
                        pe.wait_ge(got_s[i % RING], 16 * (i // RING + 1))
                        if i >= 4:
                            pe.wait_ge(added, i - 3)
                        pe.matmul(ps[0:TN, i % 4, :], hot[:, i, :], got[:, i % RING, :], start=True, stop=True)\
                            .then_inc(summed, 1)


def route_tokens(nc, c, xn_t, wr_d, b2_d, slot_tok, y_row, gate, part_d, acc, prefetch):
    with ExitStack() as ctx:
        sb = lambda name, shape, dt=F32: ctx.enter_context(nc.sbuf_tensor(f"{name}_{nc.next_id()}", shape, dt))
        wr = sb("rt_w", [128, DC, EXPERTS])
        b2 = sb("rt_b2", [EXPERTS, D])
        logit = sb("rt_logit", [TN, NT, EXPERTS])
        probs = sb("rt_probs", [TN, NT, EXPERTS])
        small = sb("rt_small", [TN, 4, NT])
        top = sb("rt_top", [TN, NT, 8])
        idx = sb("rt_idx", [TN, NT, 8], U32)
        expert = sb("rt_expert", [TN, 2, NT])
        hot = sb("rt_hot", [TN, 2, NT, EXPERTS], BF16)
        both = sb("rt_both", [TN, NT, EXPERTS], BF16)
        before = sb("rt_before", [TN, NT, EXPERTS])
        mine = sb("rt_mine", [TN, NT, EXPERTS])
        pos = sb("rt_pos", [TN, 2, NT])
        keep = sb("rt_keep", [TN, 2, NT])
        place = sb("rt_place", [TN, 2, NT, CAP])
        named = sb("rt_named", [TN, 2, NT, EXPERTS])
        spread = sb("rt_spread", [TN, NT, EXPERTS])
        spread_t = sb("rt_spreadt", [EXPERTS, NT, TN])
        part = sb("rt_part", [TN, NT, D])
        ps = ctx.enter_context(nc.psum_tensor(f"rt_ps_{nc.next_id()}", [128, 8, 512], F32))
        turn_bank = (0, 1, 5)
        with stage(nc, "loaded", "own", "logits", "shifted", "exps", "hot_ready", "ranked", "named_ready", "tokens",
                   "spread_ready", "turned", "copied", "biased", "kept", "part_in", "both_in", "fetched") as (
                block, loaded, own_s, logits, shifted, exps, hot_ready, ranked, named_ready, tokens, spread_ready,
                turned, copied, biased, kept, part_in, both_in, fetched):
            @block.sync
            def _(sp):
                sp.dma_start(wr[:, :, :], wr_d).then_inc(loaded, 16)
                sp.dma_start(b2[:, :], b2_d).then_inc(loaded, 16)
                sp.dma_start(part[:, :, :], tiles_of(part_d)).then_inc(part_in, 16)
                prefetch(sp, fetched)

            @block.gpsimd
            def _(pool):
                pool.wait_ge(part_in, 16)
                for i in range(NT):
                    pool.tensor_tensor(acc[:, i, :], acc[:, i, :], part[:, i, :], ALU.add).then_inc(both_in, 1)
                    pool.wait_ge(both_in, i + 1)

            @block.tensor
            def _(pe):
                pe.wait_ge(loaded, 32)
                for i in range(NT):
                    for k in range(DC):
                        ins = pe.matmul(ps[0:TN, i // 8, EXPERTS * (i % 8):EXPERTS * (i % 8) + EXPERTS],
                                        xn_t[:, k, TN * i:TN * i + TN], wr[:, k, :], start=(k == 0), stop=(k == DC - 1))
                    ins.then_inc(logits, 1)
                pe.wait_ge(hot_ready, 1)
                for i in range(NT):
                    dst = ps[0:TN, 2 + i // 8, EXPERTS * (i % 8):EXPERTS * (i % 8) + EXPERTS]
                    for j in range(i):
                        pe.matmul(dst, c.ones[0:TN, 0:TN], both[:, j, :], start=(j == 0), stop=False)
                    pe.matmul(dst, c.lower[0:TN, 0:TN], both[:, i, :], start=(i == 0), stop=True).then_inc(ranked, 1)
                pe.wait_ge(named_ready, 1)
                for n in range(2 * NT):
                    ins = pe.matmul(ps[0:CAP, 4, 0:EXPERTS], place[:, n % 2, n // 2, :], named[:, n % 2, n // 2, :],
                                    start=(n == 0), stop=(n == 2 * NT - 1))
                ins.then_inc(tokens, 1)
                pe.wait_ge(spread_ready, 1)
                for i in range(NT):
                    ins = pe.transpose(ps[0:EXPERTS, turn_bank[i // 4], TN * (i % 4):TN * (i % 4) + TN], spread[:, i, :],
                                       c.ident[0:TN, 0:TN])
                    if i % 4 == 3 or i == NT - 1:
                        ins.then_inc(turned, 1)
                for i in range(NT):
                    pe.wait_ge(copied, i // 4 + 1)
                    if i >= 2:
                        pe.wait_ge(kept, i - 1)
                    pe.matmul(ps[0:TN, 6 + i % 2, :], spread_t[:, i, :], b2[:, :], start=True, stop=True).then_inc(biased, 1)

            @block.scalar
            def _(act):
                act.wait_ge(shifted, 1)
                act.activation(probs[:, :, :], logit[:, :, :], ACT.Exp).then_inc(exps, 1)
                for n in range(-(-NT // 4)):
                    m = min(4, NT - 4 * n)
                    act.wait_ge(turned, n + 1)
                    act.activation(spread_t[:, 4 * n:4 * n + m, :],
                                   ps[0:EXPERTS, turn_bank[n], 0:TN * m].rearrange("p (a b) -> p a b", b=TN), ACT.Copy)\
                        .then_inc(copied, 1)

            @block.vector
            def _(dve):
                own = Chain(dve, own_s)
                peak, total, inv, pair = (small[:, n, :] for n in range(4))
                bc = lambda a, n: a.unsqueeze(2).to_broadcast((TN, NT, n))
                dve.wait_ge(logits, NT)
                for i in range(0, NT, 8):
                    m = min(8, NT - i)
                    own.mark(dve.tensor_copy(logit[:, i:i + m, :], ps[0:TN, i // 8, 0:EXPERTS * m]
                                             .rearrange("p (a b) -> p a b", b=EXPERTS)))
                own.join()
                own.step(dve.tensor_reduce(peak, logit[:, :, :], AX, ALU.max))
                dve.tensor_tensor(logit[:, :, :], logit[:, :, :], bc(peak, EXPERTS), ALU.subtract).then_inc(shifted, 1)
                dve.wait_ge(exps, 1)
                own.step(dve.tensor_reduce(total, probs[:, :, :], AX, ALU.add))
                own.step(dve.reciprocal(inv, total))
                own.step(dve.tensor_tensor(probs[:, :, :], probs[:, :, :], bc(inv, EXPERTS), ALU.mult))
                for i in range(NT):
                    own.mark(dve.max(top[:, i, :], probs[:, i, :]))
                own.join()
                for i in range(NT):
                    own.mark(dve.max_index(idx[:, i, :], top[:, i, :], probs[:, i, :]))
                own.step(dve.tensor_tensor(pair, top[:, :, 0], top[:, :, 1], ALU.add))
                own.step(dve.reciprocal(pair, pair))
                for k in range(2):
                    own.mark(dve.tensor_copy(expert[:, k, :], idx[:, :, k]))
                    own.mark(dve.tensor_tensor(gate[:, k, :], top[:, :, k], pair, ALU.mult))
                own.join()
                count = lambda n: c.iota[0:TN, 0:n].unsqueeze(1).to_broadcast((TN, NT, n))
                for k in range(2):
                    own.mark(dve.tensor_tensor(hot[:, k, :, :], count(EXPERTS), bc(expert[:, k, :], EXPERTS), ALU.is_equal))
                own.join()
                dve.tensor_tensor(both[:, :, :], hot[:, 0, :, :], hot[:, 1, :, :], ALU.add).then_inc(hot_ready, 1)
                dve.wait_ge(ranked, NT)
                for i in range(0, NT, 8):
                    m = min(8, NT - i)
                    own.mark(dve.tensor_copy(before[:, i:i + m, :], ps[0:TN, 2 + i // 8, 0:EXPERTS * m]
                                             .rearrange("p (a b) -> p a b", b=EXPERTS)))
                own.join()
                for k in range(2):
                    own.step(dve.tensor_tensor(mine[:, :, :], before[:, :, :], hot[:, k, :, :], ALU.mult))
                    own.step(dve.tensor_reduce(pos[:, k, :], mine[:, :, :], AX, ALU.add))
                for k in range(2):
                    own.mark(dve.tensor_tensor(place[:, k, :, :], count(CAP), bc(pos[:, k, :], CAP), ALU.is_equal))
                    own.mark(dve.tensor_tensor(named[:, k, :, :], hot[:, k, :, :], bc(c.node[0:TN, :], EXPERTS), ALU.mult))
                own.join()
                dve.engine_nop().then_inc(named_ready, 1)
                own.step(dve.tensor_scalar(keep[:, :, :], pos[:, :, :], float(CAP), None, ALU.is_lt))
                own.mark(dve.tensor_tensor(gate[:, :, :], gate[:, :, :], keep[:, :, :], ALU.mult))
                own.step(dve.tensor_scalar(pos[:, :, :], pos[:, :, :], float(CAP - 1), None, ALU.min))
                own.step(dve.scalar_tensor_tensor(y_row[:, :, :], expert[:, :, :], float(CAP), pos[:, :, :],
                                                  ALU.mult, ALU.add))
                for k, dst in enumerate((spread, mine)):
                    own.mark(dve.tensor_tensor(dst[:, :, :], hot[:, k, :, :], bc(gate[:, k, :], EXPERTS), ALU.mult))
                own.join()
                dve.tensor_tensor(spread[:, :, :], spread[:, :, :], mine[:, :, :], ALU.add).then_inc(spread_ready, 1)
                dve.wait_ge(tokens, 1)
                own.mark(dve.tensor_copy(slot_tok[:, :], ps[0:CAP, 4, 0:EXPERTS]))
                for i in range(NT):
                    dve.wait_ge(both_in, i + 1)
                    dve.wait_ge(biased, i + 1)
                    dve.tensor_tensor(acc[:, i, :], acc[:, i, :], ps[0:TN, 6 + i % 2, :], ALU.add).then_inc(kept, 1)
                own.join()
                dve.wait_ge(kept, NT)


SLOTS = 8


def load_expert(sp, w1, w2, w1_d, w2_d, slot, e, sem):
    for dst, src in ((w1, w1_d), (w2, w2_d)):
        src = src.rearrange("e (k p) f -> p e k f", p=128)[:, bass.ds(e, 1), :, :].rearrange("p e k f -> p (e k) f")
        sp.dma_start(dst[:, slot, :, :], src).then_inc(sem, 16)


def prefetch_experts(sp, w1, w2, w1_d, w2_d, sem):
    for e in range(SLOTS):
        load_expert(sp, w1, w2, w1_d, w2_d, e, e, sem)
    sp.wait_ge(sem, 32 * SLOTS)


def run_experts(nc, c, z_d, slot_tok, w1, w2, w1_d, w2_d, y_d):
    TURN, XS = 32, 8
    MC = FF // 128
    with ExitStack() as ctx:
        sb = lambda name, shape, dt=F32: ctx.enter_context(nc.sbuf_tensor(f"{name}_{nc.next_id()}", shape, dt))
        ids = sb("mo_ids", [CAP, EXPERTS], I32)
        ids_now = sb("mo_idsnow", [CAP, TURN], I32)
        b1_now = sb("mo_b1", [128, TURN * MC])
        x = sb("mo_x", [CAP, XS, D])
        x_t = sb("mo_xt", [128, 2, DC, CAPW])
        h_t = sb("mo_ht", [128, 2, MC, CAPW])
        y = sb("mo_y", [CAP, 2, D])
        pt = ctx.enter_context(nc.psum_tensor(f"mo_pt_{nc.next_id()}", [128, 2, 512], F32))
        ph = ctx.enter_context(nc.psum_tensor(f"mo_ph_{nc.next_id()}", [128, 2, 512], F32))
        py = ctx.enter_context(nc.psum_tensor(f"mo_py_{nc.next_id()}", [128, 2, 512], F32))
        with stage(nc, "ready") as (block, ready):
            @block.vector
            def _(dve):
                dve.tensor_copy(ids[:, :], slot_tok[:, :]).then_inc(ready, 1)
                dve.memset(x_t[:, :, :, :], 0.0).then_inc(ready, 1)
                dve.wait_ge(ready, 2)

        def turn(g, last):
            with stage(nc, "now_ready", "turned", "xt_ready", "h_sum", "h_ready", "y_sum", "y_ready", "y0", "y1",
                       *(f"x{i}" for i in range(XS)), *(f"w{i}" for i in range(SLOTS))) as (
                    block, now_ready, turned, xt_ready, h_sum, h_ready, y_sum, y_ready, y0, y1, *more):
                stores, x_in, w_in = (y0, y1), more[:XS], more[XS:]
                loads = TURN - SLOTS if last else TURN

                @block.sync
                def _(sp):
                    for e in range(loads):
                        sp.wait_ge(y_sum, e + 1)
                        load_expert(sp, w1, w2, w1_d, w2_d, e % SLOTS, g * TURN + (e + SLOTS), w_in[e % SLOTS])
                    for s in range(SLOTS):
                        sp.wait_ge(w_in[s], 32 * (loads // SLOTS))

                @block.gpsimd
                def _(pool):
                    pool.wait_ge(now_ready, 1)
                    for e in range(TURN + XS):
                        if e < TURN:
                            if e >= XS:
                                pool.wait_ge(turned, e - XS + 1)
                            pool.indirect_dma_start(x[:, e % XS, :], None, z_d,
                                                    bass.IndirectOffsetOnAxis(ap=ids_now[:, e:e + 1], axis=0))\
                                .then_inc(x_in[e % XS], 16)
                        if e >= XS:
                            f = e - XS
                            pool.wait_ge(y_ready, f + 1)
                            pool.dma_start(y_d[bass.ds(g * TURN + f, 1), :, :].rearrange("e s d -> (e s) d"),
                                           y[:, f % 2, :]).then_inc(stores[f % 2], 16)
                    for s in stores:
                        pool.wait_ge(s, 16 * TURN // 2)

                @block.tensor
                def _(pe):
                    for e in range(TURN + 2):
                        if e < TURN:
                            pe.wait_ge(x_in[e % XS], 16 * (e // XS + 1))
                            if e >= 2:
                                pe.wait_ge(xt_ready, e - 1)
                            for k in range(DC):
                                ins = pe.transpose(pt[:, e % 2, 128 * k:128 * k + CAP], x[:, e % XS, 128 * k:128 * k + 128],
                                                   c.ident[0:CAP, 0:CAP])
                            ins.then_inc(turned, 1)
                        if 1 <= e <= TURN:
                            f = e - 1
                            if f >= SLOTS:
                                pe.wait_ge(w_in[f % SLOTS], 32 * (f // SLOTS))
                            pe.wait_ge(xt_ready, f + 1)
                            if f >= 2:
                                pe.wait_ge(h_ready, f - 1)
                            for m in range(MC):
                                for k in range(DC):
                                    ins = pe.matmul(ph[:, f % 2, 128 * m:128 * m + CAPW],
                                                    w1[:, f % SLOTS, k, 128 * m:128 * m + 128],
                                                    x_t[:, f % 2, k, :], start=(k == 0), stop=(k == DC - 1))
                            ins.then_inc(h_sum, 1)
                        if e >= 2:
                            f = e - 2
                            pe.wait_ge(h_ready, f + 1)
                            if f >= 2:
                                pe.wait_ge(y_ready, f - 1)
                            for m in range(MC):
                                ins = pe.matmul(py[0:CAP, f % 2, :], h_t[:, f % 2, m, 0:CAP],
                                                w2[:, f % SLOTS, m, :], start=(m == 0), stop=(m == MC - 1))
                            ins.then_inc(y_sum, 1)

                @block.scalar
                def _(act):
                    act.wait_ge(now_ready, 2)
                    for e in range(TURN + 1):
                        if e < TURN:
                            act.wait_ge(turned, e + 1)
                            if e >= 2:
                                act.wait_ge(h_sum, e - 1)
                            for k in range(DC):
                                ins = act.activation(x_t[:, e % 2, k, 0:CAP], pt[:, e % 2, 128 * k:128 * k + CAP], ACT.Identity,
                                                     bias=c.pcol[:, PCOL["ln2_b"]][:, k:k + 1],
                                                     scale=c.pcol[:, PCOL["ln2_g"]][:, k:k + 1])
                            ins.then_inc(xt_ready, 1)
                        if e >= 1:
                            f = e - 1
                            act.wait_ge(h_sum, f + 1)
                            if f >= 2:
                                act.wait_ge(y_sum, f - 1)
                            for m in range(MC):
                                ins = act.activation(h_t[:, f % 2, m, :], ph[:, f % 2, 128 * m:128 * m + CAPW],
                                                     ACT.Gelu_apprx_tanh, bias=b1_now[:, MC * f + m:MC * f + m + 1])
                            ins.then_inc(h_ready, 1)

                @block.vector
                def _(dve):
                    dve.tensor_copy(ids_now[:, :], ids[:, bass.ds(g * TURN, TURN)]).then_inc(now_ready, 1)
                    dve.tensor_copy(b1_now[:, :], c.pcol[:, PCOL["moe_b1"]][:, bass.ds(g * (TURN * MC), TURN * MC)])\
                        .then_inc(now_ready, 1)
                    for f in range(TURN):
                        dve.wait_ge(y_sum, f + 1)
                        if f >= 2:
                            dve.wait_ge(stores[f % 2], 16 * (f // 2))
                        dve.tensor_copy(y[:, f % 2, :], py[0:CAP, f % 2, :]).then_inc(y_ready, 1)

        with nc.Fori(0, EXPERTS // TURN - 1) as g:
            turn(g, False)
        turn(EXPERTS // TURN - 1, True)


def combine_experts(nc, c, y_d, y_row, gate, acc):
    with ExitStack() as ctx:
        sb = lambda name, shape, dt=F32: ctx.enter_context(nc.sbuf_tensor(f"{name}_{nc.next_id()}", shape, dt))
        ids = sb("cb_ids", [TN, 2, NT], I32)
        got = sb("cb_got", [TN, NT, 2, D])
        rows = y_d.rearrange("e s d -> (e s) d")
        with stage(nc, "ready", "added", *(f"got{i}" for i in range(NT))) as (block, ready, added, *got_s):
            @block.gpsimd
            def _(pool):
                pool.wait_ge(ready, 1)
                for i in range(NT):
                    for k in range(2):
                        pool.indirect_dma_start(got[:, i, k, :], None, rows,
                                                bass.IndirectOffsetOnAxis(ap=ids[:, k, i:i + 1], axis=0))\
                            .then_inc(got_s[i], 16)

            @block.vector
            def _(dve):
                dve.tensor_copy(ids[:, :, :], y_row[:, :, :]).then_inc(ready, 1)
                steps = [(0, 0)]
                for i in range(NT):
                    steps += ([(i + 1, 0)] if i + 1 < NT else []) + [(i, 1)]
                done = {}
                for n, (i, k) in enumerate(steps):
                    if k == 0:
                        dve.wait_ge(got_s[i], 32)
                    else:
                        dve.wait_ge(added, done[i, 0])
                    dve.scalar_tensor_tensor(acc[:, i, :], got[:, i, k, :], gate[:, k, i:i + 1], acc[:, i, :],
                                             ALU.mult, ALU.add).then_inc(added, 1)
                    done[i, k] = n + 1
                dve.wait_ge(added, 2 * NT)


def edge_mlp(nc, c, table_d, w_d, h_d):
    HG = GE // 2
    W = HG * TE
    HW = W // 2
    with ExitStack() as ctx:
        sb = lambda name, shape, dt=F32: ctx.enter_context(nc.sbuf_tensor(f"{name}_{nc.next_id()}", shape, dt))
        edges = sb("em_edges", [128, NS, ROW])
        attr = sb("em_attr", [128, NS, 8])
        w1 = sb("em_w1", [GE * 8, HG, 128])
        w23 = sb("em_w23", [128, 2, 128])
        a_t = sb("em_at", [GE * 8, 2, TE])
        h = sb("em_h", [128, 3, 2, W])
        ps = ctx.enter_context(nc.psum_tensor(f"em_ps_{nc.next_id()}", [128, 8, 512], F32))
        with stage(nc, "zeroed", "loaded", "wts", "packed") as (block, zeroed, loaded, wts, packed):
            @block.vector
            def _(dve):
                dve.memset(w1[:, :, :], 0.0).then_inc(zeroed, 1)
                dve.memset(w23[:, :, :], 0.0).then_inc(zeroed, 1)
                dve.wait_ge(loaded, 16)
                dve.tensor_copy(attr[:, :, :], edges[:, :, 8:16]).then_inc(packed, 1)
                dve.wait_ge(packed, 1)

            @block.sync
            def _(sp):
                sp.dma_start(edges[:, :, :], table_d.rearrange("(p t) c -> p t c", p=128)).then_inc(loaded, 16)
                sp.wait_ge(zeroed, 2)
                for i in range(HG):
                    sp.dma_start(w1[8 * i:8 * i + 8, i, 0:64], w_d[0]).then_inc(wts, 16)
                    sp.dma_start(w1[8 * (i + HG):8 * (i + HG) + 8, i, 64:128], w_d[0]).then_inc(wts, 16)
                for n in range(2):
                    sp.dma_start(w23[0:64, n, 0:64], w_d[1 + n]).then_inc(wts, 16)
                    sp.dma_start(w23[64:128, n, 64:128], w_d[1 + n]).then_inc(wts, 16)
                sp.wait_ge(wts, 16 * (2 * HG + 4))
        with stage(nc, "turned", "copied", "s1", "s2", "s3", "a1", "a2", "a3", "st0", "st1") as (
                block, turned, copied, s1, s2, s3, a1, a2, a3, st0, st1):
            s, a, st = (s1, s2, s3), (a1, a2, a3), (st0, st1)
            @block.tensor
            def _(pe):
                for g in range(GROUPS + 3):
                    if g < GROUPS:
                        if g >= 2:
                            pe.wait_ge(copied, g - 1)
                        pe.transpose(ps[0:GE * 8, 6 + g % 2, 0:TE], attr[:, g * GE:(g + 1) * GE, :]
                                     .rearrange("p t c -> p (t c)"), c.ident[:, :]).then_inc(turned, 1)
                    for layer in range(3):
                        t = g - 1 - layer
                        if not 0 <= t < GROUPS:
                            continue
                        if layer == 0:
                            pe.wait_ge(copied, t + 1)
                        else:
                            pe.wait_ge(a[layer - 1], 2 * (t + 1))
                        if t >= 1:
                            pe.wait_ge(a[layer], 2 * t)
                        for half in range(2):
                            dst = ps[:, 2 * layer + half, :]
                            if layer == 0:
                                for i in range(HG):
                                    lo, hi = max(i * TE, half * HW), min((i + 1) * TE, (half + 1) * HW)
                                    if lo < hi:
                                        ins = pe.matmul(dst[:, lo - half * HW:hi - half * HW], w1[:, i, :],
                                                        a_t[:, t % 2, lo - i * TE:hi - i * TE], start=True, stop=True)
                            else:
                                ins = pe.matmul(dst[:, 0:HW], w23[:, layer - 1, :],
                                                h[:, layer - 1, t % 2, half * HW:(half + 1) * HW], start=True, stop=True)
                            ins.then_inc(s[layer], 1)

            @block.vector
            def _(dve):
                for g in range(GROUPS):
                    dve.wait_ge(turned, g + 1)
                    if g >= 2:
                        dve.wait_ge(s1, 2 * (g - 1))
                    dve.tensor_copy(a_t[:, g % 2, :], ps[0:GE * 8, 6 + g % 2, 0:TE]).then_inc(copied, 1)

            @block.scalar
            def _(act):
                for g in range(GROUPS + 3):
                    for layer in range(3):
                        t = g - 1 - layer
                        if not 0 <= t < GROUPS:
                            continue
                        if t >= 2:
                            if layer < 2:
                                act.wait_ge(s[layer + 1], 2 * (t - 1))
                            else:
                                act.wait_ge(st[t % 2], 16 * (t // 2))
                        for half in range(2):
                            act.wait_ge(s[layer], 2 * t + half + 1)
                            act.activation(h[:, layer, t % 2, half * HW:(half + 1) * HW],
                                           ps[:, 2 * layer + half, 0:HW], ACT.Silu,
                                           scale=(8 ** -0.5, SILU_GAIN / 8, SILU_GAIN / 8)[layer]).then_inc(a[layer], 1)

            @block.sync
            def _(sp):
                for g in range(GROUPS):
                    sp.wait_ge(a3, 2 * (g + 1))
                    sp.dma_start(h_d[g, :, :], h[:, 2, g % 2, :]).then_inc(st[g % 2], 16)
                for x in st:
                    sp.wait_ge(x, 16 * GROUPS // 2)


def up_project(nc, c, x_t, up_d, out_d):
    with ExitStack() as ctx:
        sb = lambda name, shape, dt=F32: ctx.enter_context(nc.sbuf_tensor(f"{name}_{nc.next_id()}", shape, dt))
        up = sb("up_w", [128, 2, 128])
        y = sb("up_y", [TN, NT, D])
        ps = ctx.enter_context(nc.psum_tensor(f"up_ps_{nc.next_id()}", [128, 4, 512], F32))
        with stage(nc, "loaded", "summed", "copied", "stored") as (block, loaded, summed, copied, stored):
            @block.sync
            def _(sp):
                for n in range(2):
                    sp.dma_start(up[:, n, :], up_d[n]).then_inc(loaded, 16)
                for i in range(NT):
                    sp.wait_ge(copied, i + 1)
                    sp.dma_start(tiles_of(out_d)[:, i, :], y[:, i, :]).then_inc(stored, 16)
                sp.wait_ge(stored, 16 * NT)

            @block.tensor
            def _(pe):
                pe.wait_ge(loaded, 32)
                for i in range(NT):
                    if i >= 4:
                        pe.wait_ge(copied, i - 3)
                    for k in range(4):
                        ins = pe.matmul(ps[0:TN, i % 4, 128 * k:128 * k + 128], x_t[:, k, TN * i:TN * i + TN],
                                        up[:, min(k, 1), :], start=True, stop=True)
                    ins.then_inc(summed, 1)

            @block.scalar
            def _(act):
                for i in range(NT):
                    act.wait_ge(summed, i + 1)
                    act.activation(y[:, i, :], ps[0:TN, i % 4, :], ACT.Copy, scale=128 ** -0.5).then_inc(copied, 1)


def graph_sum1(nc, c, table_d, tile_base, nodes_d, h_d, w4_d, out0_d, out1_d, x):
    HG = GE // 2
    with ExitStack() as ctx:
        sb = lambda name, shape, dt=F32: ctx.enter_context(nc.sbuf_tensor(f"{name}_{nc.next_id()}", shape, dt))
        acc = sb("g1_acc", [TN, NT, 2 * D])
        w4 = sb("g1_w4", [128, 2, D])
        wo = sb("g1_wo", [128, 2, 2, 128])
        with ExitStack() as inner:
            sb2 = lambda name, shape, dt=F32: inner.enter_context(nc.sbuf_tensor(f"{name}_{nc.next_id()}", shape, dt))
            edges = sb2("g1_edges", [128, GL, ROW])
            h = sb2("g1_h", [128, GL // GE, HG * TE])
            got = sb2("g1_got", [128, RING, D])
            hot = sb2("g1_hot", [128, 3, 2, TN])
            w = sb2("g1_w", [128, 3, D])
            dot = sb2("g1_dot", [128, 3, 128])
            both = sb2("g1_both", [128, 3, 128])
            msg = sb2("g1_msg", [128, 3, 2 * D])
            pw = inner.enter_context(nc.psum_tensor(f"g1_pw_{nc.next_id()}", [128, 2, 512], F32))
            pm = inner.enter_context(nc.psum_tensor(f"g1_pm_{nc.next_id()}", [128, 4, 512], F32))
            with stage(nc, "loaded", "own", "rest_zero") as (block, loaded, own_s, rest_zero):
                @block.vector
                def _(dve):
                    dve.memset(w4[:, :, :], 0.0).then_inc(own_s, 1)
                    dve.memset(acc[:, 0:6, :], 0.0).then_inc(own_s, 1)
                    dve.wait_ge(own_s, 2)

                @block.gpsimd
                def _(pool):
                    pool.memset(acc[:, 6:NT, :], 0.0).then_inc(rest_zero, 1)
                    pool.wait_ge(rest_zero, 1)

                @block.sync
                def _(sp):
                    for n in range(2):
                        sp.dma_start(wo[:, 0, n, :], out0_d[128 * n:128 * n + 128, :]).then_inc(loaded, 16)
                        sp.dma_start(wo[:, 1, n, :], out1_d[128 * n:128 * n + 128, :]).then_inc(loaded, 16)
                    sp.wait_ge(own_s, 1)
                    sp.dma_start(w4[0:64, 0, :], w4_d).then_inc(loaded, 16)
                    sp.dma_start(w4[64:128, 1, :], w4_d).then_inc(loaded, 16)
                    sp.wait_ge(loaded, 96)
            table = table_d.rearrange("(p t) c -> p t c", p=128)
            with nc.Fori(0, TURNS) as g:
                with stage(nc, "loaded", "h_in", "hot_ready", "plain_hot", "weighed", "w_copied", "bp_ready", "dp_ready", "msg_v",
                           "msg_a", "msg_p", "own", "summed", "added", *(f"got{i}" for i in range(RING))) as (
                        block, loaded, h_in, hot_ready, plain_hot, weighed, w_copied, bp_ready, dp_ready, msg_v, msg_a, msg_p,
                        own_s, summed, added, *got_s):
                    def got_wait(eng, i):
                        eng.wait_ge(got_s[i % RING], 16 * (i // RING + 1))

                    @block.sync
                    def _(sp):
                        sp.dma_start(edges[:, :, :], table[:, bass.ds(g * GL, GL), :]).then_inc(loaded, 16)
                        sp.dma_start(h[:, :, :], h_d[bass.ds(g * (GL // GE), GL // GE), :, :]
                                     .rearrange("g p n -> p g n")).then_inc(h_in, 16)
                        sp.wait_ge(loaded, 16)
                        sp.wait_ge(h_in, 16)

                    @block.gpsimd
                    def _(pool):
                        pool.wait_ge(loaded, 16)
                        ids = edges[:, :, :].bitcast(I32)
                        for i in range(GL + RING - 2):
                            if i < GL:
                                if i >= RING:
                                    pool.wait_ge(msg_v, i - RING + 1)
                                    pool.wait_ge(msg_p, i - RING + 1)
                                pool.indirect_dma_start(got[:, i % RING, :], None, nodes_d,
                                                        bass.IndirectOffsetOnAxis(ap=ids[:, i, 0:1], axis=0))\
                                    .then_inc(got_s[i % RING], 16)
                            if i >= RING - 2:
                                t = i - RING + 2
                                if t >= 3:
                                    pool.wait_ge(summed, t - 2)
                                pool.wait_ge(w_copied, t + 1)
                                got_wait(pool, t)
                                pool.tensor_tensor(
                                    msg[:, t % 3, 128:512].rearrange("p (m u) -> p m u", m=3),
                                    w[:, t % 3, 256:384].unsqueeze(1).to_broadcast((128, 3, 128)),
                                    got[:, t % RING, 128:512].rearrange("p (m u) -> p m u", m=3),
                                    ALU.mult).then_inc(msg_p, 1)

                    @block.tensor
                    def _(pe):
                        pe.wait_ge(h_in, 16)
                        for i in range(GL + 2):
                            if i < GL:
                                if i >= 2:
                                    pe.wait_ge(w_copied, i - 1)
                                r = i % GE
                                col = TE * (r % HG)
                                pe.matmul(pw[:, i % 2, :], h[:, i // GE, col:col + TE], w4[:, r // HG, :],
                                          start=True, stop=True).then_inc(weighed, 1)
                            if i >= 2:
                                t = i - 2
                                pe.wait_ge(hot_ready, t + 1)
                                pe.wait_ge(msg_v, t + 1)
                                pe.wait_ge(msg_a, t + 1)
                                pe.wait_ge(msg_p, t + 1)
                                if t >= 2:
                                    pe.wait_ge(added, t - 1)
                                for n in range(2):
                                    ins = pe.matmul(pm[0:TN, 2 * (t % 2) + n, :], hot[:, t % 3, n, :],
                                                    msg[:, t % 3, 512 * n:512 * n + 512], start=True, stop=True)
                                ins.then_inc(summed, 1)

                    @block.scalar
                    def _(act):
                        act.wait_ge(loaded, 16)
                        for i in range(GL + 1):
                            if i < GL:
                                if i >= 3:
                                    act.wait_ge(msg_v, i - 2)
                                    act.wait_ge(msg_p, i - 2)
                                got_wait(act, i)
                                act.activation(dot[:, i % 3, :], got[:, i % RING, 128:256], ACT.Copy,
                                               scale=edges[:, i, 5:6]).then_inc(dp_ready, 1)
                                act.wait_ge(weighed, i + 1)
                                act.activation(w[:, i % 3, :], pw[:, i % 2, :], ACT.Copy).then_inc(w_copied, 1)
                                act.wait_ge(plain_hot, i + 1)
                                act.activation(hot[:, i % 3, 0, :], hot[:, i % 3, 1, :], ACT.Copy,
                                               scale=edges[:, i, 4:5]).then_inc(hot_ready, 1)
                            if i >= 1:
                                t = i - 1
                                act.wait_ge(bp_ready, t + 1)
                                if t >= 3:
                                    act.wait_ge(summed, t - 2)
                                for m in range(3):
                                    ins = act.activation(msg[:, t % 3, 640 + 128 * m:768 + 128 * m], both[:, t % 3, :],
                                                         ACT.Copy, scale=edges[:, t, 5 + m:6 + m])
                                ins.then_inc(msg_a, 1)

                    @block.vector
                    def _(dve):
                        own = Chain(dve, own_s)
                        dve.wait_ge(loaded, 16)

                        def add(t, n):
                            if n == 0:
                                dve.wait_ge(summed, t + 1)
                                if t:
                                    dve.wait_ge(added, t)
                            dst = acc[:, bass.ds(at[0], 1), 512 * n:512 * n + 512].rearrange("p a b -> p (a b)")
                            ins = dve.tensor_tensor(dst, dst, pm[0:TN, 2 * (t % 2) + n, :], ALU.add)
                            if n == 1:
                                ins.then_inc(added, 1)

                        at = [None]
                        for i in range(GL + 3):
                            t = i - 3
                            if t >= 0:
                                at[0] = dve.value_load(tile_base[0:1, bass.ds(g * GL + t, 1)], min_val=0, max_val=NT - 1)
                            if i < GL:
                                s0 = got[:, i % RING, 0:128]
                                if i >= 3:
                                    dve.wait_ge(summed, i - 2)
                                dve.tensor_scalar(hot[:, i % 3, 1, :], c.iota[:, 0:TN], edges[:, i, 1:2], None,
                                                  ALU.is_equal).then_inc(plain_hot, 1)
                                got_wait(dve, i)
                                dve.wait_ge(dp_ready, i + 1)
                                own.mark(dve.scalar_tensor_tensor(dot[:, i % 3, :], got[:, i % RING, 256:384],
                                                                  edges[:, i, 6:7], dot[:, i % 3, :], ALU.mult, ALU.add))
                                dve.wait_ge(w_copied, i + 1)
                                if i >= 3:
                                    dve.wait_ge(msg_a, i - 2)
                                dve.tensor_tensor(both[:, i % 3, :], w[:, i % 3, 128:256], s0, ALU.mult).then_inc(bp_ready, 1)
                                own.mark(dve.tensor_tensor(msg[:, i % 3, 0:128], w[:, i % 3, 0:128], s0, ALU.mult))
                            if t >= 0:
                                add(t, 0)
                            if i < GL:
                                own.join()
                                own.mark(dve.scalar_tensor_tensor(dot[:, i % 3, :], got[:, i % RING, 384:512],
                                                                  edges[:, i, 7:8], dot[:, i % 3, :], ALU.mult, ALU.add))
                            if t >= 0:
                                add(t, 1)
                            if i < GL:
                                own.join()
                                dve.tensor_tensor(msg[:, i % 3, 512:640], w[:, i % 3, 384:512], dot[:, i % 3, :],
                                                  ALU.mult).then_inc(msg_v, 1)
                        dve.wait_ge(added, GL)
        acc_t = sb("g1_acct", [128, 2, 8, TN])
        p8 = ctx.enter_context(nc.psum_tensor(f"g1_pt_{nc.next_id()}", [128, 4, 512], F32))
        po = ctx.enter_context(nc.psum_tensor(f"g1_po_{nc.next_id()}", [128, 2, 512], F32))
        gain = SILU_GAIN / 8 / 16 / 10
        with stage(nc, "turned", "copied", "summed", "left", "added") as (block, turned, copied, summed, left, added):
            @block.tensor
            def _(pe):
                for i in range(NT + 1):
                    if i < NT:
                        if i >= 2:
                            pe.wait_ge(copied, i - 1)
                        for k in range(8):
                            ins = pe.transpose(p8[:, 2 * (i % 2) + k // 4, TN * (k % 4):TN * (k % 4) + TN],
                                               acc[:, i, 128 * k:128 * k + 128], c.ident[0:TN, 0:TN])
                        ins.then_inc(turned, 1)
                    if i >= 1:
                        t = i - 1
                        pe.wait_ge(copied, t + 1)
                        if t >= 2:
                            pe.wait_ge(left, t - 1)
                            pe.wait_ge(added, t - 1)
                        for o, (a, b) in enumerate(((0, 4), (5, 1), (6, 2), (7, 3))):
                            for n, k in enumerate((a, b)):
                                ins = pe.matmul(po[0:TN, t % 2, 128 * o:128 * o + 128], acc_t[:, t % 2, k, :],
                                                wo[:, min(o, 1), n, :], start=(n == 0), stop=(n == 1))
                        ins.then_inc(summed, 1)

            @block.scalar
            def _(act):
                for i in range(NT):
                    act.wait_ge(turned, i + 1)
                    if i >= 2:
                        act.wait_ge(summed, i - 1)
                    for k in range(8):
                        ins = act.activation(acc_t[:, i % 2, k, :], p8[:, 2 * (i % 2) + k // 4, TN * (k % 4):TN * (k % 4) + TN],
                                             ACT.Copy, scale=gain * (3 ** -0.5 if k == 4 else 1.0))
                    ins.then_inc(copied, 1)

            @block.vector
            def _(dve):
                for i in range(NT):
                    dve.wait_ge(summed, i + 1)
                    dve.tensor_tensor(x[:, i, 0:128], x[:, i, 0:128], po[0:TN, i % 2, 0:128], ALU.add).then_inc(left, 1)
                    xm = x[:, i, 128:512].rearrange("p (v m) -> p m v", m=3)
                    dve.tensor_tensor(xm, xm, po[0:TN, i % 2, 128:512].rearrange("p (m v) -> p m v", m=3),
                                      ALU.add).then_inc(added, 1)
                dve.wait_ge(left, NT)
                dve.wait_ge(added, NT)


def pick_experts(nc, c, x_d, w1_d, w2_d, b2_d, picked):
    with ExitStack() as ctx:
        sb = lambda name, shape, dt=F32: ctx.enter_context(nc.sbuf_tensor(f"{name}_{nc.next_id()}", shape, dt))
        x = sb("ro_x", [TN, NT, D])
        w1 = sb("ro_w1", [128, DC, 128])
        w2 = sb("ro_w2", [128, 8])
        b2 = sb("ro_b2", [1, 8])
        pooled = sb("ro_pool", [128, DC])
        hid = sb("ro_h", [128, 1])
        row = sb("ro_row", [1, 4, 8])
        top = sb("ro_top", [1, 2, 8])
        idx = sb("ro_idx", [1, 2, 8], U32)
        pad = sb("ro_pad", [1, 2, 8])
        ps = ctx.enter_context(nc.psum_tensor(f"ro_ps_{nc.next_id()}", [128, 3, 512], F32))
        with stage(nc, "loaded", "own", "pool_sum", "pool_ready", "h_sum", "h_ready", "l_sum", "shifted", "exps") as (
                block, loaded, own_s, pool_sum, pool_ready, h_sum, h_ready, l_sum, shifted, exps):
            @block.sync
            def _(sp):
                sp.dma_start(x[:, :, :], tiles_of(x_d)).then_inc(loaded, 16)
                sp.dma_start(w1[:, :, :], w1_d).then_inc(loaded, 16)
                sp.dma_start(w2[:, :], w2_d).then_inc(loaded, 16)
                sp.dma_start(b2[:, :], b2_d).then_inc(loaded, 16)

            @block.tensor
            def _(pe):
                pe.wait_ge(loaded, 64)
                for k in range(DC):
                    for i in range(NT):
                        ins = pe.matmul(ps[:, 0, k:k + 1], x[:, i, 128 * k:128 * k + 128], c.mean_col[0:TN, :],
                                        start=(i == 0), stop=(i == NT - 1))
                ins.then_inc(pool_sum, 1)
                pe.wait_ge(pool_ready, 1)
                for k in range(DC):
                    ins = pe.matmul(ps[:, 1, 0:1], w1[:, k, :], pooled[:, k:k + 1], start=(k == 0), stop=(k == DC - 1))
                ins.then_inc(h_sum, 1)
                pe.wait_ge(h_ready, 1)
                pe.matmul(ps[0:1, 2, 0:8], hid[:, :], w2[:, :], start=True, stop=True).then_inc(l_sum, 1)

            @block.scalar
            def _(act):
                act.wait_ge(h_sum, 1)
                act.activation(hid[:, :], ps[:, 1, 0:1], ACT.Gelu, bias=c.pcol[:, PCOL["rt_b1"]]).then_inc(h_ready, 1)
                act.wait_ge(shifted, 1)
                act.activation(row[:, 1, :], row[:, 0, :], ACT.Exp).then_inc(exps, 1)

            @block.vector
            def _(dve):
                own = Chain(dve, own_s)
                own.mark(dve.memset(pad[:, :, :], -1.0))
                dve.wait_ge(pool_sum, 1)
                dve.tensor_copy(pooled[:, :], ps[:, 0, 0:DC]).then_inc(pool_ready, 1)
                dve.wait_ge(l_sum, 1)
                dve.wait_ge(loaded, 64)
                own.step(dve.tensor_tensor(row[:, 2, :], ps[0:1, 2, 0:8], b2[:, :], ALU.add))
                own.step(dve.tensor_reduce(row[:, 3, 0:1], row[:, 2, :], AX, ALU.max))
                dve.tensor_scalar(row[:, 0, :], row[:, 2, :], row[:, 3, 0:1], None, ALU.subtract).then_inc(shifted, 1)
                dve.wait_ge(exps, 1)
                own.step(dve.tensor_reduce(row[:, 3, 1:2], row[:, 1, :], AX, ALU.add))
                own.step(dve.reciprocal(row[:, 3, 2:3], row[:, 3, 1:2]))
                for n in range(2):
                    own.mark(dve.tensor_scalar(pad[:, n, 0:4], row[:, 1, 4 * n:4 * n + 4], row[:, 3, 2:3], None, ALU.mult))
                own.join()
                for n in range(2):
                    own.mark(dve.max(top[:, n, :], pad[:, n, :]))
                own.join()
                for n in range(2):
                    own.mark(dve.max_index(idx[:, n, :], top[:, n, :], pad[:, n, :]))
                own.join()
                own.step(dve.tensor_copy(picked[:, :], idx[:, :, 0]))


def program(nc, a, out):
    dram = lambda name, shape, dt=F32: nc.dram_tensor(name, shape, dt, kind="Internal").ap()
    rows = lambda name: dram(name, [N, D])
    kview = lambda w: w.rearrange("(k p) o -> p k o", p=128)
    c = Core()
    with ExitStack() as ctx:
        sb = lambda name, shape, dt=F32: ctx.enter_context(nc.sbuf_tensor(name, shape, dt))
        c.pcol_d = a["pcol"]
        c.pcol = sb("pcol", [128, NPCOL])
        c.ident = sb("ident", [128, 128])
        c.lower = sb("lower", [128, 128], BF16)
        c.ones = sb("ones", [128, 128], BF16)
        c.causal = sb("causal", [TN, 2 * TN])
        c.mean_col = sb("mean_col", [128, 1])
        c.iota_i = sb("iota_i", [128, 256], I32)
        c.node_i = sb("node_i", [128, NT], I32)
        c.iota = sb("iota", [128, 256])
        c.node = sb("node", [128, NT])
        base0 = sb("base0", [1, NS], I32)
        base1 = sb("base1", [1, NS], I32)
        picked = sb("picked", [1, 2], I32)
        col = lambda n: c.pcol[:, PCOL[n]]
        make_constants(nc, c)

        table0, table1 = dram("table0", [128 * NS, ROW]), dram("table1", [128 * NS, ROW])
        x_sb = sb("x_sb", [TN, NT, D])
        place = lambda key, other, *to, **more: place_edges(
            nc, c, a[key], a[other], a["edge_weight"], a["edge_attr_4"], a["edge_attr_8"], *to, **more)
        support, x1, xa, z2 = (rows(n) for n in ("support", "x1", "xa", "z2"))
        y_moe = dram("y_moe", [EXPERTS, CAP, D])
        with ExitStack() as layer0:
            s0 = lambda name, shape, dt=F32: layer0.enter_context(nc.sbuf_tensor(name, shape, dt))
            rows1, slots1 = s0("rows1", [TN, EC, ROW]), s0("slots1", [TN, EC], I32)
            with nc.sbuf_tensor("rows0", [TN, EC, ROW], F32) as rows0, nc.sbuf_tensor("slots0", [TN, EC], I32) as slots0:
                send0 = (table0, rows0, slots0)
                place("src", "dst", table0, base0, rows0, slots0)
                place("dst", "src", table1, base1, rows1, slots1, send=send0, columns=range(0, 36))
                with nc.sbuf_tensor("n0_t", [128, DC, N], F32) as n_t:
                    normalize(nc, c, a["x"], targets=[(n_t, None, None)], send=send0, columns=range(36, 80))
                    project_tokens(nc, c, n_t, DC, kview(a["L0_gnn_weight"]), support, send=send0, columns=range(80, 121))
                graph_sum0(nc, c, table0, base0, support, a["x"], a["L0_gnn_bias"], x_sb, send0, range(121, EC))

            s_t = s0("s0_t", [128, DC, N])
            with nc.sbuf_tensor("o0_t", [128, DC, N], F32) as o_t:
                normalize(nc, c, x1, x=x_sb, first_out=xa, double=True, targets=[(s_t, col("ln1_g"), col("ln1_b"))])
                pairs = [lambda e, j, w=a[f"L0_ffn_w{n}"]: kview(w)[:, :, bass.ds(j * 128, 128)] for n in "qkv"]
                attention(nc, c, s_t, s_t, o_t, *pairs, None, None, None, send=(table1, rows1, slots1))
                project_tokens(nc, c, o_t, DC, kview(a["L0_ffn_wo"]), None, residuals=[xa], y=x_sb)
            normalize(nc, c, None, x=x_sb, last_out=z2, targets=[(s_t, col("ln2_g"), col("ln2_b"))])
            slot_tok = s0("slot_tok", [CAP, EXPERTS])
            y_row, gate = s0("y_row", [TN, 2, NT]), s0("gate", [TN, 2, NT])
            ring = s0("w1_ring", [128, SLOTS, DC, FF]), s0("w2_ring", [128, SLOTS, FF // 128, D])
            experts = (*ring, a["L0_ffn_w1"], a["L0_ffn_w2"])
            route_tokens(nc, c, s_t, kview(a["L0_ffn_wr"]), a["L0_ffn_b2"], slot_tok, y_row, gate, x1, x_sb,
                         lambda sp, sem: prefetch_experts(sp, *experts, sem))
            run_experts(nc, c, z2, slot_tok, *experts, y_moe)
            combine_experts(nc, c, y_moe, y_row, gate, x_sb)

        nodes, x4 = rows("nodes"), rows("x4")
        h_d = dram("h_edges", [GROUPS, 128, GE // 2 * TE])
        with nc.sbuf_tensor("n1_t", [128, DC, N], F32) as n_t:
            normalize(nc, c, None, x=x_sb, targets=[(n_t, None, None)],
                      column=lambda k: slice(0, 128) if k == 0 else slice(128 + k - 1, 512, 3))
            up_project(nc, c, n_t, [a["L1_gnn_W_up0"], a["L1_gnn_W_up1"]], nodes)
        edge_mlp(nc, c, table1, [a[f"L1_gnn_W_mlp{n}"] for n in (1, 2, 3)], h_d)
        graph_sum1(nc, c, table1, base1, nodes, h_d, a["L1_gnn_W_mlp4"], a["L1_gnn_W_out0"], a["L1_gnn_W_out1"], x_sb)

        xc, x5 = rows("xc"), rows("x5")
        with ExitStack() as acts:
            sa = lambda name: acts.enter_context(nc.sbuf_tensor(name, [128, DC, N], F32))
            with ExitStack() as mid:
                s_t = sa("s1_t")
                t_t, o_t = (mid.enter_context(nc.sbuf_tensor(n, [128, DC, N], F32)) for n in ("t1_t", "o1_t"))
                normalize(nc, c, x4, x=x_sb, first_out=xc, double=True,
                          targets=[(s_t, col("ns_w"), col("ns_b")), (t_t, col("nt_w"), col("nt_b"))])
                pick_experts(nc, c, xc, kview(a["router_w1"]), a["router_w2"], a["router_b2"], picked)
                spatial, temporal = picked[0:1, 0:1], picked[0:1, 1:2]

                ek = lambda w, e: w[bass.ds(e, 1), :, :].rearrange("e (k p) o -> p (e k) o", p=128)
                wpair = lambda w, n=0: (lambda e, j: ek(w, e)[:, :, bass.ds(j * 128 + D * n, 128)])
                bcol = lambda b, n=0: (lambda e: b[bass.ds(e, 1), :, DC * n:DC * n + DC].rearrange("e p c -> (e p) c"))
                all_w = lambda w: (lambda e: ek(w, e))
                all_b = lambda b: (lambda e: b[bass.ds(e, 1), :, :].rearrange("e p c -> (e p) c"))
                attention(nc, c, t_t, t_t, o_t, wpair(a["tq_w"]), wpair(a["tk_w"]), wpair(a["tv_w"]),
                          bcol(a["tq_bcol"]), bcol(a["tk_bcol"]), bcol(a["tv_bcol"]), causal=True, pick=temporal)
                project_features(nc, c, o_t, all_w(a["tp_w"]), all_b(a["tp_b"]), DC, t_t, residual_t=t_t, pick=temporal)
                sw, sbr = a["sp_in_w"], a["sp_in_bcol"]
                attention(nc, c, s_t, s_t, o_t, wpair(sw, 0), wpair(sw, 1), wpair(sw, 2),
                          bcol(sbr, 0), bcol(sbr, 1), bcol(sbr, 2), pick=spatial)
                project_features(nc, c, o_t, all_w(a["sp_out_w"]), all_b(a["sp_out_b"]), DC, s_t, pick=spatial)
                cw, cbr = a["cross_in_w"], a["cross_in_bcol"]
                zero = lambda f: (lambda e, j: f(0, j))
                zerob = lambda f: (lambda e: f(0))
                attention(nc, c, s_t, t_t, o_t, zero(wpair(cw, 0)), zero(wpair(cw, 1)), zero(wpair(cw, 2)),
                          zerob(bcol(cbr, 0)), zerob(bcol(cbr, 1)), zerob(bcol(cbr, 2)))
                project_tokens(nc, c, o_t, DC, kview(a["cross_out_w"]), None, bias_d=a["cross_out_b"], residuals=[xc],
                               y=x_sb)
            normalize(nc, c, x5, x=x_sb, targets=[(s_t, col("nm_w"), col("nm_b"))])
            mlp(nc, c, s_t, kview(a["mlp_w1"]), kview(a["mlp_w2"]), col("mlp_b1"), a["mlp_b2"], [x5, x4], out)


def kernel(**inputs):
    import concourse.bacc as bacc
    from concourse.bass_utils import run_bass_kernel_spmd as run

    g = {k: np.asarray(v) for k, v in inputs.items()}
    f = {k[7:]: v for k, v in g.items() if k.startswith("L1_ffn_")}
    cols = lambda v: v.reshape(-1, 128).T
    ecols = lambda v: v.reshape(v.shape[0], -1, 128).transpose(0, 2, 1)
    packed = {"ln1_g": cols(g["L0_ffn_ln1_g"]), "ln1_b": cols(g["L0_ffn_ln1_b"]),
              "ln2_g": cols(g["L0_ffn_ln2_g"]), "ln2_b": cols(g["L0_ffn_ln2_b"]),
              "ns_w": cols(f["norm_s_w"]), "ns_b": cols(f["norm_s_b"]),
              "nt_w": cols(f["norm_t_w"]), "nt_b": cols(f["norm_t_b"]),
              "nm_w": cols(f["norm_mlp_w"]), "nm_b": cols(f["norm_mlp_b"]),
              "mlp_b1": cols(f["mlp_b1"]), "rt_b1": cols(f["router_b1"]),
              "moe_b1": g["L0_ffn_b1"].reshape(EXPERTS * 2, 128).T}
    arrays = {"pcol": np.concatenate([packed[n] for n in PCOL], axis=1)}
    for n in ("x", "src", "dst", "edge_attr_4", "edge_attr_8", "edge_weight", "L0_gnn_weight", "L0_ffn_wq", "L0_ffn_wk",
              "L0_ffn_wv", "L0_ffn_wo", "L0_ffn_wr", "L0_ffn_w1", "L0_ffn_w2", "L0_ffn_b2", "L1_gnn_W_up0",
              "L1_gnn_W_up1", "L1_gnn_W_mlp1", "L1_gnn_W_mlp2", "L1_gnn_W_mlp3", "L1_gnn_W_mlp4", "L1_gnn_W_out0",
              "L1_gnn_W_out1"):
        arrays[n] = g[n]
    arrays["L0_gnn_bias"] = g["L0_gnn_bias"].reshape(1, D)
    for n in ("sp_in", "sp_out", "tq", "tk", "tv", "tp"):
        arrays[f"{n}_w"] = f[f"{n}_w"].transpose(0, 2, 1)
    for n in ("sp_out", "tp"):
        arrays[f"{n}_b"] = ecols(f[f"{n}_b"])
    for n in ("tq", "tk", "tv", "sp_in"):
        arrays[f"{n}_bcol"] = ecols(f[f"{n}_b"])
    arrays["cross_in_w"] = f["cross_in_w"].T[None]
    arrays["cross_in_bcol"] = ecols(f["cross_in_b"][None])
    arrays["cross_out_w"], arrays["cross_out_b"] = f["cross_out_w"].T, f["cross_out_b"][None]
    arrays["mlp_w1"] = f["mlp_w1"].T
    arrays["mlp_w2"], arrays["mlp_b2"] = f["mlp_w2"].T, f["mlp_b2"][None]
    arrays["router_w1"], arrays["router_w2"], arrays["router_b2"] = f["router_w1"].T, f["router_w2"].T, f["router_b2"][None]
    arrays = {k: np.ascontiguousarray(v) for k, v in arrays.items()}

    nc = bacc.Bacc("TRN2", target_bir_lowering=False, num_devices=1)
    aps = {k: nc.dram_tensor(f"in_{k}", v.shape, mybir.dt.from_np(v.dtype), kind="ExternalInput").ap()
           for k, v in arrays.items()}
    out = nc.dram_tensor("out_0", (N, D), F32, kind="ExternalOutput").ap()
    program(nc, aps, out)
    r = run(nc, [{f"in_{k}": v for k, v in arrays.items()}], core_ids=[0])
    return r.results[0]["out_0"]
```
